# Optimizing a Trainium2 kernel written in Bass

```python
import numpy as np
import jax
import jax.numpy as jnp

def _softmax(x, axis=-1):
    return jax.nn.softmax(x, axis=axis)

def _gelu(x):
    return jax.nn.gelu(x, approximate=True)

def _silu(x):
    return jax.nn.silu(x)

def _sigmoid(x):
    return jax.nn.sigmoid(x)

def _layernorm(x, axis=-1, eps=1e-05):
    m = jnp.mean(x, axis=axis, keepdims=True)
    v = jnp.var(x, axis=axis, keepdims=True)
    return (x - m) / jnp.sqrt(v + eps)

def _scatter_add(tgt, idx, src, axis=0):
    return tgt.at[idx].add(src)

def _segment_sum(src, seg, n):
    return jax.ops.segment_sum(src, seg, n)
kernel_name = 'mk_decoder_postln_d2_seqx_r4_0fb831'

def setup_inputs(seed: int=0):
    np.random.seed(seed)
    _w = jnp.asarray

    def _rec_inputs():
        import jax
        import jax.numpy as jnp
        _rk = jax.random.key(seed)
        x = -0.0002928 + 1 * jax.random.normal(jax.random.fold_in(_rk, 1), (8, 256, 256), jnp.float32)
        _lenS = 256 - jax.random.randint(jax.random.fold_in(_rk, 7), (8,), 0, max(1, 256 // 4) + 1, jnp.int32)
        _lenS2 = 256 - jax.random.randint(jax.random.fold_in(_rk, 8), (8,), 0, max(1, 256 // 4) + 1, jnp.int32)
        _ctx_1024P = jax.random.normal(jax.random.fold_in(_rk, 11), (8, 16, 256), jnp.float32)
        _ctx_1024c = jax.random.dirichlet(jax.random.fold_in(_rk, 511), 0.3 * jnp.ones((16,), jnp.float32), (8, 256))
        _ctx_1024t = jnp.einsum('bsk,bkd->bsd', _ctx_1024c, _ctx_1024P)
        _ctx_1024t = _ctx_1024t * jax.lax.rsqrt(jnp.mean(jnp.square(_ctx_1024t)) + 1e-12) * 0.953939
        ctx_1024 = -1.39393e-06 + 0.999914 * (_ctx_1024t + 0.3 * jax.random.normal(jax.random.fold_in(_rk, 611), (8, 256, 256), jnp.float32))
        return (x, ctx_1024)
    x, ctx_1024 = _rec_inputs()

    def _L0_attn_setup():
        import jax, jax.numpy as jnp
        import numpy as np
        DIM = 256
        DIM_HEAD = 64
        HEADS = DIM // DIM_HEAD
        SCALE = DIM_HEAD ** (-0.5)
        RMS_EPS = 1e-08
        LN_EPS = 1e-05

        def _layernorm(x, g, b):
            mu = jnp.mean(x, axis=-1, keepdims=True)
            var = jnp.mean(jnp.square(x - mu), axis=-1, keepdims=True)
            return (x - mu) * jax.lax.rsqrt(var + LN_EPS) * g + b

        def _rmsnorm(x, gamma):
            norm = jnp.sqrt(jnp.sum(jnp.square(x), axis=-1, keepdims=True)) * DIM_HEAD ** (-0.5)
            return x / jnp.maximum(norm, RMS_EPS) * gamma
        key = jax.random.key(seed)
        ks = jax.random.split(key, 8)
        b, n = (2, 512)
        x = jax.random.normal(ks[0], (b, n, DIM), dtype=jnp.float32)
        init = 1.0 / np.sqrt(DIM)
        Wq = jax.random.uniform(ks[1], (DIM, DIM), jnp.float32, -init, init)
        Wk = jax.random.uniform(ks[2], (DIM, DIM), jnp.float32, -init, init)
        Wv = jax.random.uniform(ks[3], (DIM, DIM), jnp.float32, -init, init)
        Wo = jax.random.uniform(ks[4], (DIM, DIM), jnp.float32, -init, init)
        bo = jax.random.uniform(ks[5], (DIM,), jnp.float32, -init, init)
        ln_g = jnp.ones((DIM,), jnp.float32)
        ln_b = jnp.zeros((DIM,), jnp.float32)
        q_gamma = jnp.ones((DIM_HEAD,), jnp.float32)
        k_gamma = jnp.ones((DIM_HEAD,), jnp.float32)
        return dict(x=x, Wq=Wq, Wk=Wk, Wv=Wv, Wo=Wo, bo=bo, ln_g=ln_g, ln_b=ln_b, q_gamma=q_gamma, k_gamma=k_gamma)
    _L0_attn_all = _L0_attn_setup()
    _L0_attn_in = {k: v for k, v in _L0_attn_all.items() if k in ('Wq', 'Wk', 'Wv', 'Wo', 'bo', 'ln_g', 'ln_b', 'q_gamma', 'k_gamma')}
    del _L0_attn_all

    def _L0_xattn_setup():
        import jax, jax.numpy as jnp
        import numpy as np
        H, DK, DV = (16, 64, 64)
        MEM = 128
        D_MODEL = 256
        OUT_DIM = 256
        key = jax.random.key(seed)
        ks = jax.random.split(key, 12)
        B, S = (2, 512)
        scale = 1.0 / np.sqrt(D_MODEL)
        inp = {'queries': jax.random.normal(ks[0], (B, S, D_MODEL), jnp.float32), 'keys': jax.random.normal(ks[1], (B, S, D_MODEL), jnp.float32), 'values': jax.random.normal(ks[2], (B, S, D_MODEL), jnp.float32), 'wq_w': jax.random.normal(ks[3], (D_MODEL, H * DK), jnp.float32) * scale, 'wq_b': jnp.zeros((H * DK,), jnp.float32), 'wk_w': jax.random.normal(ks[4], (D_MODEL, H * DK), jnp.float32) * scale, 'wk_b': jnp.zeros((H * DK,), jnp.float32), 'wv_w': jax.random.normal(ks[5], (D_MODEL, H * DV), jnp.float32) * scale, 'wv_b': jnp.zeros((H * DV,), jnp.float32), 'mk': jax.random.normal(ks[6], (1, MEM, H * DK), jnp.float32) * (0.1 / DK), 'mv': jax.random.normal(ks[7], (1, MEM, H * DV), jnp.float32) * (0.1 / MEM), 'wo_w': jax.random.normal(ks[8], (H * DV, OUT_DIM), jnp.float32) * (1.0 / np.sqrt(H * DV)), 'wo_b': jnp.zeros((OUT_DIM,), jnp.float32)}
        return inp
    _L0_xattn_all = _L0_xattn_setup()
    _L0_xattn_in = {k: v for k, v in _L0_xattn_all.items() if k in ('wq_w', 'wq_b', 'wk_w', 'wk_b', 'wv_w', 'wv_b', 'mk', 'mv', 'wo_w', 'wo_b')}
    del _L0_xattn_all

    def _L0_ffn_setup():
        import jax, jax.numpy as jnp
        import numpy as np
        B, S, H, F, E, K = (4, 1024, 256, 1024, 8, 2)
        LN_EPS = 1e-05
        key = jax.random.key(seed)
        kx, kr, k1, k2 = jax.random.split(key, 4)
        x = jax.random.normal(kx, (B, S, H), dtype=jnp.float32)
        gamma = jnp.ones((H,), jnp.float32)
        beta = jnp.zeros((H,), jnp.float32)
        Wr = jax.random.normal(kr, (H, E), jnp.float32) * 0.02
        br = jnp.zeros((E,), jnp.float32)
        W1 = jax.random.normal(k1, (E, H, F), jnp.float32) * (1.0 / np.sqrt(H))
        b1 = jnp.zeros((E, F), jnp.float32)
        W2 = jax.random.normal(k2, (E, F, H), jnp.float32) * (1.0 / np.sqrt(F))
        b2 = jnp.zeros((E, H), jnp.float32)
        return {'x': x, 'gamma': gamma, 'beta': beta, 'Wr': Wr, 'br': br, 'W1': W1, 'b1': b1, 'W2': W2, 'b2': b2}
    _L0_ffn_all = _L0_ffn_setup()
    _L0_ffn_in = {k: v for k, v in _L0_ffn_all.items() if k in ('gamma', 'beta', 'Wr', 'br', 'W1', 'b1', 'W2', 'b2')}
    del _L0_ffn_all

    def _L1_attn_setup():
        import jax, jax.numpy as jnp
        import numpy as np
        D_MODEL, D_STATE, DT_RANK = (256, 16, 64)
        DT_MIN, DT_MAX = (0.001, 0.1)
        key = jax.random.key(seed)
        ks = jax.random.split(key, 8)
        B, L = (4, 512)
        x = jax.random.normal(ks[0], (B, L, D_MODEL), jnp.float32)
        A_log = jnp.log(jnp.tile(jnp.arange(1, D_STATE + 1, dtype=jnp.float32), (D_MODEL, 1)))
        D = jnp.ones((D_MODEL,), jnp.float32)
        dt_std = DT_RANK ** (-0.5)
        dt_proj_w = jax.random.uniform(ks[1], (D_MODEL, DT_RANK), jnp.float32, -dt_std, dt_std)
        dt = jnp.exp(jax.random.uniform(ks[2], (D_MODEL,), jnp.float32) * (np.log(DT_MAX) - np.log(DT_MIN)) + np.log(DT_MIN))
        dt_proj_b = dt + jnp.log(-jnp.expm1(-dt))
        scale = D_MODEL ** (-0.5)
        x_proj_w = jax.random.normal(ks[3], (DT_RANK, D_MODEL), jnp.float32) * scale
        B_proj_w = jax.random.normal(ks[4], (D_STATE, D_MODEL), jnp.float32) * scale
        C_proj_w = jax.random.normal(ks[5], (D_STATE, D_MODEL), jnp.float32) * scale
        return dict(x=x, A_log=A_log, D=D, dt_proj_w=dt_proj_w, dt_proj_b=dt_proj_b, x_proj_w=x_proj_w, B_proj_w=B_proj_w, C_proj_w=C_proj_w)
    _L1_attn_all = _L1_attn_setup()
    _L1_attn_in = {k: v for k, v in _L1_attn_all.items() if k in ('A_log', 'D', 'dt_proj_w', 'dt_proj_b', 'x_proj_w', 'B_proj_w', 'C_proj_w')}
    del _L1_attn_all

    def _L1_xattn_setup():
        import jax, jax.numpy as jnp
        import numpy as np
        DIM = 256
        NUM_HEADS = 16
        HEAD_DIM = DIM // NUM_HEADS
        B, L = (4, 1024)

        def _heads(x):
            Bb, Ll, _ = x.shape
            return x.reshape(Bb, Ll, NUM_HEADS, HEAD_DIM).transpose(0, 2, 1, 3)
        key = jax.random.key(seed)
        ks = jax.random.split(key, 11)
        s = 1.0 / np.sqrt(DIM)
        inp = {'q_seq': jax.random.normal(ks[0], (B, L, DIM), jnp.float32), 'k_seq': jax.random.normal(ks[1], (B, L, DIM), jnp.float32), 'v_seq': jax.random.normal(ks[2], (B, L, DIM), jnp.float32), 'Wq': jax.random.normal(ks[3], (DIM, DIM), jnp.float32) * s, 'bq': jax.random.normal(ks[4], (DIM,), jnp.float32) * s, 'Wk': jax.random.normal(ks[5], (DIM, DIM), jnp.float32) * s, 'bk': jax.random.normal(ks[6], (DIM,), jnp.float32) * s, 'Wv': jax.random.normal(ks[7], (DIM, DIM), jnp.float32) * s, 'bv': jax.random.normal(ks[8], (DIM,), jnp.float32) * s, 'Wo': jax.random.normal(ks[9], (DIM, DIM), jnp.float32) * s, 'bo': jax.random.normal(ks[10], (DIM,), jnp.float32) * s, 'extract_common': 1}
        return inp
    _L1_xattn_all = _L1_xattn_setup()
    _L1_xattn_in = {k: v for k, v in _L1_xattn_all.items() if k in ('Wq', 'bq', 'Wk', 'bk', 'Wv', 'bv', 'Wo', 'bo')}
    del _L1_xattn_all

    def _L1_ffn_setup():
        import jax, jax.numpy as jnp
        import numpy as np
        TOP_K = 2

        def _gelu(x):
            return jax.nn.gelu(x, approximate=False)
        key = jax.random.key(seed)
        ks = jax.random.split(key, 6)
        B, S, D, F, E = (2, 512, 256, 512, 8)
        sc_g = 1.0 / np.sqrt(D)

        def xav(k, shape, fan_in, fan_out):
            lim = np.sqrt(6.0 / (fan_in + fan_out))
            return jax.random.uniform(k, shape, jnp.float32, -lim, lim)
        return {'x': jax.random.normal(ks[0], (B, S, D), jnp.float32), 'Wg': xav(ks[1], (D, E), D, E), 'Wu': xav(ks[2], (E, D, F), D, F), 'Wd': xav(ks[3], (E, F, D), F, D), 'W1': xav(ks[4], (D, F), D, F), 'W2': xav(ks[5], (F, D), F, D)}
    _L1_ffn_all = _L1_ffn_setup()
    _L1_ffn_in = {k: v for k, v in _L1_ffn_all.items() if k in ('Wg', 'Wu', 'Wd', 'W1', 'W2')}
    del _L1_ffn_all
    return {'x': x, 'ctx_1024': ctx_1024, 'L0_attn_Wq': _L0_attn_in['Wq'], 'L0_attn_Wk': _L0_attn_in['Wk'], 'L0_attn_Wv': _L0_attn_in['Wv'], 'L0_attn_Wo': _L0_attn_in['Wo'], 'L0_attn_bo': _L0_attn_in['bo'], 'L0_attn_ln_g': _L0_attn_in['ln_g'], 'L0_attn_ln_b': _L0_attn_in['ln_b'], 'L0_attn_q_gamma': _L0_attn_in['q_gamma'], 'L0_attn_k_gamma': _L0_attn_in['k_gamma'], 'L0_xattn_wq_w': _L0_xattn_in['wq_w'], 'L0_xattn_wq_b': _L0_xattn_in['wq_b'], 'L0_xattn_wk_w': _L0_xattn_in['wk_w'], 'L0_xattn_wk_b': _L0_xattn_in['wk_b'], 'L0_xattn_wv_w': _L0_xattn_in['wv_w'], 'L0_xattn_wv_b': _L0_xattn_in['wv_b'], 'L0_xattn_mk': _L0_xattn_in['mk'], 'L0_xattn_mv': _L0_xattn_in['mv'], 'L0_xattn_wo_w': _L0_xattn_in['wo_w'], 'L0_xattn_wo_b': _L0_xattn_in['wo_b'], 'L0_ffn_gamma': _L0_ffn_in['gamma'], 'L0_ffn_beta': _L0_ffn_in['beta'], 'L0_ffn_Wr': _L0_ffn_in['Wr'], 'L0_ffn_br': _L0_ffn_in['br'], 'L0_ffn_W1': _L0_ffn_in['W1'], 'L0_ffn_b1': _L0_ffn_in['b1'], 'L0_ffn_W2': _L0_ffn_in['W2'], 'L0_ffn_b2': _L0_ffn_in['b2'], 'L1_attn_A_log': _L1_attn_in['A_log'], 'L1_attn_D': _L1_attn_in['D'], 'L1_attn_dt_proj_w': _L1_attn_in['dt_proj_w'], 'L1_attn_dt_proj_b': _L1_attn_in['dt_proj_b'], 'L1_attn_x_proj_w': _L1_attn_in['x_proj_w'], 'L1_attn_B_proj_w': _L1_attn_in['B_proj_w'], 'L1_attn_C_proj_w': _L1_attn_in['C_proj_w'], 'L1_xattn_Wq': _L1_xattn_in['Wq'], 'L1_xattn_bq': _L1_xattn_in['bq'], 'L1_xattn_Wk': _L1_xattn_in['Wk'], 'L1_xattn_bk': _L1_xattn_in['bk'], 'L1_xattn_Wv': _L1_xattn_in['Wv'], 'L1_xattn_bv': _L1_xattn_in['bv'], 'L1_xattn_Wo': _L1_xattn_in['Wo'], 'L1_xattn_bo': _L1_xattn_in['bo'], 'L1_ffn_Wg': _L1_ffn_in['Wg'], 'L1_ffn_Wu': _L1_ffn_in['Wu'], 'L1_ffn_Wd': _L1_ffn_in['Wd'], 'L1_ffn_W1': _L1_ffn_in['W1'], 'L1_ffn_W2': _L1_ffn_in['W2']}

def reference(x, ctx_1024, L0_attn_Wq, L0_attn_Wk, L0_attn_Wv, L0_attn_Wo, L0_attn_bo, L0_attn_ln_g, L0_attn_ln_b, L0_attn_q_gamma, L0_attn_k_gamma, L0_xattn_wq_w, L0_xattn_wq_b, L0_xattn_wk_w, L0_xattn_wk_b, L0_xattn_wv_w, L0_xattn_wv_b, L0_xattn_mk, L0_xattn_mv, L0_xattn_wo_w, L0_xattn_wo_b, L0_ffn_gamma, L0_ffn_beta, L0_ffn_Wr, L0_ffn_br, L0_ffn_W1, L0_ffn_b1, L0_ffn_W2, L0_ffn_b2, L1_attn_A_log, L1_attn_D, L1_attn_dt_proj_w, L1_attn_dt_proj_b, L1_attn_x_proj_w, L1_attn_B_proj_w, L1_attn_C_proj_w, L1_xattn_Wq, L1_xattn_bq, L1_xattn_Wk, L1_xattn_bk, L1_xattn_Wv, L1_xattn_bv, L1_xattn_Wo, L1_xattn_bo, L1_ffn_Wg, L1_ffn_Wu, L1_ffn_Wd, L1_ffn_W1, L1_ffn_W2):
    import jax
    import jax.numpy as jnp

    def _L0_attn_ref(x, Wq, Wk, Wv, Wo, bo, ln_g, ln_b, q_gamma, k_gamma):
        import jax, jax.numpy as jnp
        import numpy as np
        DIM = 256
        DIM_HEAD = 64
        HEADS = DIM // DIM_HEAD
        SCALE = DIM_HEAD ** (-0.5)
        RMS_EPS = 1e-08
        LN_EPS = 1e-05

        def _layernorm(x, g, b):
            mu = jnp.mean(x, axis=-1, keepdims=True)
            var = jnp.mean(jnp.square(x - mu), axis=-1, keepdims=True)
            return (x - mu) * jax.lax.rsqrt(var + LN_EPS) * g + b

        def _rmsnorm(x, gamma):
            norm = jnp.sqrt(jnp.sum(jnp.square(x), axis=-1, keepdims=True)) * DIM_HEAD ** (-0.5)
            return x / jnp.maximum(norm, RMS_EPS) * gamma
        b, n, _ = x.shape
        xn = _layernorm(x, ln_g, ln_b)

        def split_heads(t):
            return t.reshape(b, n, HEADS, DIM_HEAD).transpose(0, 2, 1, 3)
        q = split_heads(xn @ Wq.T)
        k = split_heads(xn @ Wk.T)
        v = split_heads(xn @ Wv.T)
        q = _rmsnorm(q, q_gamma) * SCALE
        k = _rmsnorm(k, k_gamma)
        sim = jnp.einsum('bhid,bhjd->bhij', q, k)
        attn = jax.nn.softmax(sim, axis=-1)
        out = jnp.einsum('bhij,bhjd->bhid', attn, v)
        out = out.transpose(0, 2, 1, 3).reshape(b, n, DIM)
        return out @ Wo.T + bo

    def _L0_xattn_ref(queries, keys, values, wq_w, wq_b, wk_w, wk_b, wv_w, wv_b, mk, mv, wo_w, wo_b):
        import jax, jax.numpy as jnp
        import numpy as np
        H, DK, DV = (16, 64, 64)
        MEM = 128
        D_MODEL = 256
        OUT_DIM = 256
        B, S, _ = queries.shape
        q = (queries @ wq_w + wq_b).reshape(B, S, H, DK).transpose(0, 2, 1, 3)
        k_proj = keys @ wk_w + wk_b
        v_proj = values @ wv_w + wv_b
        k_ext = jnp.concatenate([k_proj, jnp.broadcast_to(mk, (B, MEM, H * DK))], axis=1)
        v_ext = jnp.concatenate([v_proj, jnp.broadcast_to(mv, (B, MEM, H * DV))], axis=1)
        T = S + MEM
        k = k_ext.reshape(B, T, H, DK).transpose(0, 2, 1, 3)
        v = v_ext.reshape(B, T, H, DV).transpose(0, 2, 1, 3)
        scores = jnp.einsum('bhsd,bhtd->bhst', q, k) / jnp.sqrt(jnp.float32(DK))
        attn = jax.nn.softmax(scores, axis=-1)
        out = jnp.einsum('bhst,bhtd->bhsd', attn, v)
        out = out.transpose(0, 2, 1, 3).reshape(B, S, H * DV)
        return out @ wo_w + wo_b

    def _L0_ffn_ref(x, gamma, beta, Wr, br, W1, b1, W2, b2):
        import jax, jax.numpy as jnp
        import numpy as np
        B, S, H, F, E, K = (4, 1024, 256, 1024, 8, 2)
        LN_EPS = 1e-05
        residual = x
        mu = jnp.mean(x, axis=-1, keepdims=True)
        var = jnp.var(x, axis=-1, keepdims=True)
        xn = (x - mu) * jax.lax.rsqrt(var + LN_EPS) * gamma + beta
        probs = jax.nn.softmax(xn @ Wr + br, axis=-1)
        scores, idx = jax.lax.top_k(probs, K)

        def expert_fn(w):
            W1_e, b1_e, W2_e, b2_e = w
            return jax.nn.relu(xn @ W1_e + b1_e) @ W2_e + b2_e
        full = jax.lax.map(expert_fn, (W1, b1, W2, b2))
        full = jnp.moveaxis(full, 0, 2)
        c = jnp.einsum('ef,efh->eh', jax.nn.relu(b1), W2) + b2
        c_total = c.sum(axis=0)
        sel_full = jnp.take_along_axis(full, idx[..., None], axis=2)
        c_sel = c[idx]
        output = jnp.sum(scores[..., None] * (sel_full - c_sel + c_total), axis=2)
        return residual + output

    def _L1_attn_ref(x, A_log, D, dt_proj_w, dt_proj_b, x_proj_w, B_proj_w, C_proj_w):
        import jax, jax.numpy as jnp
        import numpy as np
        D_MODEL, D_STATE, DT_RANK = (256, 16, 64)
        DT_MIN, DT_MAX = (0.001, 0.1)
        A = -jnp.exp(A_log)
        r = jnp.einsum('blm,rm->blr', x, x_proj_w)
        delta = jax.nn.softplus(jnp.einsum('blr,dr->bld', r, dt_proj_w) + dt_proj_b)
        delta = jnp.clip(delta, DT_MIN, DT_MAX)
        Bm = jnp.einsum('blm,nm->bln', x, B_proj_w)
        Cm = jnp.einsum('blm,nm->bln', x, C_proj_w)

        def step(h, inp):
            x_t, d_t, B_t, C_t = inp
            A_bar = jnp.exp(d_t[:, :, None] * A)
            h = A_bar * h + (d_t * x_t)[:, :, None] * B_t[:, None, :]
            y_t = jnp.einsum('bdn,bn->bd', h, C_t)
            return (h, y_t)
        bsz = x.shape[0]
        h0 = jnp.zeros((bsz, D_MODEL, D_STATE), x.dtype)
        xs = (jnp.swapaxes(x, 0, 1), jnp.swapaxes(delta, 0, 1), jnp.swapaxes(Bm, 0, 1), jnp.swapaxes(Cm, 0, 1))
        _, ys = jax.lax.scan(step, h0, xs)
        y = jnp.swapaxes(ys, 0, 1) + D * x
        return y

    def _L1_xattn_ref(q_seq, k_seq, v_seq, Wq, bq, Wk, bk, Wv, bv, Wo, bo, extract_common):
        import jax, jax.numpy as jnp
        import numpy as np
        DIM = 256
        NUM_HEADS = 16
        HEAD_DIM = DIM // NUM_HEADS
        B, L = (4, 1024)

        def _heads(x):
            Bb, Ll, _ = x.shape
            return x.reshape(Bb, Ll, NUM_HEADS, HEAD_DIM).transpose(0, 2, 1, 3)
        Q = _heads(q_seq @ Wq.T + bq)
        K = _heads(k_seq @ Wk.T + bk)
        V = _heads(v_seq @ Wv.T + bv)
        K_probs = jax.nn.softmax(K, axis=2)
        context = jnp.einsum('bhld,bhle->bhde', K_probs, V)
        attended = jnp.einsum('bhld,bhde->bhle', Q, context)
        if extract_common:
            target = attended
        else:
            target = V - attended
        Bb, _, Ll, _ = target.shape
        target = target.transpose(0, 2, 1, 3).reshape(Bb, Ll, DIM)
        return target @ Wo.T + bo

    def _L1_ffn_ref(x, Wg, Wu, Wd, W1, W2):
        import jax, jax.numpy as jnp
        import numpy as np
        TOP_K = 2

        def _gelu(x):
            return jax.nn.gelu(x, approximate=False)
        B, S, D = x.shape
        E = Wu.shape[0]
        T = B * S
        xt = x.reshape(T, D)
        probs = jax.nn.softmax(xt @ Wg, axis=-1)
        topv, topi = jax.lax.top_k(probs, TOP_K)
        topv = topv / jnp.sum(topv, axis=-1, keepdims=True)
        cw = jnp.zeros((T, E), x.dtype).at[jnp.arange(T)[:, None], topi].set(topv)
        h = _gelu(jnp.einsum('td,edf->tef', xt, Wu))
        y = jnp.einsum('tef,efd->ted', h, Wd)
        moe = jnp.einsum('ted,te->td', y, cw)
        shared = _gelu(xt @ W1) @ W2
        return (shared + moe).reshape(B, S, D)
    x = _layernorm(x + _L0_attn_ref(x, L0_attn_Wq, L0_attn_Wk, L0_attn_Wv, L0_attn_Wo, L0_attn_bo, L0_attn_ln_g, L0_attn_ln_b, L0_attn_q_gamma, L0_attn_k_gamma), axis=-1)
    x = _layernorm(x + _L0_xattn_ref(x, ctx_1024, ctx_1024, L0_xattn_wq_w, L0_xattn_wq_b, L0_xattn_wk_w, L0_xattn_wk_b, L0_xattn_wv_w, L0_xattn_wv_b, L0_xattn_mk, L0_xattn_mv, L0_xattn_wo_w, L0_xattn_wo_b), axis=-1)
    x = _layernorm(x + _L0_ffn_ref(x, L0_ffn_gamma, L0_ffn_beta, L0_ffn_Wr, L0_ffn_br, L0_ffn_W1, L0_ffn_b1, L0_ffn_W2, L0_ffn_b2), axis=-1)
    x = _layernorm(x + _L1_attn_ref(x, L1_attn_A_log, L1_attn_D, L1_attn_dt_proj_w, L1_attn_dt_proj_b, L1_attn_x_proj_w, L1_attn_B_proj_w, L1_attn_C_proj_w), axis=-1)
    x = _layernorm(x + _L1_xattn_ref(x, ctx_1024, ctx_1024, L1_xattn_Wq, L1_xattn_bq, L1_xattn_Wk, L1_xattn_bk, L1_xattn_Wv, L1_xattn_bv, L1_xattn_Wo, L1_xattn_bo, 1), axis=-1)
    x = _layernorm(x + _L1_ffn_ref(x, L1_ffn_Wg, L1_ffn_Wu, L1_ffn_Wd, L1_ffn_W1, L1_ffn_W2), axis=-1)
    return x

_drawn_inputs = setup_inputs


def setup_inputs(seed=0):
    import zlib

    import numpy as np

    out = dict(_drawn_inputs(seed))
    spreads = {'L0_attn_ln_g': (1.0, 0.2),
     'L0_attn_ln_b': (0.0, 0.1),
     'L0_attn_q_gamma': (1.0, 0.575),
     'L0_attn_k_gamma': (1.0, 0.6),
     'L0_xattn_wq_b': (0.0, 0.1),
     'L0_xattn_wk_b': (0.0, 0.279),
     'L0_xattn_wv_b': (0.0, 0.1),
     'L0_xattn_wo_b': (0.0, 0.1),
     'L0_ffn_gamma': (1.0, 0.2),
     'L0_ffn_beta': (0.0, 0.1),
     'L0_ffn_br': (0.0, 0.1),
     'L0_ffn_b1': (0.0, 0.1),
     'L0_ffn_b2': (0.0, 0.1),
     'L1_attn_D': (1.0, 0.2)}
    factors = {'L0_xattn_mk': 8.0, 'L0_xattn_mv': 8.0, 'L1_xattn_bk': 8.0}
    for name, (base, spread) in spreads.items():
        noise = np.random.default_rng([zlib.crc32(name.encode()), seed]).standard_normal(out[name].shape)
        drawn = base * np.exp(spread * noise) if base else spread * noise
        out[name] = jnp.asarray(drawn.astype(out[name].dtype))
    for name, factor in factors.items():
        out[name] = (out[name] * factor).astype(out[name].dtype)
    return out
```

```python
import concourse.bass as bass
from concourse import mybir
from contextlib import ExitStack

ALU = mybir.AluOpType
ACT = mybir.ActivationFunctionType
AX = mybir.AxisListType
TOP_K = 2
SLOTS = 256
SLOT_BITS = 8
LN_EPS = 1e-5
RMS_EPS = 1e-8
SCALE = 64 ** -0.5
DT_MIN, DT_MAX = 0.001, 0.1


def attention_layers(nc, sems, x_in, ctx_in, x_out, slots, w):
    fp32, fp32r = mybir.dt.float32, mybir.dt.float32r
    B, S, D = x_in.shape
    HX, MEM = 16, w["mvx"].shape[0]
    PX = HX // 2
    P0 = 2
    ND = S // 128
    KD = D // 128
    KEYS = S + MEM
    KX = KEYS // 128
    U0, UX = 4 * P0, 4 * PX
    U = U0 + UX
    PAIRS = P0 + PX
    assert ND == 2 and KD == 2 and U % 4 == 0 and PAIRS % 2 == 0
    R_LAG, T_LAG, C_LAG, V_LAG, O_LAG, L_LAG = 2, 5, 5, 11, 12, 13
    SIDE, Q_SIDE = 2, 2
    RING = 8
    BANKS = 3
    TAIL = L_LAG - 4

    JOB = {n: j for j, n in enumerate(
        ["first ctxT", "first xnT", "first vself", "k0", "k1", "qkT0", "qkT1", "v0", "v1", "v2", "v3", "k2", "k3", "oself"]
        + [f"k{p}" for p in range(4, PX)] + ["x1T"] + [f"q{p}" for p in range(PX)] + ["ctxT", "xnT", "vself", "ox"])}
    JOBS = len(JOB) - 3
    assert JOBS % 2 == 0

    ctx = ExitStack()
    with ctx:
        def sb(n, shape, dt=fp32):
            return ctx.enter_context(nc.sbuf_tensor(f"a_{n}", shape, dt))

        def sem(n):
            sems.append(nc.alloc_semaphore(f"a_{n}"))
            return sems[-1]

        def pair_of(n, shape):
            return [sb(n + part, shape, fp32r) for part in ("_high", "_low")]

        x = sb("x", [128, ND, D])
        cx = sb("cx", [128, ND, D])
        xn = sb("xn", [128, ND, D])
        x1 = sb("x1", [128, ND, D])
        x1b = sb("x1b", [128, ND, D])
        xo = sb("xo", [128, ND, D])
        xT = pair_of("xT", [128, KD, S])
        cT = pair_of("cT", [128, KD, S])
        wqkv = pair_of("wqkv", [128, KD, 3 * D])
        wo0 = pair_of("wo0", [128, KD, D])
        wq = pair_of("wq", [128, KD, HX * 64])
        wk = pair_of("wk", [128, KD, HX * 64])
        wv = pair_of("wv", [128, KD, HX * 64])
        wox = pair_of("wox", [128, PX, D])
        bqx = sb("bqx", [128, PX])
        bkx = sb("bkx", [128, PX])
        bvx = sb("bvx", [128, HX * 64])
        bo0 = sb("bo0", [128, D])
        box = sb("box", [128, D])
        gb = sb("gb", [128, 2, KD])
        qkg = sb("qkg", [128, 2])
        ident = sb("ident", [128, 128])
        work = sb("work", [128, 3, 4, S])
        sq = work[:, 0:2].rearrange("p a b s -> p (a b s)")[:, 0:ND * 2 * D].rearrange("p (t n) -> p t n", t=ND)
        qkf = work[:, 2]
        kself = pair_of("kself", [128, P0, S])
        vself = sb("vself", [128, ND, D])
        qs = pair_of("qs", [128, 2, 2, S])
        ks = pair_of("ks", [128, PX, KEYS])
        vx = sb("vx", [128, KX, HX * 64])
        pexp_own = sb("pexp", [128, RING // 2, KEYS])
        pexp_work = work[:, 0:2].rearrange("p a b s -> p (a b s)")[:, 0:RING // 2 * KEYS].rearrange("p (r n) -> p r n", r=RING // 2)
        pexp = [(pexp_own, pexp_work)[r % 2][:, r // 2, :] for r in range(RING)]
        pT = sb("pT", [128, 2, 2, KX, S])
        oT = pair_of("oT", [128, PX, S])
        zero = sb("zero", [128, D])
        st = sb("st", [128, ND, 6])
        mv = sb("mv", [128, ND, 2])
        var = sb("var", [128, ND * 8])
        root = sb("root", [128, ND * 8])
        tmp = sb("tmp", [128, ND * 8])
        nmax = sb("nmax", [128, RING])
        sums = sb("sums", [128, RING])
        rsum = sb("rsum", [128, RING])

        ps = [ctx.enter_context(nc.psum_tensor(f"a_ps{n}", [128, 512], fp32)) for n in range(8)]
        ps_s, ps_t, ps_o, ps_j = ps[0:3], ps[3:5], ps[5], ps[6:8]

        s_ln = sem("s_ln")
        s_zero = sem("s_zero"); s_filled = sem("s_filled")
        s_w = [sem(f"s_w{n}") for n in range(2)]; w_high = sem("w_high"); w_low = sem("w_low"); s_small = sem("s_small")
        s_gc = sem("s_gc"); s_scaled = sem("s_scaled")
        x_loaded = sem("x_loaded"); ctx_loaded = sem("ctx_loaded")
        s_dve = sem("s_dve"); var_ready = sem("var_ready"); ln_done = sem("ln_done"); root_ready = sem("root_ready")
        rows_ready = sem("rows_ready"); xb_ready = sem("xb_ready")
        job_raw = sem("job_raw"); qk_raw = sem("qk_raw"); qk_normed = sem("qk_normed"); job_free = [sem("job_free0"), sem("job_free1")]
        act_part = sem("act_part"); dve_part = sem("dve_part"); k_low = sem("k_low"); q_low = sem("q_low"); q_high = sem("q_high")
        scores_raw = sem("scores_raw"); maxed = sem("maxed"); exped = sem("exped"); recip = sem("recip")
        normed = sem("normed"); pt_raw = sem("pt_raw"); pt_copied = [sem("pt_copied0"), sem("pt_copied1")]
        o_raw = sem("o_raw"); o_high = sem("o_high"); o_split = sem("o_split"); s_out = sem("s_out")

        rows = lambda a: a.rearrange("a (t p) d -> p (a t) d", p=128)
        stage = [pT[:].rearrange("p a b c s -> p (a b c s)"), work[:].rearrange("p a b s -> p (a b s)")]
        flat3 = lambda t: t[:].rearrange("p a b -> p (a b)")
        SPLIT = [(w["wqkv"], [t[:] for t in wqkv]), (w["wo0"], [t[:] for t in wo0]), (w["wq"], [t[:] for t in wq]),
                 (w["wk"], [t[:] for t in wk]), (w["wv"], [t[:] for t in wv]), (w["wox"], [t[:] for t in wox]),
                 (w["mk"], [t[:, :, S:KEYS] for t in ks])]

        def staged(n):
            a = SPLIT[n][0]
            return stage[n % 2][:, 0:a.shape[1] * a.shape[2]].rearrange("p (k n) -> p k n", k=a.shape[1])

        def schedule(units, first_pair):
            at = lambda v, lag: (v - lag) // 4 if v >= lag and (v - lag) % 4 == 0 and (v - lag) // 4 < units // 4 else None
            for v in range(units + TAIL + 2):
                inside = lambda u: u if 0 <= u < units else None
                yield v, inside(v), inside(v - T_LAG), inside(v - C_LAG), at(v, V_LAG), at(v, O_LAG), at(v, L_LAG)

        acts = ["first ctxT", "first qk0", "first qk1"] + [f"k{p}" for p in range(PX)] + ["x1T", "ctxT", "qk0", "qk1"]
        ACT_PART = {n: k + 1 for k, n in enumerate(acts)}
        ACT_PARTS = len(acts) - 3
        ROOTS = {"first": 1, "first qk": 2, "x1": 3, "xn": 4, "qk": 5, "xo": 6}
        CTX_SLOT, XN_SLOT = 4 * (PX - 2) + Q_SIDE - 1, 4 * (PX - 2) + Q_SIDE + 2
        QK_SLOT = UX + T_LAG
        FILL = {2: 0, 4: 1, 6: 2, 8: 3}

        def FREED(i, name):
            return i * (JOBS // 2) + JOB[name] // 2 + 2

        def copy_pt(eng, copy, i, base, first_pair, u):
            m = first_pair + u // 4
            kx = KX if base else ND
            eng.wait_ge(pt_raw, i * U + base + u + 1 + RING)
            eng.wait_ge(o_raw, i * PAIRS + m - 1 + 2)
            copy(pT[:, m % 2, u // 2 % 2, 0:kx, u % 2 * 128:u % 2 * 128 + 128],
                 ps_t[u % 2][:, 0:kx * 128].rearrange("p (k s) -> p k s", k=kx)).then_inc(pt_copied[u % 2], 1)

        with nc.Block() as block:
            @block.sync
            def _(sp):
                for n, (src, _) in enumerate(SPLIT):
                    if n >= 2:
                        sp.wait_ge(w_low, n - 1)
                        sp.wait_ge(w_high, n - 1)
                    sp.dma_start(staged(n), src).then_inc(s_w[n % 2], 16)
                for dst, src in ((bqx[:], w["bqx"]), (bkx[:], w["bkx"]), (bvx[:], w["bvx"].partition_broadcast(128)),
                                 (bo0[:], w["bo0"].partition_broadcast(128)), (box[:], w["box"].partition_broadcast(128)),
                                 (gb[:, 0, :], w["ln_g"]), (gb[:, 1, :], w["ln_b"]), (qkg[:, 0:1], w["qg"]), (qkg[:, 1:2], w["kg"]),
                                 (vx[:, ND, :], w["mvx"])):
                    sp.dma_start(dst, src).then_inc(s_small, 16)

                def load(i):
                    sp.dma_start(x[:], rows(x_in[bass.ds(i, 1)])).then_inc(x_loaded, 16)
                    sp.dma_start(cx[:], rows(ctx_in[bass.ds(i, 1)])).then_inc(ctx_loaded, 16)

                def store(i):
                    sp.wait_ge(ln_done, i + 1)
                    sp.dma_start(rows(x_out[bass.ds(i, 1)]), xo[:]).then_inc(s_out, 16)

                sp.sem_inc(s_out, 16)
                load(0)
                sp.wait_ge(s_zero, 1)
                sp.dma_start(slots.rearrange("(p r) d -> p r d", p=128), zero[:].unsqueeze(1).to_broadcast([128, slots.shape[0] // 128, D])).then_inc(s_filled, 16)
                with sp.Fori(0, B - 1) as i:
                    sp.wait_ge(rows_ready, 2 * i + 2)
                    load(i + 1)
                    store(i)
                sp.wait_ge(rows_ready, 2 * B)
                load(0)
                store(B - 1)
                sp.wait_ge(s_out, 16 * B + 16)

            @block.gpsimd
            def _(pool):
                nc.gpsimd.memset(zero[:], 0.0).then_inc(s_zero, 1)
                nc.gpsimd.memset(ident[:], 0.0).then_inc(s_gc, 1)
                pool.wait_ge(s_gc, 1)
                nc.gpsimd.affine_select(out=ident[:], in_=ident[:], compare_op=ALU.not_equal, fill=1.0, base=0,
                                        pattern=[[-1, 128]], channel_multiplier=1).then_inc(s_gc, 1)
                for part in range(2):
                    pool.wait_ge(s_gc, 2 + 2 * part)
                    nc.gpsimd.memset(qs[part][64:128, :, 0, :].bitcast(fp32), 0.0).then_inc(s_gc, 1)
                    pool.wait_ge(s_gc, 3 + 2 * part)
                    nc.gpsimd.memset(qs[part][0:64, :, 1, :].bitcast(fp32), 0.0).then_inc(s_gc, 1)

                pool.wait_ge(s_gc, 6)

                def low_k(i, p):
                    pool.wait_ge(act_part, i * ACT_PARTS + ACT_PART[f"k{p}"])
                    nc.gpsimd.tensor_tensor(ks[1][:, p, 0:S], qkf[:, p % 2, :], ks[0][:, p, 0:S], ALU.subtract).then_inc(k_low, 1)

                def norm(i, base, u):
                    pool.wait_ge(recip, i * U + base + u + 1)
                    n = KEYS if base else S
                    nc.gpsimd.tensor_tensor(pexp[u % RING][:, 0:n], pexp[u % RING][:, 0:n], rsum[:, u % RING:u % RING + 1].to_broadcast([128, n]), ALU.mult)\
                        .then_inc(normed, 1)

                with pool.Fori(0, B) as i:
                    pool.wait_ge(rows_ready, 2 * i + 1)
                    nc.gpsimd.tensor_tensor(x[:], x[:], bo0[:].unsqueeze(1).to_broadcast([128, ND, D]), ALU.add).then_inc(xb_ready, 1)
                    low_k(i, 0)
                    low_k(i, 1)
                    for u in range(U0):
                        norm(i, 0, u)
                    low_k(i, 2)
                    low_k(i, 3)
                    for p in range(4, PX):
                        low_k(i, p)
                    pool.wait_ge(rows_ready, 2 * i + 2)
                    nc.gpsimd.tensor_tensor(x1b[:], x1[:], box[:].unsqueeze(1).to_broadcast([128, ND, D]), ALU.add).then_inc(xb_ready, 1)
                    for u in range(UX):
                        norm(i, U0, u)

            @block.scalar
            def _(act):
                nc.scalar.preload_act_table_set("natural_log_exp_and_others")
                for n, (src, parts) in enumerate(SPLIT):
                    act.wait_ge(s_w[n % 2], 16 * (n // 2 + 1))
                    nc.scalar.copy(parts[0], staged(n)).then_inc(w_high, 1)
                act.wait_ge(s_small, 160)
                act.wait_ge(s_scaled, 2)

                def take_root(i, name, n):
                    act.wait_ge(var_ready, 4 * i + ROOTS[name])
                    nc.scalar.activation(root[:, 0:n], var[:, 0:n], ACT.Ln).then_inc(s_ln, 1)
                    act.wait_ge(s_ln, 4 * i + ROOTS[name])
                    nc.scalar.activation(root[:, 0:n], root[:, 0:n], ACT.Exp, scale=-0.5).then_inc(root_ready, 1)

                def job(i, name):
                    act.wait_ge(job_raw, i * JOBS + JOB[name] + 1)
                    return ps_j[JOB[name] % 2]

                def free(name, ins):
                    ins.then_inc(job_free[JOB[name] % 2], 1)

                def keys(i, p):
                    b = job(i, f"k{p}")
                    if p >= 2:
                        act.wait_ge(k_low, i * PX + p - 1)
                    nc.scalar.activation(qkf[:, p % 2, :], b[:, 0:S], ACT.Identity, bias=bkx[:, p:p + 1]).then_inc(job_free[JOB[f"k{p}"] % 2], 1)
                    act.wait_ge(job_free[JOB[f"k{p}"] % 2], FREED(i, f"k{p}"))
                    nc.scalar.copy(ks[0][:, p, 0:S], qkf[:, p % 2, :]).then_inc(act_part, 1)

                def queries(i, p):
                    b = job(i, f"q{p}")
                    if p >= 2:
                        act.wait_ge(q_low, i * PX + p - 1)
                    nc.scalar.activation(qkf[:, 2 + p % 2, :], b[:, 0:S], ACT.Identity, bias=bqx[:, p:p + 1], scale=SCALE)\
                        .then_inc(job_free[JOB[f"q{p}"] % 2], 1)

                def attend(i, base, first_pair, units, side):
                    n = KEYS if base else S
                    for v, us, ut, uc, pv, po, pl in schedule(units, first_pair):
                        if us is not None:
                            act.wait_ge(maxed, i * U + base + us + 1)
                            act.wait_ge(pt_raw, i * U + base + (us + 1 if us >= RING else RING))
                            nc.scalar.activation(pexp[us % RING][:, 0:n], ps_s[us % BANKS][:, 0:n], ACT.Exp, bias=nmax[:, us % RING:us % RING + 1],
                                                 accum_out=sums[:, us % RING:us % RING + 1]).then_inc(exped, 1)
                        side(v)
                        if uc is not None and uc % 2 == 1:
                            copy_pt(act, nc.scalar.copy, i, base, first_pair, uc)
                        if po is not None:
                            m = first_pair + po
                            act.wait_ge(o_raw, i * PAIRS + m + 1 + 2)
                            nc.scalar.copy(oT[0][:, po, :], ps_o[:, 0:S]).then_inc(o_high, 1)

                def context(i, name):
                    b = job(i, name)
                    nc.scalar.copy(cT[0][:], b[:].rearrange("p (k s) -> p k s", k=KD)).then_inc(act_part, 1)

                def scaled_rows(i, name):
                    b = job(i, name)
                    for k in range(KD):
                        last = nc.scalar.activation(xn[:, k, :], b[:, k * S:(k + 1) * S], ACT.Identity, bias=gb[:, 1, k:k + 1], scale=gb[:, 0, k:k + 1])
                    free(name, last)

                def self_values(i, name):
                    b = job(i, name)
                    free(name, nc.scalar.copy(vself[:], b[:].rearrange("p (t d) -> p t d", t=ND)))

                def squares(entry, s):
                    act.wait_ge(qk_raw, ND * entry + s + 1)
                    nc.scalar.activation(sq[:, s, :], ps_s[s][:], ACT.Square).then_inc(act_part, 1)

                act.sem_inc(exped, BANKS)
                take_root(0, "first", ND)
                context(0, "first ctxT")
                scaled_rows(0, "first xnT")
                self_values(0, "first vself")
                squares(0, 0)
                squares(0, 1)
                take_root(0, "first qk", ND * 8)
                with act.Fori(0, B) as i:
                    keys(i, 0)
                    keys(i, 1)
                    act.wait_ge(k_low, i * PX + 2)
                    for s in range(ND):
                        b = job(i, f"qkT{s}")
                        for qk in range(2):
                            last = nc.scalar.activation(qkf[:, 2 * qk:2 * qk + 2, s * 128:(s + 1) * 128],
                                                        b[:, 256 * qk:256 * qk + 256].rearrange("p (m s) -> p m s", m=2), ACT.Copy,
                                                        scale=qkg[:, qk:qk + 1])
                        free(f"qkT{s}", last)
                    attend(i, 0, 0, U0, lambda v: keys(i, FILL[v]) if FILL.get(v, 0) >= 2 else None)
                    for p in range(4, PX):
                        keys(i, p)
                    take_root(i, "x1", ND)
                    b = job(i, "x1T")
                    nc.scalar.copy(xT[0][:], b[:].rearrange("p (k s) -> p k s", k=KD)).then_inc(act_part, 1)
                    queries(i, 0)
                    queries(i, 1)

                    def side(v):
                        if v % 4 == Q_SIDE and v // 4 + 2 < PX:
                            queries(i, v // 4 + 2)
                        if v == 6:
                            take_root(i, "xn", ND)
                        if v == CTX_SLOT + 1:
                            context(i, "ctxT")
                        if v == XN_SLOT + 1:
                            scaled_rows(i, "xnT")
                        if v == QK_SLOT + 2:
                            self_values(i, "vself")
                            squares(i + 1, 0)
                            squares(i + 1, 1)

                    attend(i, U0, P0, UX, side)
                    take_root(i, "qk", ND * 8)
                    take_root(i, "xo", ND)


            LINKS = 25

            @block.vector
            def _(dve):
                chain = [0]

                def link(i, ins):
                    chain[0] += 1
                    ins.then_inc(s_dve, 1)
                    dve.wait_ge(s_dve, i * LINKS + chain[0])

                for n, (src, parts) in enumerate(SPLIT):
                    dve.wait_ge(w_high, n + 1)
                    nc.vector.tensor_tensor(parts[1], staged(n), parts[0], ALU.subtract).then_inc(w_low, 1)
                dve.wait_ge(s_small, 160)
                nc.vector.tensor_scalar(bqx[:], bqx[:], SCALE, None, ALU.mult).then_inc(s_scaled, 1)
                nc.vector.tensor_scalar(qkg[:, 0:1], qkg[:, 0:1], SCALE, None, ALU.mult).then_inc(s_scaled, 1)

                def refine_root(i, name, n):
                    dve.wait_ge(root_ready, 4 * i + ROOTS[name])
                    link(i, nc.vector.tensor_tensor(tmp[:, 0:n], root[:, 0:n], root[:, 0:n], ALU.mult))
                    link(i, nc.vector.tensor_tensor(tmp[:, 0:n], tmp[:, 0:n], var[:, 0:n], ALU.mult))
                    link(i, nc.vector.tensor_scalar(tmp[:, 0:n], tmp[:, 0:n], -0.5, 1.5, ALU.mult, ALU.add))
                    link(i, nc.vector.tensor_tensor(root[:, 0:n], root[:, 0:n], tmp[:, 0:n], ALU.mult))

                def norm_stats(i, src):
                    for s in range(ND):
                        last = nc.vector.bn_stats(st[:, s, :], src[:, s, :])
                    link(i, last)
                    nc.vector.memset(tmp[:, 0:1], 0.0)
                    for s in range(ND):
                        last = nc.vector.bn_aggr(mv[:, s, :], st[:, s, :])
                    link(i, last)
                    nc.vector.tensor_scalar(var[:, 0:ND], mv[:, :, 1], LN_EPS, None, ALU.add).then_inc(var_ready, 1)

                def norm_apply(i, name, src, dst, done):
                    refine_root(i, name, ND)
                    for s in range(ND):
                        last = nc.vector.tensor_scalar(dst[:, s, :], src[:, s, :], mv[:, s, 0:1], root[:, s:s + 1], ALU.subtract, ALU.mult)
                    last.then_inc(done, 1)

                def job(i, name):
                    dve.wait_ge(job_raw, i * JOBS + JOB[name] + 1)
                    return ps_j[JOB[name] % 2]

                def after_act(i, name):
                    dve.wait_ge(act_part, i * ACT_PARTS + ACT_PART[name])
                    return ps_j[JOB[name] % 2]

                def after_free(i, name):
                    dve.wait_ge(job_free[JOB[name] % 2], FREED(i, name))

                def free(name, ins):
                    ins.then_inc(job_free[JOB[name] % 2], 1)

                def values(i, n):
                    b = job(i, f"v{n}")
                    s, half = n // 2, n % 2
                    free(f"v{n}", nc.vector.tensor_tensor(vx[:, s, half * 512:half * 512 + 512], b[:], bvx[:, half * 512:half * 512 + 512], ALU.add))

                def split_q(i, p):
                    after_free(i, f"q{p}")
                    for h in range(2):
                        last = nc.vector.tensor_copy(qs[0][64 * h:64 * h + 64, p % 2, h, :], qkf[64 * h:64 * h + 64, 2 + p % 2, :])
                    last.then_inc(q_high, 1)
                    dve.wait_ge(q_high, i * PX + p + 1)
                    for h in range(2):
                        last = nc.vector.tensor_tensor(qs[1][64 * h:64 * h + 64, p % 2, h, :], qkf[64 * h:64 * h + 64, 2 + p % 2, :],
                                                       qs[0][64 * h:64 * h + 64, p % 2, h, :], ALU.subtract)
                    last.then_inc(q_low, 1)

                def attend(i, base, first_pair, units, side):
                    n = KEYS if base else S
                    for v, us, ut, uc, pv, po, pl in schedule(units, first_pair):
                        if us is not None:
                            dve.wait_ge(scores_raw, i * U + base + us + 1)
                            nc.vector.tensor_reduce(nmax[:, us % RING:us % RING + 1], ps_s[us % BANKS][:, 0:n], AX.X, ALU.max, negate=True).then_inc(maxed, 1)
                        if 0 <= v - R_LAG < units:
                            r = (v - R_LAG) % RING
                            dve.wait_ge(exped, i * U + base + v - R_LAG + 1 + BANKS)
                            nc.vector.reciprocal(rsum[:, r:r + 1], sums[:, r:r + 1]).then_inc(recip, 1)
                        if uc is not None and uc % 2 == 0:
                            copy_pt(dve, nc.vector.tensor_copy, i, base, first_pair, uc)
                        side(v)
                        if pl is not None:
                            po = pl
                            m = first_pair + po
                            dve.wait_ge(o_high, i * PAIRS + m + 1)
                            nc.vector.tensor_tensor(oT[1][:, po, :], ps_o[:, 0:S], oT[0][:, po, :], ALU.subtract).then_inc(o_split, 1)

                def context(i, name):
                    b = after_act(i, name)
                    free(name, nc.vector.tensor_tensor(cT[1][:], b[:].rearrange("p (k s) -> p k s", k=KD), cT[0][:], ALU.subtract))

                def split_rows(i, name):
                    after_free(i, name)
                    link(i, nc.vector.tensor_copy(xT[0][:], xn[:]))
                    nc.vector.tensor_tensor(xT[1][:], xn[:], xT[0][:], ALU.subtract).then_inc(dve_part, 1)

                def norm_qk(i, name, first):
                    for s in range(ND):
                        dve.wait_ge(act_part, i * ACT_PARTS + ACT_PART[f"{first}qk{s}"])
                        last = nc.vector.tensor_reduce(var[:, s * 8:s * 8 + 8], sq[:, s, :].rearrange("p (h d) -> p h d", d=64), AX.X, ALU.add)
                    link(i, last)
                    nc.vector.tensor_scalar(var[:], var[:], 1.0 / 64, RMS_EPS * RMS_EPS, ALU.mult, ALU.max).then_inc(var_ready, 1)
                    refine_root(i, name, ND * 8)
                    for s in range(ND):
                        nc.vector.tensor_tensor(sq[:, s, :].rearrange("p (h d) -> p h d", d=64), ps_s[s][:].rearrange("p (h d) -> p h d", d=64),
                                                root[:, s * 8:s * 8 + 8].unsqueeze(2).to_broadcast([128, 8, 64]), ALU.mult).then_inc(qk_normed, 1)

                dve.sem_inc(o_split, 2)
                dve.wait_ge(x_loaded, 16)
                norm_stats(0, x)
                norm_apply(0, "first", x, xn, rows_ready)
                context(0, "first ctxT")
                split_rows(0, "first xnT")
                norm_qk(0, "first qk", "first ")
                before = chain[0]
                with dve.Fori(0, B) as i:
                    chain[0] = before
                    after_free(i, "qkT0")
                    after_free(i, "qkT1")
                    nc.vector.tensor_copy(kself[0][:], qkf[:, 2:4, :])
                    for h in range(2):
                        last = nc.vector.tensor_copy(qs[0][64 * h:64 * h + 64, :, h, :], qkf[64 * h:64 * h + 64, 0:2, :])
                    link(i, last)
                    nc.vector.tensor_tensor(kself[1][:], qkf[:, 2:4, :], kself[0][:], ALU.subtract)
                    for h in range(2):
                        last = nc.vector.tensor_tensor(qs[1][64 * h:64 * h + 64, :, h, :], qkf[64 * h:64 * h + 64, 0:2, :],
                                                       qs[0][64 * h:64 * h + 64, :, h, :], ALU.subtract)
                    last.then_inc(dve_part, 1)
                    values(i, 0)
                    values(i, 1)
                    attend(i, 0, 0, U0, lambda v: values(i, 2 + FILL[v]) if FILL.get(v, 2) < 2 else None)
                    b = job(i, "oself")
                    dve.wait_ge(xb_ready, 2 * i + 1)
                    free("oself", nc.vector.tensor_tensor(x1[:], b[:].rearrange("p (t d) -> p t d", t=ND), x[:], ALU.add))
                    after_free(i, "oself")
                    norm_stats(i, x1)
                    norm_apply(i, "x1", x1, x1, rows_ready)
                    b = after_act(i, "x1T")
                    free("x1T", nc.vector.tensor_tensor(xT[1][:], b[:].rearrange("p (k s) -> p k s", k=KD), xT[0][:], ALU.subtract))
                    split_q(i, 0)

                    def side(v):
                        if v % 4 == SIDE and v // 4 + 1 < PX:
                            split_q(i, v // 4 + 1)
                        if v == 5:
                            dve.wait_ge(x_loaded, 16 * i + 32)
                            norm_stats(i, x)
                        if v == 8:
                            norm_apply(i, "xn", x, xn, rows_ready)
                        if v == CTX_SLOT + 2:
                            context(i, "ctxT")
                        if v == XN_SLOT + 2:
                            split_rows(i, "xnT")

                    attend(i, U0, P0, UX, side)
                    norm_qk(i, "qk", "")
                    b = job(i, "ox")
                    dve.wait_ge(xb_ready, 2 * i + 2)
                    dve.wait_ge(s_out, 16 * i + 16)
                    free("ox", nc.vector.tensor_tensor(xo[:], b[:].rearrange("p (t d) -> p t d", t=ND), x1b[:], ALU.add))
                    after_free(i, "ox")
                    norm_stats(i, xo)
                    norm_apply(i, "xo", xo, xo, ln_done)
                    assert chain[0] - before == LINKS, chain[0] - before

            @block.tensor
            def _(pe):
                pe.wait_ge(w_high, len(SPLIT))
                pe.wait_ge(w_low, len(SPLIT))
                pe.wait_ge(s_small, 160)
                pe.wait_ge(s_gc, 6)

                def bank(i, name):
                    pe.wait_ge(job_free[JOB[name] % 2], FREED(i, name) - 1)
                    return ps_j[JOB[name] % 2]

                def product(out, terms):
                    n = 0
                    for stat, mov in terms:
                        for a, b in ((0, 0), (1, 0), (0, 1)):
                            last = nc.tensor.matmul(out, stat[a], mov[b], start=(n == 0), stop=(n == 3 * len(terms) - 1))
                            n += 1
                    return last

                both = lambda t, f: [f(t[0]), f(t[1])]

                def transposed(i, name, src):
                    b = bank(i, name)
                    for k in range(KD):
                        for s in range(ND):
                            last = nc.tensor.transpose(b[:, k * S + s * 128:k * S + s * 128 + 128], src[:, s, k * 128:k * 128 + 128], ident[:])
                    last.then_inc(job_raw, 1)

                def values(i, n):
                    b = bank(i, f"v{n}")
                    s, half = n // 2, n % 2
                    product(b[:], [(both(cT, lambda t: t[:, k, s * 128:s * 128 + 128]), both(wv, lambda t: t[:, k, half * 512:half * 512 + 512]))
                                   for k in range(KD)]).then_inc(job_raw, 1)

                def project(i, name, wt, p, src):
                    b = bank(i, name)
                    product(b[:, 0:S], [(both(wt, lambda t: t[:, k, p * 128:p * 128 + 128]), both(src, lambda t: t[:, k, :]))
                                        for k in range(KD)]).then_inc(job_raw, 1)

                def output(i, name, wt, pairs):
                    b = bank(i, name)
                    for s in range(ND):
                        last = product(b[:, s * D:s * D + D], [(both(oT, lambda t: t[:, p, s * 128:s * 128 + 128]), both(wt, lambda t: t[:, p, :]))
                                                               for p in range(pairs)])
                    last.then_inc(job_raw, 1)

                def attend(i, base, first_pair, units, side):
                    n = KEYS if base else S
                    kx = KX if base else ND
                    for v, us, ut, uc, pv, po, pl in schedule(units, first_pair):
                        if us is not None:
                            p, h, s = us // 4, us // 2 % 2, us % 2
                            if us % 4 == 0 and base:
                                pe.wait_ge(k_low, i * PX + p + 1)
                                pe.wait_ge(q_low, i * PX + p + 1)
                            pe.wait_ge(exped, i * U + base + (us + 1 if us >= BANKS else BANKS))
                            k_parts = both(ks, lambda t: t[:, p, :]) if base else both(kself, lambda t: t[:, p, :])
                            product(ps_s[us % BANKS][:, 0:n], [(both(qs, lambda t: t[:, p % 2, h, s * 128:s * 128 + 128]), k_parts)])\
                                .then_inc(scores_raw, 1)
                        side(v)
                        if ut is not None:
                            g = i * U + base + ut
                            pe.wait_ge(normed, g + 1)
                            pe.wait_ge(pt_copied[ut % 2], i * (U // 2) + (base + ut) // 2 + 1)
                            for k in range(kx):
                                last = nc.tensor.transpose(ps_t[ut % 2][:, k * 128:k * 128 + 128], pexp[ut % RING][:, k * 128:k * 128 + 128], ident[:])
                            last.then_inc(pt_raw, 1)
                        if pv is not None:
                            m = first_pair + pv
                            pe.wait_ge(o_split, i * PAIRS + m + 2)
                            pe.wait_ge(pt_copied[0], i * (U // 2) + 2 * m + 3)
                            pe.wait_ge(pt_copied[1], i * (U // 2) + 2 * m + 3)
                            vals = vx if base else vself
                            for k in range(kx):
                                for h in range(2):
                                    last = nc.tensor.matmul(ps_o[64 * h:64 * h + 64, 0:S], vals[:, k, pv * 128 + 64 * h:pv * 128 + 64 * h + 64],
                                                            pT[:, m % 2, h, k, :], start=(k == 0), stop=(k == kx - 1))
                            last.then_inc(o_raw, 1)

                pe.sem_inc(pt_raw, RING)
                pe.sem_inc(o_raw, 2)
                for b in range(2):
                    pe.sem_inc(job_free[b], 1)
                    pe.sem_inc(pt_copied[b], 1)
                def self_values(i, name):
                    b = bank(i, name)
                    for s in range(ND):
                        last = product(b[:, s * D:s * D + D], [(both(xT, lambda t: t[:, k, s * 128:s * 128 + 128]), both(wqkv, lambda t: t[:, k, 2 * D:3 * D]))
                                                               for k in range(KD)])
                    last.then_inc(job_raw, 1)

                def queries_keys(s):
                    product(ps_s[s][:], [(both(xT, lambda t: t[:, k, s * 128:s * 128 + 128]), both(wqkv, lambda t: t[:, k, 0:2 * D])) for k in range(KD)])\
                        .then_inc(qk_raw, 1)

                pe.wait_ge(ctx_loaded, 16)
                transposed(0, "first ctxT", cx)
                pe.wait_ge(rows_ready, 1)
                transposed(0, "first xnT", xn)
                pe.wait_ge(dve_part, 1)
                self_values(0, "first vself")
                queries_keys(0)
                queries_keys(1)
                with pe.Fori(0, B) as i:
                    project(i, "k0", wk, 0, cT)
                    project(i, "k1", wk, 1, cT)
                    for s in range(ND):
                        b = bank(i, f"qkT{s}")
                        pe.wait_ge(qk_normed, ND * i + s + 1)
                        for k in range(4):
                            last = nc.tensor.transpose(b[:, k * 128:k * 128 + 128], sq[:, s, k * 128:k * 128 + 128], ident[:])
                        last.then_inc(job_raw, 1)
                    values(i, 0)
                    values(i, 1)
                    pe.wait_ge(dve_part, 2 * i + 2)

                    def fill(v):
                        n = FILL.get(v)
                        if n is not None:
                            values(i, 2 + n) if n < 2 else project(i, f"k{n}", wk, n, cT)

                    attend(i, 0, 0, U0, fill)
                    pe.wait_ge(o_split, i * PAIRS + P0 + 2)
                    output(i, "oself", wo0, P0)
                    for p in range(4, PX):
                        project(i, f"k{p}", wk, p, cT)
                    pe.wait_ge(rows_ready, 2 * i + 2)
                    transposed(i, "x1T", x1)
                    pe.wait_ge(job_free[JOB["x1T"] % 2], FREED(i, "x1T"))
                    project(i, "q0", wq, 0, xT)
                    project(i, "q1", wq, 1, xT)

                    def side(v):
                        if v % 4 == Q_SIDE and v // 4 + 2 < PX:
                            project(i, f"q{v // 4 + 2}", wq, v // 4 + 2, xT)
                        if v == CTX_SLOT:
                            pe.wait_ge(ctx_loaded, 16 * i + 32)
                            transposed(i, "ctxT", cx)
                        if v == XN_SLOT:
                            pe.wait_ge(rows_ready, 2 * i + 3)
                            transposed(i, "xnT", xn)
                        if v == QK_SLOT:
                            pe.wait_ge(dve_part, 2 * i + 3)
                            self_values(i, "vself")
                            queries_keys(0)
                            queries_keys(1)

                    attend(i, U0, P0, UX, side)
                    pe.wait_ge(o_split, i * PAIRS + PAIRS + 2)
                    output(i, "ox", wox, PX)


def moe_layer(nc, sems, name, x_in, x_out, w_router, b_router, ln_rows, w_up, b_up, w_down, b_down, slots, results, act, shared, renorm):
    fp32, fp32r, i32, u32 = mybir.dt.float32, mybir.dt.float32r, mybir.dt.int32, mybir.dt.uint32
    T, D = x_in.shape
    F = w_up.shape[3]
    E = w_router.shape[1]
    KD, FT, TT = D // 128, F // 128, T // 128
    TILES_SHARED = T // SLOTS if shared else 0
    TILES_ROUTED = (TOP_K * T + E * (SLOTS - 1)) // SLOTS
    TILES = TILES_SHARED + TILES_ROUTED
    assert TILES % 2 == 1 and TILES_SHARED % 2 == 0 and KD == 2 and FT % 4 == 0
    PAIRS, PAIRS_SHARED = TILES // 2, TILES_SHARED // 2
    DVE_LOWS, POOL_LOWS = FT // 4, FT - FT // 4
    GATHERS = 4
    GROUP = 4
    GROUPS = TT // GROUP
    first_slot = T if shared else 0
    slots, results = slots[0:TILES * SLOTS, :], results[0:TILES * SLOTS, :]
    RING = 4

    ctx = ExitStack()
    with ctx:
        def sb(n, shape, dt=fp32):
            return ctx.enter_context(nc.sbuf_tensor(f"{name}_{n}", shape, dt))

        def sem(n):
            sems.append(nc.alloc_semaphore(f"{name}_{n}"))
            return sems[-1]

        x = sb("x", [128, TT, D])
        xn = sb("xn", [128, TT, D]) if ln_rows is not None else x
        bcast = sb("bcast", [128, 2, D])
        wr = sb("wr", [128, KD, E])
        br = sb("br", [128, E])
        ident = sb("ident", [128, 128])
        tri = sb("tri", [128, 128])
        ones = sb("ones", [128, 128])
        iota_e = sb("iota_e", [128, E])
        tile_start = sb("tile_start", [128, TILES_ROUTED])
        not_first = sb("not_first", [128, E, TT])
        stats = sb("stats", [128, TT, 6])
        mv = sb("mv", [128, TT, 2])
        rstd = sb("rstd", [128, TT])
        xT_r = sb("xT_r", [128, 2, KD, 128])
        prob = sb("prob", [128, TT, E])
        red = sb("red", [128, TT])
        top = sb("top", [128, TT, 8])
        topi = sb("topi", [128, TT, 8], u32)
        topf = sb("topf", [128, TT, 2])
        wt = sb("wt", [128, TT, 2])
        wsum = sb("wsum", [128, TT])
        hot = sb("hot", [128, 2, TT, E])
        hots = sb("hots", [128, TT, E])
        tot = sb("tot", [128, E, TT])
        incl = sb("incl", [128, E, TT])
        rank = sb("rank", [128, TT, E])
        cnt = sb("cnt", [128, 4, E])
        cnt_i = sb("cnt_i", [128, 2, E], i32)
        slot_f = sb("slot_f", [128, 2, TT])
        slot_i = sb("slot_i", [128, 2, TT], i32)
        cmp = sb("cmp", [128, TILES_ROUTED, E])
        te_f = sb("te_f", [128, TILES])
        te = sb("te", [128, TILES], i32)
        b2s = sb("b2s", [E, D])
        ctot = sb("ctot", [128, D])
        rb1a = sb("rb1a", [128, FT])

        xrow = sb("xrow", [128, 2, 2, D])
        xT = sb("xT", [128, 2, 2, KD, SLOTS], fp32r)
        w1 = sb("w1", [128, 2, KD, F])
        w2 = sb("w2", [128, 2, FT, D])
        w1s = [[sb(f"w1s{b}{h}", [128, KD, F], fp32r) for h in range(2)] for b in range(2)]
        w2s = [[sb(f"w2s{b}{h}", [128, FT, D], fp32r) for h in range(2)] for b in range(2)]
        b1 = sb("b1", [128, 2, FT])
        rb1 = sb("rb1", [128, 2, FT])
        hact = sb("hact", [128, RING, SLOTS])
        hs = [sb(f"hs{h}", [128, RING, SLOTS], fp32r) for h in range(2)]
        yrow = sb("yrow", [128, 2, 2, D])
        gath = w1[:].rearrange("p b k f -> p (b k f)").rearrange("p (n d) -> p n d", d=D)
        own = w2[:].rearrange("p b f d -> p (b f) d")

        ps = [ctx.enter_context(nc.psum_tensor(f"{name}_ps{n}", [128, 512], fp32)) for n in range(8)]
        ps_h, ps_c, ps_t, ps_r = ps[0:4], ps[4], ps[6], ps[7]
        ps_hid = [ps[r][:, 0:SLOTS] for r in range(RING)]
        ps_y = [ps[4 + b][:].rearrange("p (s d) -> p s d", s=2) for b in range(2)]

        def weights_of(i, b, kept=False):
            k = b - TILES_SHARED + shared
            return (0, 0, 0) if kept else (i * 2 + k, i + k // 2, k % 2)

        def run_tiles(eng, steps):
            if shared:
                with eng.Fori(0, PAIRS_SHARED - 1) as i:
                    steps(i, 0, True, True, False)
                    steps(i, 1, True, True, False)
                steps(PAIRS_SHARED - 1, 0, True, True, False)
                steps(PAIRS_SHARED - 1, 1, True, False, False)
            with eng.Fori(PAIRS_SHARED, PAIRS) as i:
                steps(i, 0, False, False, False)
                steps(i, 1, False, False, False)
            steps(PAIRS, 0, False, False, True)

        def chunk(c, weights):
            w1v, w2v = weights
            return w1v[:, :, c * 128:(c + 2) * 128] if c % 2 == 0 else w2v[:, c - 1:c + 1, :]

        def low_ready(eng, n, c):
            if c % 4 == 3:
                eng.wait_ge(w_low_dve, (n + 2) * DVE_LOWS + c // 4 + 1)
            else:
                eng.wait_ge(w_low_pool, (n + 2) * POOL_LOWS + c - c // 4 + 1)

        def make_low(op, wb, c, done):
            op(chunk(c, (w1s[wb][1], w2s[wb][1])), chunk(c, (w1[:, wb], w2[:, wb])),
               chunk(c, (w1s[wb][0], w2s[wb][0])), ALU.subtract).then_inc(done, 1)


        s_x = [sem(f"s_x{g}") for g in range(TT // 4)]; s_const = sem("s_const"); s_gconst = sem("s_gconst")
        s_xn = sem("s_xn"); s_tr = sem("s_tr"); s_ev = sem("s_ev"); s_logit = sem("s_logit")
        s_soft = sem("s_soft"); s_exp = sem("s_exp"); s_hot = sem("s_hot"); s_cnt = sem("s_cnt")
        s_slots = sem("s_slots"); s_te = sem("s_te"); s_scat = sem("s_scat"); s_dve = sem("s_dve")
        s_ctw = [sem(f"s_ctw{b}") for b in range(2)]; s_ctb = sem("s_ctb"); s_ctm = sem("s_ctm")
        s_ctp = sem("s_ctp"); s_var = sem("s_var"); s_rstd = sem("s_rstd"); s_ctot = sem("s_ctot")
        xrow_loaded = [sem(f"xrow_loaded{b}") for b in range(2)]
        w_loaded = [sem(f"w_loaded{b}") for b in range(2)]
        xT_raw = sem("xT_raw"); xT_split = sem("xT_split")
        w_high = sem("w_high"); w_low_pool = sem("w_low_pool"); w_low_dve = sem("w_low_dve"); bias_ready = sem("bias_ready")
        h_raw = sem("h_raw"); h_act = sem("h_act"); h_high = sem("h_high"); h_split = sem("h_split"); h_used = sem("h_used")
        y_copied = sem("y_copied"); y_stored = [sem(f"y_stored{b}") for b in range(2)]
        s_gath = [sem(f"s_gath{b}") for b in range(GATHERS)]; s_own = [sem(f"s_own{b}") for b in range(GATHERS)] if shared else None; s_comb = sem("s_comb"); s_norm = sem("s_norm")
        s_out = sem("s_out")

        x_rows = x_in.rearrange("(t p) d -> p t d", p=128)
        out_rows = x_out.rearrange("(t p) d -> p t d", p=128)

        with nc.Block() as block:
            @block.sync
            def _(sp):
                sp.dma_start(wr[:], w_router.rearrange("(k p) e -> p k e", p=128)).then_inc(s_const, 16)
                if b_router is not None:
                    sp.dma_start(br[:], b_router.partition_broadcast(128)).then_inc(s_const, 16)
                if ln_rows is not None:
                    for n in range(2):
                        sp.dma_start(bcast[:, n, :], ln_rows[n].partition_broadcast(128)).then_inc(s_const, 16)
                for c in range(4):
                    sp.dma_start(x[:, c * TT // 4:(c + 1) * TT // 4, :],
                                 x_rows[:, c * TT // 4:(c + 1) * TT // 4, :]).then_inc(s_x[c], 16)
                if b_down is not None:
                    sp.dma_start(b2s[:], b_down).then_inc(s_ctb, 16)
                    for e in range(E):
                        if e >= 2:
                            sp.wait_ge(s_ctm, e - 1)
                        sp.dma_start(w2[:, e % 2, :, :], w_down[e]).then_inc(s_ctw[e % 2], 16)
                        sp.dma_start(b1[:, e % 2, :], b_up[e]).then_inc(s_ctw[e % 2], 16)
                    sp.wait_ge(s_ctm, E)

                def load_rows(i, b, source):
                    tile = i * 2 + b
                    sp.wait_ge(xT_raw, tile + 1)
                    sp.dma_start(xrow[:, b, :, :],
                                 source[bass.ds(tile * SLOTS, SLOTS), :].rearrange("(s p) d -> p s d", p=128)).then_inc(xrow_loaded[b], 16)

                def load_weights(i, b):
                    n, half, wb = weights_of(i, b)
                    e = sp.value_load(te[0:1, bass.ds(i * 2 + b, 1)], min_val=0, max_val=w_up.shape[0] - 1)
                    sp.wait_ge(w_low_pool, (n + 1) * POOL_LOWS)
                    sp.dma_start(w1[:, wb, :, :], w_up[bass.ds(e, 1)].rearrange("a p k f -> p (a k) f")).then_inc(w_loaded[wb], 16)
                    sp.wait_ge(w_low_dve, (n + 1) * DVE_LOWS)
                    sp.dma_start(w2[:, wb, :, :], w_down[bass.ds(e, 1)].rearrange("a p f d -> p (a f) d")).then_inc(w_loaded[wb], 16)
                    if b_up is not None:
                        sp.wait_ge(h_split, n * FT + 1)
                        sp.dma_start(b1[:, wb, :], b_up[bass.ds(e, 1)].rearrange("a p f -> p (a f)")).then_inc(w_loaded[wb], 16)

                if shared:
                    sp.dma_start(w1[:, 0, :, :], w_up[E]).then_inc(w_loaded[0], 16)
                    sp.dma_start(w2[:, 0, :, :], w_down[E]).then_inc(w_loaded[0], 16)
                    with sp.Fori(0, PAIRS_SHARED) as i:
                        load_rows(i, 0, x_in)
                        load_rows(i, 1, x_in)
                sp.wait_ge(s_te, 1)
                load_weights(PAIRS_SHARED, 0)
                sp.wait_ge(s_scat, 16 * 2 * TT)
                with sp.Fori(PAIRS_SHARED, PAIRS) as i:
                    for b in range(2):
                        load_rows(i, b, slots)
                        load_weights(i, b + 1)
                load_rows(PAIRS, 0, slots)
                if shared:
                    sp.wait_ge(y_stored[0], 16 * (PAIRS + 2))
                    sp.wait_ge(y_stored[1], 16 * (PAIRS + 1))
                    for t in range(TT):
                        if t >= GATHERS:
                            sp.wait_ge(s_comb, t - GATHERS + 1)
                        sp.dma_start(own[:, t % GATHERS, :], results[t * 128:(t + 1) * 128, :]).then_inc(s_own[t % GATHERS], 16)
                for g in range(GROUPS):
                    sp.wait_ge(s_norm, GROUP * (g + 1))
                    sp.dma_start(out_rows[:, g * GROUP:(g + 1) * GROUP, :], x[:, g * GROUP:(g + 1) * GROUP, :]).then_inc(s_out, 16)
                sp.wait_ge(s_out, 16 * GROUPS)

            @block.gpsimd
            def _(pool):
                nc.gpsimd.memset(ident[:], 0.0).then_inc(s_gconst, 1)
                nc.gpsimd.memset(ones[:], 1.0).then_inc(s_gconst, 1)
                nc.gpsimd.memset(not_first[:], 1.0).then_inc(s_gconst, 1)
                nc.gpsimd.iota(iota_e[:], [[1, E]], base=0, channel_multiplier=0, allow_small_or_imprecise_dtypes=True).then_inc(s_gconst, 1)
                nc.gpsimd.iota(tile_start[:], [[SLOTS, TILES_ROUTED]], base=0, channel_multiplier=0, allow_small_or_imprecise_dtypes=True).then_inc(s_gconst, 1)
                pool.wait_ge(s_gconst, 5)
                nc.gpsimd.affine_select(out=ident[:], in_=ident[:], compare_op=ALU.not_equal, fill=1.0, base=0,
                                        pattern=[[-1, 128]], channel_multiplier=1).then_inc(s_gconst, 1)
                nc.gpsimd.affine_select(out=tri[:], in_=ones[:], compare_op=ALU.is_gt, fill=0.0, base=0,
                                        pattern=[[1, 128]], channel_multiplier=-1).then_inc(s_gconst, 1)
                nc.gpsimd.memset(not_first[:, :, 0:1], 0.0).then_inc(s_gconst, 1)
                pool.wait_ge(s_slots, 1)
                for t in range(TT):
                    for k in range(2):
                        nc.gpsimd.indirect_dma_start(slots, bass.IndirectOffsetOnAxis(ap=slot_i[:, k, t:t + 1], axis=0),
                                                     xn[:, t, :], None).then_inc(s_scat, 16)

                def low_parts(i, b):
                    n, half, wb = weights_of(i, b)
                    for c in range(FT):
                        if c % 4 != 3:
                            pool.wait_ge(w_high, n * FT + c + 1)
                            make_low(nc.gpsimd.tensor_tensor, wb, c, w_low_pool)

                if shared:
                    low_parts(PAIRS_SHARED, 0)
                with pool.Fori(PAIRS_SHARED, PAIRS) as i:
                    low_parts(i, 1)
                    low_parts(i, 2)
                pool.wait_ge(y_stored[0], 16 * (PAIRS + 2))
                pool.wait_ge(y_stored[1], 16 * (PAIRS + 1))
                for t in range(TT):
                    if t >= GATHERS:
                        pool.wait_ge(s_comb, t - GATHERS + 1)
                    for k in range(2):
                        nc.gpsimd.indirect_dma_start(gath[:, t % GATHERS * 2 + k, :], None, results,
                                                     bass.IndirectOffsetOnAxis(ap=slot_i[:, k, t:t + 1], axis=0)).then_inc(s_gath[t % GATHERS], 16)

            @block.scalar
            def _(act_e):
                def take_root(g, count):
                    act_e.wait_ge(s_var, count)
                    cols = slice(g * GROUP, (g + 1) * GROUP)
                    nc.scalar.activation(rstd[:, cols], rstd[:, cols], ACT.Sqrt).then_inc(s_rstd, 1)

                for g in range(GROUPS):
                    if ln_rows is not None:
                        take_root(g, g + 1)
                    for t in range(g * GROUP, (g + 1) * GROUP):
                        act_e.wait_ge(s_tr, t + 1)
                        if t >= 2:
                            act_e.wait_ge(s_logit, t - 1)
                        nc.scalar.copy(xT_r[:, t % 2, :, :], ps_h[t % 2][:, 0:KD * 128].rearrange("p (k n) -> p k n", k=KD)).then_inc(s_ev, 1)
                act_e.wait_ge(s_soft, 1)
                nc.scalar.activation(prob[:], prob[:], ACT.Exp).then_inc(s_exp, 1)

                def high_part(weights, tile, c):
                    n, half, wb = weights
                    if c == 0:
                        act_e.wait_ge(w_loaded[wb], (half + 1) * W_DMAS * 16)
                        if tile is not None:
                            act_e.wait_ge(h_used, tile * FT + 1)
                    nc.scalar.copy(chunk(c, (w1s[wb][0], w2s[wb][0])), chunk(c, (w1[:, wb], w2[:, wb]))).then_inc(w_high, 1)

                def hidden(i, b, ft, weights):
                    wb = weights[2]
                    n = (i * 2 + b) * FT + ft
                    act_e.wait_ge(h_raw, n + 1)
                    act_e.wait_ge(h_split, n + 2 + FT - RING)
                    if b_up is not None and ft == 0:
                        act_e.wait_ge(w_loaded[wb], (weights[1] + 1) * W_DMAS * 16)
                    nc.scalar.activation(hact[:, ft % RING, :], ps_hid[ft % RING], act,
                                         bias=b1[:, wb, ft:ft + 1] if b_up is not None else 0.0).then_inc(h_act, 1)

                def result(i, b):
                    tile = i * 2 + b
                    act_e.wait_ge(h_used, tile * FT + FT + FT + 1)
                    act_e.wait_ge(y_stored[b], i * 16 + 16)
                    nc.scalar.copy(yrow[:, b, :, :], ps_y[b]).then_inc(y_copied, 1)
                    act_e.wait_ge(y_copied, tile + 3)
                    act_e.dma_start(results[bass.ds(tile * SLOTS, SLOTS), :].rearrange("(s p) d -> p s d", p=128),
                                    yrow[:, b, :, :]).then_inc(y_stored[b], 16)

                W_DMAS = 3 if b_up is not None else 2
                act_e.sem_inc(h_act, RING)
                act_e.sem_inc(y_copied, 2)
                for b in range(2):
                    act_e.sem_inc(y_stored[b], 16)
                first = weights_of(0, 0, shared)
                for c in range(FT):
                    high_part(first, None, c)
                hidden(0, 0, 0, first)
                hidden(0, 0, 1, first)

                def tile_steps(i, b, kept, next_kept, last):
                    ni, nb = (i, 1) if b == 0 else (i + 1, 0)
                    now, nxt = weights_of(i, b, kept), weights_of(i, b + 1, next_kept)
                    for ft in range(FT):
                        if ft + 2 < FT:
                            hidden(i, b, ft + 2, now)
                        elif not last:
                            hidden(ni, nb, ft + 2 - FT, nxt)
                        if not last and not next_kept:
                            high_part(nxt, i * 2 + b + 1, ft)
                    result(i, b)

                run_tiles(act_e, tile_steps)
                for g in range(GROUPS):
                    take_root(g, (GROUPS if ln_rows is not None else 0) + g + 1)

            @block.vector
            def _(dve):
                chain, norms = [0], [0]

                def link(ins):
                    chain[0] += 1
                    ins.then_inc(s_dve, 1)
                    dve.wait_ge(s_dve, chain[0])

                def norm_stats(g):
                    group = range(g * GROUP, (g + 1) * GROUP)
                    for t in group:
                        last = nc.vector.bn_stats(stats[:, t, :], x[:, t, :])
                    link(last)
                    for t in group:
                        last = nc.vector.bn_aggr(mv[:, t, :], stats[:, t, :])
                    link(last)
                    cols = slice(g * GROUP, (g + 1) * GROUP)
                    nc.vector.tensor_scalar(rstd[:, cols], mv[:, cols, 1], LN_EPS, None, ALU.add).then_inc(s_var, 1)

                def inverse_root(g):
                    norms[0] += 1
                    dve.wait_ge(s_rstd, norms[0])
                    cols = slice(g * GROUP, (g + 1) * GROUP)
                    link(nc.vector.reciprocal(rstd[:, cols], rstd[:, cols]))

                dve.wait_ge(s_const, 16 * (1 + (b_router is not None) + 2 * (ln_rows is not None)))
                for g in range(GROUPS):
                    dve.wait_ge(s_x[g], 16)
                    if ln_rows is not None:
                        norm_stats(g)
                        for t in range(g * GROUP, (g + 1) * GROUP):
                            last = nc.vector.scalar_tensor_tensor(xn[:, t, :], x[:, t, :], mv[:, t, 0:1], bcast[:, 0, :], ALU.subtract, ALU.mult)
                        link(last)
                        inverse_root(g)
                        for t in range(g * GROUP, (g + 1) * GROUP):
                            nc.vector.scalar_tensor_tensor(xn[:, t, :], xn[:, t, :], rstd[:, t:t + 1], bcast[:, 1, :], ALU.mult, ALU.add).then_inc(s_xn, 1)
                dve.wait_ge(s_logit, TT)
                dve.wait_ge(s_gconst, 8)
                logits = ps_r[:, 0:TT * E].rearrange("p (t e) -> p t e", e=E)
                if b_router is not None:
                    link(nc.vector.tensor_tensor(prob[:], logits, br[:].unsqueeze(1).to_broadcast([128, TT, E]), ALU.add))
                else:
                    link(nc.vector.tensor_copy(prob[:], logits))
                link(nc.vector.tensor_reduce(red[:], prob[:], AX.X, ALU.max))
                nc.vector.tensor_tensor(prob[:], prob[:], red[:].unsqueeze(2).to_broadcast([128, TT, E]), ALU.subtract).then_inc(s_soft, 1)
                dve.wait_ge(s_exp, 1)
                link(nc.vector.tensor_reduce(red[:], prob[:], AX.X, ALU.add))
                link(nc.vector.reciprocal(red[:], red[:]))
                link(nc.vector.tensor_tensor(prob[:], prob[:], red[:].unsqueeze(2).to_broadcast([128, TT, E]), ALU.mult))
                for t in range(TT):
                    last = nc.vector.max(top[:, t, :], prob[:, t, :])
                link(last)
                for t in range(TT):
                    last = nc.vector.max_index(topi[:, t, :], top[:, t, :], prob[:, t, :])
                link(last)
                nc.vector.tensor_copy(topf[:], topi[:, :, 0:2])
                link(nc.vector.tensor_tensor(wsum[:], top[:, :, 0], top[:, :, 1], ALU.add))
                if renorm:
                    link(nc.vector.reciprocal(red[:], wsum[:]))
                    link(nc.vector.tensor_tensor(wt[:], top[:, :, 0:2], red[:].unsqueeze(2).to_broadcast([128, TT, 2]), ALU.mult))
                else:
                    link(nc.vector.tensor_copy(wt[:], top[:, :, 0:2]))
                for k in range(2):
                    last = nc.vector.tensor_tensor(hot[:, k, :, :], iota_e[:].unsqueeze(1).to_broadcast([128, TT, E]),
                                                   topf[:, :, k:k + 1].to_broadcast([128, TT, E]), ALU.is_equal)
                link(last)
                nc.vector.tensor_tensor(hots[:], hot[:, 0, :, :], hot[:, 1, :, :], ALU.add).then_inc(s_hot, 1)
                dve.wait_ge(s_cnt, 1)
                link(nc.vector.tensor_copy(tot[:], ps_h[3][:, 0:TT * E].rearrange("p (t e) -> p e t", e=E)))
                link(nc.vector.tensor_tensor_scan(incl[:].rearrange("p e t -> p (e t)"), not_first[:].rearrange("p e t -> p (e t)"),
                                                  tot[:].rearrange("p e t -> p (e t)"), 0.0, ALU.mult, ALU.add))
                link(nc.vector.tensor_tensor(tot[:], incl[:], tot[:], ALU.subtract))
                link(nc.vector.tensor_scalar(cnt_i[:, 0, :], incl[:, :, TT - 1], float(SLOTS - 1), None, ALU.add))
                link(nc.vector.tensor_scalar(cnt_i[:, 1, :], cnt_i[:, 0, :], SLOT_BITS, SLOT_BITS, ALU.logical_shift_right, ALU.logical_shift_left))
                link(nc.vector.tensor_copy(cnt[:, 2, :], cnt_i[:, 1, :]))
                link(nc.vector.tensor_tensor_scan(cnt[:, 3, :], ones[:, 0:E], cnt[:, 2, :], 0.0, ALU.mult, ALU.add))
                link(nc.vector.tensor_tensor(cnt[:, 0, :], cnt[:, 3, :], cnt[:, 2, :], ALU.subtract))
                link(nc.vector.tensor_tensor(rank[:], ps_h[2][:, 0:TT * E].rearrange("p (t e) -> p t e", e=E),
                                             tot[:].rearrange("p e t -> p t e"), ALU.add))
                link(nc.vector.tensor_tensor(rank[:], rank[:], cnt[:, 0, :].unsqueeze(1).to_broadcast([128, TT, E]), ALU.add))
                for k in range(2):
                    last = nc.vector.tensor_tensor(hot[:, k, :, :], hot[:, k, :, :], rank[:], ALU.mult)
                link(last)
                for k in range(2):
                    last = nc.vector.tensor_reduce(slot_f[:, k, :], hot[:, k, :, :], AX.X, ALU.add)
                link(last)
                nc.vector.tensor_scalar(slot_i[:], slot_f[:], float(first_slot), None, ALU.add).then_inc(s_slots, 1)
                link(nc.vector.tensor_tensor(cmp[:], cnt[:, 3, :].unsqueeze(1).to_broadcast([128, TILES_ROUTED, E]),
                                             tile_start[:].unsqueeze(2).to_broadcast([128, TILES_ROUTED, E]), ALU.is_le))
                if shared:
                    link(nc.vector.memset(te_f[:], float(E)))
                link(nc.vector.tensor_reduce(te_f[:, TILES_SHARED:TILES], cmp[:], AX.X, ALU.add))
                link(nc.vector.tensor_scalar(te_f[:, TILES_SHARED:TILES], te_f[:, TILES_SHARED:TILES], float(E - 1), None, ALU.min))
                nc.vector.tensor_copy(te[:], te_f[:]).then_inc(s_te, 1)
                if b_down is not None:
                    for e in range(E):
                        dve.wait_ge(s_ctw[e % 2], (e // 2 + 1) * 32)
                        if e >= 1:
                            dve.wait_ge(s_ctm, e)
                        nc.vector.tensor_scalar(rb1a[:], b1[:, e % 2, :], 0.0, None, ALU.max).then_inc(s_ctp, 1)
                    dve.wait_ge(s_ctm, E + 1)
                    nc.vector.tensor_copy(ctot[:], ps_c[:, 0:D]).then_inc(s_ctot, 1)
                    link(nc.vector.tensor_scalar(x[:], x[:], 2.0, None, ALU.mult))

                def split_x(i, b):
                    tile = i * 2 + b
                    dve.wait_ge(xT_raw, tile + 3)
                    view = ps_t[:, 0:KD * SLOTS].rearrange("p (k n) -> p k n", k=KD)
                    nc.vector.tensor_copy(xT[:, b, 0, :, :], view).then_inc(xT_split, 1)
                    dve.wait_ge(xT_split, 2 * tile + 2)
                    nc.vector.tensor_tensor(xT[:, b, 1, :, :], view, xT[:, b, 0, :, :], ALU.subtract).then_inc(xT_split, 1)

                def split_hidden(i, b, ft, weights):
                    half, wb = weights[1:]
                    n = (i * 2 + b) * FT + ft
                    r = ft % RING
                    if b_up is not None and ft == 0:
                        dve.wait_ge(w_loaded[wb], (half + 1) * 48)
                        nc.vector.tensor_scalar(rb1[:, wb, :], b1[:, wb, :], 0.0, None, ALU.max).then_inc(bias_ready, 1)
                        dve.wait_ge(bias_ready, i * 2 + b + 1)
                    dve.wait_ge(h_act, n + 1 + RING)
                    dve.wait_ge(h_used, n + 2 + FT - RING)
                    if b_up is not None:
                        nc.vector.tensor_scalar(hs[0][:, r, :], hact[:, r, :], rb1[:, wb, ft:ft + 1], None, ALU.subtract).then_inc(h_high, 1)
                        dve.wait_ge(h_high, n + 1)
                        nc.vector.scalar_tensor_tensor(hs[1][:, r, :], hact[:, r, :], rb1[:, wb, ft:ft + 1], hs[0][:, r, :],
                                                       ALU.subtract, ALU.subtract).then_inc(h_split, 1)
                    else:
                        nc.vector.tensor_copy(hs[0][:, r, :], hact[:, r, :]).then_inc(h_high, 1)
                        dve.wait_ge(h_high, n + 1)
                        nc.vector.tensor_tensor(hs[1][:, r, :], hact[:, r, :], hs[0][:, r, :], ALU.subtract).then_inc(h_split, 1)

                dve.sem_inc(h_split, FT + 1)
                dve.sem_inc(xT_split, 1)
                dve.sem_inc(w_low_pool, 2 * POOL_LOWS)
                dve.sem_inc(w_low_dve, 2 * DVE_LOWS)
                first = weights_of(0, 0, shared)
                for c in range(FT):
                    dve.wait_ge(w_high, c + 1)
                    make_low(nc.vector.tensor_tensor, 0, c, w_low_dve if c % 4 == 3 else w_low_pool)
                split_x(0, 0)
                split_hidden(0, 0, 0, first)
                split_hidden(0, 0, 1, first)

                def tile_steps(i, b, kept, next_kept, last):
                    ni, nb = (i, 1) if b == 0 else (i + 1, 0)
                    now, nxt = weights_of(i, b, kept), weights_of(i, b + 1, next_kept)
                    for ft in range(FT):
                        if ft == FT // 2 and not last:
                            split_x(ni, nb)
                        if ft + 2 < FT:
                            split_hidden(i, b, ft + 2, now)
                        elif not last:
                            split_hidden(ni, nb, ft + 2 - FT, nxt)
                        if ft % 4 == 3 and not last and not next_kept:
                            n, half, wb = nxt
                            dve.wait_ge(w_high, n * FT + ft + 1)
                            make_low(nc.vector.tensor_tensor, wb, ft, w_low_dve)

                run_tiles(dve, tile_steps)

                for g in range(GROUPS):
                    for t in range(g * GROUP, (g + 1) * GROUP):
                        dve.wait_ge(s_gath[t % GATHERS], 16 * 2 * (t // GATHERS + 1))
                        r = t % GATHERS * 2
                        link(nc.vector.scalar_tensor_tensor(x[:, t, :], gath[:, r, :], wt[:, t, 0:1], x[:, t, :], ALU.mult, ALU.add))
                        link(nc.vector.scalar_tensor_tensor(x[:, t, :], gath[:, r + 1, :], wt[:, t, 1:2], x[:, t, :], ALU.mult, ALU.add))
                        if shared:
                            dve.wait_ge(s_own[t % GATHERS], 16 * (t // GATHERS + 1))
                            nc.vector.tensor_tensor(x[:, t, :], own[:, t % GATHERS, :], x[:, t, :], ALU.add).then_inc(s_comb, 1)
                        else:
                            nc.vector.scalar_tensor_tensor(x[:, t, :], ctot[:], wsum[:, t:t + 1], x[:, t, :], ALU.mult, ALU.add).then_inc(s_comb, 1)
                    dve.wait_ge(s_comb, (g + 1) * GROUP)
                    norm_stats(g)
                    inverse_root(g)
                    for t in range(g * GROUP, (g + 1) * GROUP):
                        nc.vector.tensor_scalar(x[:, t, :], x[:, t, :], mv[:, t, 0:1], rstd[:, t:t + 1], ALU.subtract, ALU.mult).then_inc(s_norm, 1)

            @block.tensor
            def _(pe):
                pe.wait_ge(s_gconst, 8)
                pe.wait_ge(s_const, 16)

                def router_logits(t):
                    pe.wait_ge(s_ev, t + 1)
                    for k in range(KD):
                        last = nc.tensor.matmul(ps_r[:, t * E:(t + 1) * E], xT_r[:, t % 2, k, :], wr[:, k, :],
                                                start=(k == 0), stop=(k == KD - 1))
                    last.then_inc(s_logit, 1)

                for t in range(TT):
                    if ln_rows is not None:
                        pe.wait_ge(s_xn, t + 1)
                    elif t % GROUP == 0:
                        pe.wait_ge(s_x[t // GROUP], 16)
                    if t >= 2:
                        pe.wait_ge(s_ev, t - 1)
                    for k in range(KD):
                        last = nc.tensor.transpose(ps_h[t % 2][:, k * 128:(k + 1) * 128], xn[:, t, k * 128:(k + 1) * 128], ident[:])
                    last.then_inc(s_tr, 1)
                    if t >= 1:
                        router_logits(t - 1)
                router_logits(TT - 1)
                pe.wait_ge(s_hot, 1)
                hot_cols = hots[:].rearrange("p t e -> p (t e)")
                nc.tensor.matmul(ps_h[2][:, 0:TT * E], tri[:], hot_cols, start=True, stop=True)
                nc.tensor.matmul(ps_h[3][:, 0:TT * E], ones[:], hot_cols, start=True, stop=True).then_inc(s_cnt, 1)
                if b_down is not None:
                    for e in range(E):
                        pe.wait_ge(s_ctp, e + 1)
                        for ft in range(FT):
                            last = nc.tensor.matmul(ps_c[:, 0:D], rb1a[:, ft:ft + 1].to_broadcast([128, 128]), w2[:, e % 2, ft, :],
                                                    start=(e == 0 and ft == 0), stop=False)
                        last.then_inc(s_ctm, 1)
                    pe.wait_ge(s_ctb, 16)
                    nc.tensor.matmul(ps_c[:, 0:D], ones[0:E, :], b2s[:], start=False, stop=True).then_inc(s_ctm, 1)

                def transposes(i, b):
                    tile = i * 2 + b
                    pe.wait_ge(xrow_loaded[b], (i + 1) * 16)
                    pe.wait_ge(xT_split, 2 * tile + 1)
                    for k in range(KD):
                        for s in range(2):
                            last = nc.tensor.transpose(ps_t[:, k * SLOTS + s * 128:k * SLOTS + (s + 1) * 128],
                                                       xrow[:, b, s, k * 128:(k + 1) * 128], ident[:])
                    last.then_inc(xT_raw, 1)

                def up(i, b, ft, weights):
                    number, half, wb = weights
                    n = (i * 2 + b) * FT + ft
                    if ft == 0:
                        pe.wait_ge(xT_split, 4 * i + 2 * b + 3)
                    if ft % 2 == 0:
                        low_ready(pe, number, ft)
                    pe.wait_ge(h_act, n + 1)
                    for k in range(KD):
                        for wp, xp in ((0, 0), (1, 0), (0, 1)):
                            last = nc.tensor.matmul(ps_hid[ft % RING], w1s[wb][wp][:, k, ft * 128:(ft + 1) * 128],
                                                    xT[:, b, xp, k, :], start=(k == 0 and wp == 0 and xp == 0),
                                                    stop=(k == KD - 1 and xp == 1))
                    last.then_inc(h_raw, 1)

                def down(i, b, ft, weights):
                    number, half, wb = weights
                    n = (i * 2 + b) * FT + ft
                    if ft == 0:
                        pe.wait_ge(y_copied, i * 2 + b + 1)
                    if ft % 2 == 0:
                        low_ready(pe, number, ft + 1)
                    pe.wait_ge(h_split, n + 2 + FT)
                    for s in range(2):
                        for hp, wp in ((0, 0), (1, 0), (0, 1)):
                            last = nc.tensor.matmul(ps_y[b][:, s, :], hs[hp][:, ft % RING, s * 128:(s + 1) * 128],
                                                    w2s[wb][wp][:, ft, :], start=(ft == 0 and s == 0 and hp == 0 and wp == 0),
                                                    stop=(ft == FT - 1 and wp == 1 and s == 1))
                    last.then_inc(h_used, 1)

                pe.sem_inc(xT_raw, 2)
                pe.sem_inc(h_used, FT + 1)
                if b_down is not None:
                    pe.wait_ge(s_ctot, 1)
                transposes(0, 0)
                first = weights_of(0, 0, shared)
                up(0, 0, 0, first)
                up(0, 0, 1, first)

                def tile_steps(i, b, kept, next_kept, last):
                    ni, nb = (i, 1) if b == 0 else (i + 1, 0)
                    now, nxt = weights_of(i, b, kept), weights_of(i, b + 1, next_kept)
                    for ft in range(FT):
                        if ft == FT // 2 and not last:
                            transposes(ni, nb)
                        if ft + 2 < FT:
                            up(i, b, ft + 2, now)
                        elif not last:
                            up(ni, nb, ft + 2 - FT, nxt)
                        down(i, b, ft, now)

                run_tiles(pe, tile_steps)


def state_space_layer(nc, sems, x_in, x_out, w):
    fp32, fp32r = mybir.dt.float32, mybir.dt.float32r
    B, S, D = x_in.shape
    T, KD, TT = B * S, D // 128, B * S // 128
    N = w["a_log"].shape[2]
    R = w["dt_w"].shape[0]
    RBC = R + 2 * N
    CH = T // 512

    ctx = ExitStack()
    with ctx:
        def sb(n, shape, dt=fp32):
            return ctx.enter_context(nc.sbuf_tensor(f"s_{n}", shape, dt))

        def sem(n):
            sems.append(nc.alloc_semaphore(f"s_{n}"))
            return sems[-1]

        x = sb("x", [128, TT, D])
        xT = sb("xT", [128, KD, T])
        delta = sb("delta", [128, KD, T])
        dx = sb("dx", [128, KD, T])
        y = x[:].rearrange("p t d -> p (t d)").rearrange("p (k n) -> p k n", k=KD)
        proj = sb("proj", [128, KD, RBC])
        dtw = sb("dtw", [RBC, D])
        dtb = sb("dtb", [128, KD])
        dskip = sb("dskip", [128, KD])
        neg_a = sb("neg_a", [128, KD, N])
        ident = sb("ident", [128, 128])
        ident_r = sb("ident_r", [128, 128], fp32r)
        rbc = sb("rbc", [RBC, T])
        rbc_p = [sb(f"rbc{n}", [RBC, T], fp32r) for n in range(2)]
        decay = sb("decay", [128, 2, T])
        inp = sb("inp", [128, 2, T])
        h = sb("h", [128, 2, T])
        hc = sb("hc", [128, 2, T])
        stats = sb("stats", [128, TT, 6])
        mv = sb("mv", [128, TT, 2])
        rstd = sb("rstd", [128, TT])
        one = sb("one", [128, 1])
        rows = decay[:].rearrange("p a n -> p (a n)").rearrange("p (t d) -> p t d", t=TT)

        bank = [ctx.enter_context(nc.psum_tensor(f"s_ps{n}", [128, 512], fp32)) for n in range(8)]
        s_x = sem("s_x"); s_w = sem("s_w"); s_gc = sem("s_gc"); s_ext = sem("s_ext"); s_zero = sem("s_zero")
        xt_raw = sem("xt_raw"); xt_copied = sem("xt_copied"); rbc_raw = sem("rbc_raw"); rbc_copied = sem("rbc_copied")
        rbc_split = sem("rbc_split"); dt_raw = sem("dt_raw"); dt_biased = sem("dt_biased"); dt_soft = sem("dt_soft"); dt_ready = sem("dt_ready")
        a_exp = sem("a_exp"); a_ready = sem("a_ready")
        b_raw = sem("b_raw"); c_raw = sem("c_raw"); decayed = sem("decayed"); cut = sem("cut"); inp_ready = sem("inp_ready")
        scanned = sem("scanned"); weighted = sem("weighted"); summed = sem("summed")
        y_init = sem("y_init"); yt_raw = sem("yt_raw"); yt_copied = sem("yt_copied"); s_dve = sem("s_dve"); s_var = sem("s_var"); s_rstd = sem("s_rstd")
        s_norm = sem("s_norm"); s_out = sem("s_out"); e_done = sem("e_done")

        x_rows = x_in.rearrange("a (t p) d -> p (a t) d", p=128)
        out_rows = x_out.rearrange("a (t p) d -> p (a t) d", p=128)

        with nc.Block() as block:
            @block.sync
            def _(sp):
                for c in range(4):
                    sp.dma_start(x[:, c * TT // 4:(c + 1) * TT // 4, :], x_rows[:, c * TT // 4:(c + 1) * TT // 4, :]).then_inc(s_x, 16)
                sp.wait_ge(s_zero, 1)
                for dst, src in ((proj[:], w["proj"]), (dtw[0:R, :], w["dt_w"]), (dtb[:], w["dt_b"]), (dskip[:], w["d"]), (neg_a[:], w["a_log"])):
                    sp.dma_start(dst, src).then_inc(s_w, 16)
                for c in range(4):
                    sp.wait_ge(s_norm, (c + 1) * TT // 4)
                    sp.dma_start(out_rows[:, c * TT // 4:(c + 1) * TT // 4, :], rows[:, c * TT // 4:(c + 1) * TT // 4, :]).then_inc(s_out, 16)
                sp.wait_ge(s_out, 64)

            @block.gpsimd
            def _(pool):
                nc.gpsimd.memset(one[:], 1.0).then_inc(s_ext, 1)
                nc.gpsimd.memset(dtw[:], 0.0).then_inc(s_zero, 1)
                pool.wait_ge(s_zero, 1)
                nc.gpsimd.memset(ident[:], 0.0).then_inc(s_gc, 1)
                pool.wait_ge(s_gc, 1)
                nc.gpsimd.affine_select(out=ident[:], in_=ident[:], compare_op=ALU.not_equal, fill=1.0, base=0,
                                        pattern=[[-1, 128]], channel_multiplier=1).then_inc(s_gc, 1)
                pool.wait_ge(s_gc, 2)
                nc.gpsimd.tensor_copy(ident_r[:], ident[:]).then_inc(s_gc, 1)
                pool.wait_ge(y_init, 1)
                for n in range(N):
                    for k in range(KD):
                        u = n * KD + k
                        pool.wait_ge(weighted, u + 1)
                        if u >= KD:
                            pool.wait_ge(summed, u - KD + 1)
                        nc.gpsimd.tensor_tensor(y[:, k, :], y[:, k, :], hc[:, k, :], ALU.add).then_inc(summed, 1)

            @block.scalar
            def _(act):
                nc.scalar.preload_act_table_set("natural_log_exp_and_others")
                for t in range(TT):
                    act.wait_ge(xt_raw, t + 1)
                    nc.scalar.copy(xT[:, :, t * 128:t * 128 + 128], bank[t % 4][:, 0:256].rearrange("p (k s) -> p k s", k=KD)).then_inc(xt_copied, 1)
                act.wait_ge(s_w, 80)
                act.wait_ge(s_ext, 1)
                nc.scalar.activation(neg_a[:], neg_a[:], ACT.Exp).then_inc(a_exp, 1)
                for c in range(CH):
                    act.wait_ge(rbc_raw, c + 1)
                    nc.scalar.copy(rbc[:, c * 512:c * 512 + 512], bank[4 + c % 2][0:RBC, :]).then_inc(rbc_copied, 1)
                for k in range(KD):
                    act.wait_ge(dt_biased, (k + 1) * CH)
                    nc.scalar.activation(delta[:, k, :], delta[:, k, :], ACT.Exp).then_inc(e_done, 1)
                    act.wait_ge(e_done, k + 1)
                    nc.scalar.activation(delta[:, k, :], delta[:, k, :], ACT.Ln, bias=one[:, 0:1]).then_inc(dt_soft, 1)
                act.wait_ge(a_ready, 1)
                for n in range(N):
                    for k in range(KD):
                        u = n * KD + k
                        if n == 0:
                            act.wait_ge(dt_ready, KD * 2)
                        if u >= 2:
                            act.wait_ge(scanned, u - 1)
                        nc.scalar.activation(decay[:, u % 2, :], delta[:, k, :], ACT.Exp, scale=neg_a[:, k, n:n + 1]).then_inc(decayed, 1)
                act.wait_ge(scanned, N * KD)
                for t in range(TT):
                    act.wait_ge(yt_raw, t + 1)
                    nc.scalar.copy(rows[:, t, :], bank[t % 4][:, 0:256]).then_inc(yt_copied, 1)
                act.wait_ge(s_var, 1)
                nc.scalar.activation(rstd[:], rstd[:], ACT.Sqrt).then_inc(s_rstd, 1)

            @block.vector
            def _(dve):
                chain = [0]

                def link(ins):
                    chain[0] += 1
                    ins.then_inc(s_dve, 1)
                    dve.wait_ge(s_dve, chain[0])

                dve.wait_ge(a_exp, 1)
                nc.vector.tensor_scalar(neg_a[:], neg_a[:], -1.0, None, ALU.mult).then_inc(a_ready, 1)
                for c in range(CH):
                    dve.wait_ge(rbc_copied, c + 1)
                    part = slice(c * 512, c * 512 + 512)
                    link(nc.vector.tensor_copy(rbc_p[0][:, part], rbc[:, part]))
                    nc.vector.tensor_tensor(rbc_p[1][:, part], rbc[:, part], rbc_p[0][:, part], ALU.subtract).then_inc(rbc_split, 1)
                for k in range(KD):
                    for c in range(CH):
                        u = k * CH + c
                        dve.wait_ge(dt_raw, u + 1)
                        nc.vector.tensor_scalar(delta[:, k, c * 512:c * 512 + 512], bank[6 + u % 2][:], dtb[:, k:k + 1], 20.0, ALU.add, ALU.min).then_inc(dt_biased, 1)
                for k in range(KD):
                    dve.wait_ge(dt_soft, k + 1)
                    nc.vector.tensor_scalar(delta[:, k, :], delta[:, k, :], DT_MIN, DT_MAX, ALU.max, ALU.min).then_inc(dt_ready, 1)
                    dve.wait_ge(dt_ready, 2 * k + 1)
                    nc.vector.tensor_tensor(dx[:, k, :], delta[:, k, :], xT[:, k, :], ALU.mult).then_inc(dt_ready, 1)
                dve.wait_ge(dt_ready, 2 * KD)
                for k in range(KD):
                    last = nc.vector.scalar_tensor_tensor(y[:, k, :], xT[:, k, :], dskip[:, k:k + 1], xT[:, k, :], ALU.mult, ALU.add)
                last.then_inc(y_init, 1)

                def weigh(n, k):
                    u = n * KD + k
                    dve.wait_ge(scanned, u + 1)
                    dve.wait_ge(c_raw, n + 1)
                    if u >= KD:
                        dve.wait_ge(summed, u - KD + 1)
                    for c in range(CH):
                        last = nc.vector.tensor_tensor(hc[:, k, c * 512:c * 512 + 512], h[:, k, c * 512:c * 512 + 512], bank[4 + c][:], ALU.mult)
                    last.then_inc(weighted, 1)

                for n in range(N):
                    for k in range(KD):
                        u = n * KD + k
                        dve.wait_ge(b_raw, n + 1)
                        for c in range(CH):
                            last = nc.vector.tensor_tensor(inp[:, k, c * 512:c * 512 + 512], dx[:, k, c * 512:c * 512 + 512], bank[c][:], ALU.mult)
                        last.then_inc(inp_ready, 1)
                        dve.wait_ge(decayed, u + 1)
                        nc.vector.memset(decay[:, u % 2, :].rearrange("p (a s) -> p a s", s=S)[:, :, 0:1], 0.0).then_inc(cut, 1)
                        dve.wait_ge(inp_ready, u + 1)
                        dve.wait_ge(cut, u + 1)
                        nc.vector.tensor_tensor_scan(h[:, k, :], decay[:, u % 2, :], inp[:, k, :], 0.0, ALU.mult, ALU.add).then_inc(scanned, 1)
                        if u >= 1:
                            weigh((u - 1) // KD, (u - 1) % KD)
                weigh(N - 1, KD - 1)
                for t in range(TT):
                    dve.wait_ge(yt_copied, t + 1)
                    last = nc.vector.bn_stats(stats[:, t, :], rows[:, t, :])
                link(last)
                for t in range(TT):
                    last = nc.vector.bn_aggr(mv[:, t, :], stats[:, t, :])
                link(last)
                nc.vector.tensor_scalar(rstd[:], mv[:, :, 1], LN_EPS, None, ALU.add).then_inc(s_var, 1)
                dve.wait_ge(s_rstd, 1)
                link(nc.vector.reciprocal(rstd[:], rstd[:]))
                for t in range(TT):
                    nc.vector.tensor_scalar(rows[:, t, :], rows[:, t, :], mv[:, t, 0:1], rstd[:, t:t + 1], ALU.subtract, ALU.mult).then_inc(s_norm, 1)

            @block.tensor
            def _(pe):
                pe.wait_ge(s_gc, 3)
                for t in range(TT):
                    if t % (TT // 4) == 0:
                        pe.wait_ge(s_x, 64)
                    if t >= 4:
                        pe.wait_ge(xt_copied, t - 3)
                    for k in range(KD):
                        last = nc.tensor.transpose(bank[t % 4][:, k * 128:k * 128 + 128], x[:, t, k * 128:k * 128 + 128], ident[:])
                    last.then_inc(xt_raw, 1)
                pe.wait_ge(s_w, 80)
                for c in range(CH):
                    pe.wait_ge(xt_copied, (c + 1) * TT // CH)
                    if c >= 2:
                        pe.wait_ge(rbc_copied, c - 1)
                    for k in range(KD):
                        last = nc.tensor.matmul(bank[4 + c % 2][0:RBC, :], proj[:, k, :], xT[:, k, c * 512:c * 512 + 512], start=(k == 0), stop=(k == KD - 1))
                    last.then_inc(rbc_raw, 1)
                for k in range(KD):
                    for c in range(CH):
                        u = k * CH + c
                        pe.wait_ge(rbc_copied, c + 1)
                        if u >= 2:
                            pe.wait_ge(dt_biased, u - 1)
                        nc.tensor.matmul(bank[6 + u % 2][:], dtw[:, k * 128:k * 128 + 128], rbc[:, c * 512:c * 512 + 512], start=True, stop=True).then_inc(dt_raw, 1)

                def spread(banks, row, done):
                    for c in range(CH):
                        for part in range(2):
                            last = nc.tensor.matmul(banks[c][:], ident_r[0:RBC, row:row + 1].to_broadcast([RBC, 128]),
                                                    rbc_p[part][:, c * 512:c * 512 + 512], start=(part == 0), stop=(part == 1))
                    last.then_inc(done, 1)

                pe.wait_ge(rbc_split, CH)
                pe.wait_ge(dt_biased, KD * CH)
                for n in range(N):
                    if n >= 1:
                        pe.wait_ge(inp_ready, n * KD)
                    spread(bank[0:4], R + n, b_raw)
                    if n >= 1:
                        pe.wait_ge(weighted, n * KD)
                    spread(bank[4:8], R + N + n, c_raw)
                pe.wait_ge(summed, N * KD)
                pe.wait_ge(inp_ready, N * KD)
                for t in range(TT):
                    if t >= 4:
                        pe.wait_ge(yt_copied, t - 3)
                    for k in range(KD):
                        last = nc.tensor.transpose(bank[t % 4][:, k * 128:k * 128 + 128], y[:, k, t * 128:t * 128 + 128], ident[:])
                    last.then_inc(yt_raw, 1)


def linear_attention_layer(nc, sems, x_in, ctx_in, x_out, w):
    fp32 = mybir.dt.float32
    B, S, D = x_in.shape
    KD, TT, ND = D // 128, B * S // 128, S // 128
    T = B * S
    HD = 16

    ctx = ExitStack()
    with ctx:
        def sb(n, shape, dt=fp32):
            return ctx.enter_context(nc.sbuf_tensor(f"l_{n}", shape, dt))

        def sem(n):
            sems.append(nc.alloc_semaphore(f"l_{n}"))
            return sems[-1]

        x = sb("x", [128, TT, D])
        cx = sb("cx", [128, TT, D])
        xT = sb("xT", [128, KD, T])
        cT = sb("cT", [128, KD, T])
        kT = sb("kT", [128, KD, T])
        kR = sb("kR", [128, TT, D])
        v = sb("v", [128, TT, D])
        qT = sb("qT", [128, KD, T])
        cm = sb("cm", [128, B, KD, 128])
        att = cT
        wts = {n: sb(n, [128, KD, D]) for n in ("wq", "wk", "wv", "wo")}
        bq = sb("bq", [128, KD])
        bk = sb("bk", [128, KD])
        bv = sb("bv", [128, D])
        bo = sb("bo", [128, D])
        mask = sb("mask", [128, KD, 128])
        ident = sb("ident", [128, 128])
        nmax = sb("nmax", [128, KD, B])
        sums = sb("sums", [128, KD, B])
        stats = sb("stats", [128, TT, 6])
        mv = sb("mv", [128, TT, 2])
        rstd = sb("rstd", [128, TT])
        bank = [ctx.enter_context(nc.psum_tensor(f"l_ps{n}", [128, 512], fp32)) for n in range(8)]

        JOBS = ([(f"cT{b}", "act" if b % 2 else "dve") for b in range(B)]
                + [(f"k{m}{c}", "act") for c in range(T // 512) for m in range(KD)]
                + [(f"v{b}", "dve") for b in range(B)]
                + [(f"xT{b}", "act") for b in range(B)]
                + [(f"q{m}{c}", "act") for c in range(T // 512) for m in range(KD)]
                + [(f"kR{b}", "act") for b in range(B)]
                + [(f"c{b}", "dve") for b in range(B)]
                + [(f"a{b}", "act") for b in range(B)]
                + [(f"o{b}", "dve") for b in range(B)])
        NUMBER = {n: j for j, (n, _) in enumerate(JOBS)}
        ENGINE = dict(JOBS)
        COUNT = {n: sum(e == ENGINE[n] for _, e in JOBS[:NUMBER[n] + 1]) for n in NUMBER}

        s_x = sem("s_x"); s_cx = sem("s_cx"); s_w = sem("s_w"); s_gc = sem("s_gc"); raw = sem("raw")
        out_of = {"act": sem("out_act"), "dve": sem("out_dve")}
        kmaxed = sem("kmaxed"); kexped = sem("kexped"); s_rs = sem("s_rs"); s_xb = sem("s_xb")
        s_dve = sem("s_dve"); s_var = sem("s_var"); s_rstd = sem("s_rstd"); s_norm = sem("s_norm"); s_out = sem("s_out")

        rows_of = lambda a: a.rearrange("a (t p) d -> p (a t) d", p=128)
        x_rows, cx_rows, out_rows = rows_of(x_in), rows_of(ctx_in), rows_of(x_out)
        QT4 = TT // 4

        with nc.Block() as block:
            @block.sync
            def _(sp):
                for dst, src in [(wts[n][:], w[n]) for n in ("wk", "wv")]:
                    sp.dma_start(dst, src).then_inc(s_w, 16)
                for c in range(4):
                    sp.dma_start(cx[:, c * QT4:(c + 1) * QT4, :], cx_rows[:, c * QT4:(c + 1) * QT4, :]).then_inc(s_cx, 16)
                for dst, src in [(wts[n][:], w[n]) for n in ("wq", "wo")] + [
                        (bq[:], w["bq"]), (bk[:], w["bk"]), (bv[:], w["bv"].partition_broadcast(128)), (bo[:], w["bo"].partition_broadcast(128)), (mask[:], w["mask"])]:
                    sp.dma_start(dst, src).then_inc(s_w, 16)
                for c in range(4):
                    sp.dma_start(x[:, c * QT4:(c + 1) * QT4, :], x_rows[:, c * QT4:(c + 1) * QT4, :]).then_inc(s_x, 16)
                for c in range(4):
                    sp.wait_ge(s_norm, (c + 1) * QT4)
                    sp.dma_start(out_rows[:, c * QT4:(c + 1) * QT4, :], x[:, c * QT4:(c + 1) * QT4, :]).then_inc(s_out, 16)
                sp.wait_ge(s_out, 64)

            @block.gpsimd
            def _(pool):
                nc.gpsimd.memset(ident[:], 0.0).then_inc(s_gc, 1)
                pool.wait_ge(s_gc, 1)
                nc.gpsimd.affine_select(out=ident[:], in_=ident[:], compare_op=ALU.not_equal, fill=1.0, base=0,
                                        pattern=[[-1, 128]], channel_multiplier=1).then_inc(s_gc, 1)
                pool.wait_ge(s_w, 144)
                for b in range(B):
                    pool.wait_ge(raw, NUMBER[f"xT{b}"] + 1)
                    nc.gpsimd.tensor_tensor(x[:, b * ND:(b + 1) * ND, :], x[:, b * ND:(b + 1) * ND, :],
                                            bo[:].unsqueeze(1).to_broadcast([128, ND, D]), ALU.add).then_inc(s_xb, 1)

            def taken(eng, me, name):
                eng.wait_ge(raw, NUMBER[name] + 1)
                return bank[NUMBER[name] % 8]

            halves = lambda a: a.rearrange("p (k s) -> p k s", k=2)

            @block.scalar
            def _(act):
                nc.scalar.preload_act_table_set("exp_and_others")
                act.wait_ge(s_w, 144)
                for b in range(B):
                    if ENGINE[f"cT{b}"] == "act":
                        p = taken(act, "act", f"cT{b}")
                        nc.scalar.copy(cT[:, :, b * S:(b + 1) * S], halves(p[:])).then_inc(out_of["act"], 1)
                for c in range(T // 512):
                    for m in range(KD):
                        p = taken(act, "act", f"k{m}{c}")
                        nc.scalar.activation(kT[:, m, c * 512:c * 512 + 512], p[:], ACT.Identity, bias=bk[:, m:m + 1]).then_inc(out_of["act"], 1)
                for b in range(B):
                    p = taken(act, "act", f"xT{b}")
                    nc.scalar.copy(xT[:, :, b * S:(b + 1) * S], halves(p[:])).then_inc(out_of["act"], 1)
                act.wait_ge(kmaxed, 1)
                for m in range(KD):
                    for b in range(B):
                        nc.scalar.activation(kT[:, m, b * S:(b + 1) * S], kT[:, m, b * S:(b + 1) * S], ACT.Exp, bias=nmax[:, m, b:b + 1],
                                             accum_out=sums[:, m, b:b + 1]).then_inc(kexped, 1)
                for c in range(T // 512):
                    for m in range(KD):
                        p = taken(act, "act", f"q{m}{c}")
                        nc.scalar.activation(qT[:, m, c * 512:c * 512 + 512], p[:], ACT.Identity, bias=bq[:, m:m + 1]).then_inc(out_of["act"], 1)
                for b in range(B):
                    p = taken(act, "act", f"kR{b}")
                    nc.scalar.copy(kR[:, b * ND:(b + 1) * ND, :], p[:].rearrange("p (t d) -> p t d", t=ND)).then_inc(out_of["act"], 1)
                for b in range(B):
                    p = taken(act, "act", f"a{b}")
                    nc.scalar.copy(att[:, :, b * S:(b + 1) * S], halves(p[:])).then_inc(out_of["act"], 1)
                act.wait_ge(s_var, 1)
                nc.scalar.activation(rstd[:], rstd[:], ACT.Sqrt).then_inc(s_rstd, 1)

            @block.vector
            def _(dve):
                chain = [0]

                def link(ins):
                    chain[0] += 1
                    ins.then_inc(s_dve, 1)
                    dve.wait_ge(s_dve, chain[0])

                for b in range(B):
                    if ENGINE[f"cT{b}"] == "dve":
                        p = taken(dve, "dve", f"cT{b}")
                        nc.vector.tensor_copy(cT[:, :, b * S:(b + 1) * S], halves(p[:])).then_inc(out_of["dve"], 1)
                dve.wait_ge(s_w, 144)
                for b in range(B):
                    p = taken(dve, "dve", f"v{b}")
                    nc.vector.tensor_tensor(v[:, b * ND:(b + 1) * ND, :], p[:].rearrange("p (t d) -> p t d", t=ND),
                                            bv[:].unsqueeze(1).to_broadcast([128, ND, D]), ALU.add).then_inc(out_of["dve"], 1)
                dve.wait_ge(out_of["act"], COUNT[f"k{KD - 1}{T // 512 - 1}"])
                nc.vector.tensor_reduce(nmax[:], kT[:].rearrange("p m (b s) -> p m b s", b=B), AX.X, ALU.max, negate=True).then_inc(kmaxed, 1)
                dve.wait_ge(kexped, KD * B)
                link(nc.vector.reciprocal(sums[:], sums[:]))
                for b in range(B):
                    p = taken(dve, "dve", f"c{b}")
                    for m in range(KD):
                        last = nc.vector.scalar_tensor_tensor(cm[:, b, m, :], p[:, m * 128:m * 128 + 128], sums[:, m, b:b + 1], mask[:, m, :], ALU.mult, ALU.mult)
                    last.then_inc(out_of["dve"], 1)
                for b in range(B):
                    p = taken(dve, "dve", f"o{b}")
                    dve.wait_ge(s_xb, b + 1)
                    nc.vector.tensor_tensor(x[:, b * ND:(b + 1) * ND, :], p[:].rearrange("p (t d) -> p t d", t=ND),
                                            x[:, b * ND:(b + 1) * ND, :], ALU.add).then_inc(out_of["dve"], 1)
                    dve.wait_ge(out_of["dve"], COUNT[f"o{b}"])
                    for t in range(b * ND, (b + 1) * ND):
                        last = nc.vector.bn_stats(stats[:, t, :], x[:, t, :])
                link(last)
                for t in range(TT):
                    last = nc.vector.bn_aggr(mv[:, t, :], stats[:, t, :])
                link(last)
                nc.vector.tensor_scalar(rstd[:], mv[:, :, 1], LN_EPS, None, ALU.add).then_inc(s_var, 1)
                dve.wait_ge(s_rstd, 1)
                link(nc.vector.reciprocal(rstd[:], rstd[:]))
                for t in range(TT):
                    nc.vector.tensor_scalar(x[:, t, :], x[:, t, :], mv[:, t, 0:1], rstd[:, t:t + 1], ALU.subtract, ALU.mult).then_inc(s_norm, 1)

            @block.tensor
            def _(pe):
                def done(name):
                    pe.wait_ge(out_of[ENGINE[name]], COUNT[name])

                def start(name):
                    j = NUMBER[name]
                    if j >= 8:
                        done(JOBS[j - 8][0])
                    return bank[j % 8]

                def transposed(name, src, b):
                    p = start(name)
                    for k in range(KD):
                        for s in range(ND):
                            last = nc.tensor.transpose(p[:, k * S + s * 128:k * S + s * 128 + 128], src[:, b * ND + s, k * 128:k * 128 + 128], ident[:])
                    last.then_inc(raw, 1)

                def project(name, wt, m, c, src):
                    p = start(name)
                    for k in range(KD):
                        last = nc.tensor.matmul(p[:], wt[:, k, m * 128:m * 128 + 128], src[:, k, c * 512:c * 512 + 512], start=(k == 0), stop=(k == KD - 1))
                    last.then_inc(raw, 1)

                def rows_product(name, b, src, wt):
                    p = start(name)
                    for s in range(ND):
                        for k in range(KD):
                            last = nc.tensor.matmul(p[:, s * D:s * D + D], src[:, k, b * S + s * 128:b * S + s * 128 + 128], wt[:, k, :],
                                                    start=(k == 0), stop=(k == KD - 1))
                    last.then_inc(raw, 1)

                pe.wait_ge(s_gc, 2)
                pe.wait_ge(s_cx, 64)
                for b in range(B):
                    transposed(f"cT{b}", cx, b)
                pe.wait_ge(s_w, 144)
                for c in range(T // 512):
                    done(f"cT{2 * c}")
                    done(f"cT{2 * c + 1}")
                    for m in range(KD):
                        project(f"k{m}{c}", wts["wk"], m, c, cT)
                for b in range(B):
                    rows_product(f"v{b}", b, cT, wts["wv"])
                pe.wait_ge(s_x, 64)
                for b in range(B):
                    transposed(f"xT{b}", x, b)
                for c in range(T // 512):
                    done(f"xT{2 * c + 1}")
                    for m in range(KD):
                        project(f"q{m}{c}", wts["wq"], m, c, xT)
                for b in range(B):
                    pe.wait_ge(kexped, B + b + 1)
                    p = start(f"kR{b}")
                    for s in range(ND):
                        for m in range(KD):
                            last = nc.tensor.transpose(p[:, s * D + m * 128:s * D + m * 128 + 128], kT[:, m, b * S + s * 128:b * S + s * 128 + 128], ident[:])
                    last.then_inc(raw, 1)
                for b in range(B):
                    done(f"kR{b}")
                    p = start(f"c{b}")
                    for m in range(KD):
                        for s in range(ND):
                            t = b * ND + s
                            last = nc.tensor.matmul(p[:, m * 128:m * 128 + 128], kR[:, t, m * 128:m * 128 + 128], v[:, t, m * 128:m * 128 + 128],
                                                    start=(s == 0), stop=(s == ND - 1))
                    last.then_inc(raw, 1)
                for b in range(B):
                    done(f"c{b}")
                    p = start(f"a{b}")
                    for m in range(KD):
                        last = nc.tensor.matmul(p[:, m * S:m * S + S], cm[:, b, m, :], qT[:, m, b * S:(b + 1) * S], start=True, stop=True)
                    last.then_inc(raw, 1)
                for b in range(B):
                    done(f"a{b}")
                    rows_product(f"o{b}", b, att, wts["wo"])


def decoder(nc, a, out):
    fp32 = mybir.dt.float32
    B, S, D = a["x"].shape
    T = B * S
    E = a["wr0"].shape[1]
    rows = T + (TOP_K * T + E * (SLOTS - 1)) // SLOTS * SLOTS
    slots = nc.dram_tensor("slots", (rows, D), fp32).ap()
    results = nc.dram_tensor("results", (rows, D), fp32).ap()
    mid = [nc.dram_tensor(f"mid{n}", (B, S, D), fp32).ap() for n in range(4)]
    flat = lambda t: t.rearrange("a s d -> (a s) d")
    sems = []

    def layer_ends():
        with nc.Block() as block:
            @block.gpsimd
            def _(pool):
                nc.clear_and_free_semaphores(sems)
        sems.clear()

    attention_layers(nc, sems, a["x"], a["ctx"], mid[0], slots, a)
    layer_ends()
    moe_layer(nc, sems, "m0", flat(mid[0]), flat(mid[1]), a["wr0"], a["br0"], (a["g0"], a["b0"]), a["up0"], a["bup0"],
              a["down0"], a["bdown0"], slots, results, ACT.Relu, False, False)
    layer_ends()
    state_space_layer(nc, sems, mid[1], mid[2], a)
    layer_ends()
    linear_attention_layer(nc, sems, mid[2], a["ctx"], mid[3], {n[2:]: t for n, t in a.items() if n.startswith("l_")})
    layer_ends()
    moe_layer(nc, sems, "m1", flat(mid[3]), flat(out), a["wr1"], None, None, a["up1"], None, a["down1"], None,
              slots, results, ACT.Gelu, True, True)


def kernel(**inputs):
    import numpy as np
    import concourse.bacc as bacc
    from concourse.bass_utils import run_bass_kernel_spmd

    g = {k: np.asarray(v) for k, v in inputs.items()}

    def tiles(a):
        *e, k, n = a.shape
        return np.moveaxis(a.reshape(*e, k // 128, 128, n), -3, -2)

    def column(a):
        return a.reshape(-1, 128).T

    A, X, F0, F1, M, L = "L0_attn_", "L0_xattn_", "L0_ffn_", "L1_ffn_", "L1_attn_", "L1_xattn_"
    heads = 128 // g[A + "q_gamma"].shape[0]
    blocks = np.kron(np.eye(8, dtype=np.float32), np.ones((16, 16), np.float32))
    arrays = {
        "x": g["x"], "ctx": g["ctx_1024"],
        "wqkv": tiles(np.concatenate([g[A + "Wq"].T, g[A + "Wk"].T, g[A + "Wv"].T], 1)), "wo0": tiles(g[A + "Wo"].T), "bo0": g[A + "bo"],
        "ln_g": column(g[A + "ln_g"]), "ln_b": column(g[A + "ln_b"]),
        "qg": np.concatenate([g[A + "q_gamma"]] * heads)[:, None], "kg": np.concatenate([g[A + "k_gamma"]] * heads)[:, None],
        "wq": tiles(g[X + "wq_w"]), "wk": tiles(g[X + "wk_w"]), "wv": tiles(g[X + "wv_w"]), "wox": tiles(g[X + "wo_w"]),
        "bqx": column(g[X + "wq_b"]), "bkx": column(g[X + "wk_b"]), "bvx": g[X + "wv_b"], "box": g[X + "wo_b"],
        "mk": tiles(g[X + "mk"][0].T), "mvx": g[X + "mv"][0],
        "wr0": g[F0 + "Wr"], "br0": g[F0 + "br"], "g0": g[F0 + "gamma"], "b0": g[F0 + "beta"],
        "up0": tiles(g[F0 + "W1"]), "bup0": np.moveaxis(g[F0 + "b1"].reshape(8, -1, 128), 1, 2), "down0": tiles(g[F0 + "W2"]), "bdown0": g[F0 + "b2"],
        "proj": tiles(np.concatenate([g[M + "x_proj_w"], g[M + "B_proj_w"], g[M + "C_proj_w"]]).T), "dt_w": g[M + "dt_proj_w"].T,
        "dt_b": column(g[M + "dt_proj_b"]), "d": column(g[M + "D"]), "a_log": tiles(g[M + "A_log"]),
        "l_wq": tiles(g[L + "Wq"].T), "l_wk": tiles(g[L + "Wk"].T), "l_wv": tiles(g[L + "Wv"].T), "l_wo": tiles(g[L + "Wo"].T),
        "l_bq": column(g[L + "bq"]), "l_bk": column(g[L + "bk"]), "l_bv": g[L + "bv"], "l_bo": g[L + "bo"],
        "l_mask": np.stack([blocks, blocks], 1),
        "wr1": g[F1 + "Wg"], "up1": tiles(np.concatenate([g[F1 + "Wu"], g[F1 + "W1"][None]])),
        "down1": tiles(np.concatenate([g[F1 + "Wd"], g[F1 + "W2"][None]])),
    }
    nc = bacc.Bacc("TRN2", target_bir_lowering=False, num_devices=1)
    arrays = {f"in_{n}": np.ascontiguousarray(v) for n, v in arrays.items()}
    a = {n[3:]: nc.dram_tensor(n, v.shape, mybir.dt.from_np(v.dtype), kind="ExternalInput").ap() for n, v in arrays.items()}
    out = nc.dram_tensor("out", g["x"].shape, mybir.dt.float32, kind="ExternalOutput").ap()
    decoder(nc, a, out)
    r = run_bass_kernel_spmd(nc, [arrays], core_ids=[0])
    return r.results[0]["out"]
```

```python
import concourse.bass as bass
from concourse import mybir
from contextlib import ExitStack

ALU = mybir.AluOpType
ACT = mybir.ActivationFunctionType
AX = mybir.AxisListType
TOP_K = 2
SLOTS = 256
SLOT_BITS = 8
LN_EPS = 1e-5
RMS_EPS = 1e-8
SCALE = 64 ** -0.5
DT_MIN, DT_MAX = 0.001, 0.1


def attention_layers(nc, sems, x_in, ctx_in, x_out, slots, w):
    fp32, fp32r = mybir.dt.float32, mybir.dt.float32r
    B, S, D = x_in.shape
    HX, MEM = 16, w["mvx"].shape[0]
    PX = HX // 2
    P0 = 2
    ND = S // 128
    KD = D // 128
    KEYS = S + MEM
    KX = KEYS // 128
    U0, UX = 4 * P0, 4 * PX
    U = U0 + UX
    PAIRS = P0 + PX
    assert ND == 2 and KD == 2 and U % 4 == 0 and PAIRS % 2 == 0
    R_LAG, T_LAG, C_LAG, V_LAG, O_LAG, L_LAG = 2, 5, 5, 11, 12, 13
    SIDE, Q_SIDE = 2, 2
    RING = 8
    BANKS = 3
    TAIL = L_LAG - 4

    JOB = {n: j for j, n in enumerate(
        ["first ctxT", "first xnT", "first vself", "k0", "k1", "qkT0", "qkT1", "v0", "v1", "v2", "v3", "k2", "k3", "oself"]
        + [f"k{p}" for p in range(4, PX)] + ["x1T"] + [f"q{p}" for p in range(PX)] + ["ctxT", "xnT", "vself", "ox"])}
    JOBS = len(JOB) - 3
    assert JOBS % 2 == 0

    ctx = ExitStack()
    with ctx:
        def sb(n, shape, dt=fp32):
            return ctx.enter_context(nc.sbuf_tensor(f"a_{n}", shape, dt))

        def sem(n):
            sems.append(nc.alloc_semaphore(f"a_{n}"))
            return sems[-1]

        def pair_of(n, shape):
            return [sb(n + part, shape, fp32r) for part in ("_high", "_low")]

        x = sb("x", [128, ND, D])
        cx = sb("cx", [128, ND, D])
        xn = sb("xn", [128, ND, D])
        x1 = sb("x1", [128, ND, D])
        x1b = sb("x1b", [128, ND, D])
        xo = sb("xo", [128, ND, D])
        xT = pair_of("xT", [128, KD, S])
        cT = pair_of("cT", [128, KD, S])
        wqkv = pair_of("wqkv", [128, KD, 3 * D])
        wo0 = pair_of("wo0", [128, KD, D])
        wq = pair_of("wq", [128, KD, HX * 64])
        wk = pair_of("wk", [128, KD, HX * 64])
        wv = pair_of("wv", [128, KD, HX * 64])
        wox = pair_of("wox", [128, PX, D])
        bqx = sb("bqx", [128, PX])
        bkx = sb("bkx", [128, PX])
        bvx = sb("bvx", [128, HX * 64])
        bo0 = sb("bo0", [128, D])
        box = sb("box", [128, D])
        gb = sb("gb", [128, 2, KD])
        qkg = sb("qkg", [128, 2])
        ident = sb("ident", [128, 128])
        work = sb("work", [128, 3, 4, S])
        sq = work[:, 0:2].rearrange("p a b s -> p (a b s)")[:, 0:ND * 2 * D].rearrange("p (t n) -> p t n", t=ND)
        qkf = work[:, 2]
        kself = pair_of("kself", [128, P0, S])
        vself = sb("vself", [128, ND, D])
        qs = pair_of("qs", [128, 2, 2, S])
        ks = pair_of("ks", [128, PX, KEYS])
        vx = sb("vx", [128, KX, HX * 64])
        pexp_own = sb("pexp", [128, RING // 2, KEYS])
        pexp_work = work[:, 0:2].rearrange("p a b s -> p (a b s)")[:, 0:RING // 2 * KEYS].rearrange("p (r n) -> p r n", r=RING // 2)
        pexp = [(pexp_own, pexp_work)[r % 2][:, r // 2, :] for r in range(RING)]
        pT = sb("pT", [128, 2, 2, KX, S])
        oT = pair_of("oT", [128, PX, S])
        zero = sb("zero", [128, D])
        st = sb("st", [128, ND, 6])
        mv = sb("mv", [128, ND, 2])
        var = sb("var", [128, ND * 8])
        root = sb("root", [128, ND * 8])
        tmp = sb("tmp", [128, ND * 8])
        nmax = sb("nmax", [128, RING])
        sums = sb("sums", [128, RING])
        rsum = sb("rsum", [128, RING])

        ps = [ctx.enter_context(nc.psum_tensor(f"a_ps{n}", [128, 512], fp32)) for n in range(8)]
        ps_s, ps_t, ps_o, ps_j = ps[0:3], ps[3:5], ps[5], ps[6:8]

        s_ln = sem("s_ln")
        s_zero = sem("s_zero"); s_filled = sem("s_filled")
        s_w = [sem(f"s_w{n}") for n in range(3)]; w_high = sem("w_high"); w_low = sem("w_low"); s_small = sem("s_small")
        s_gc = sem("s_gc"); s_scaled = sem("s_scaled")
        x_loaded = sem("x_loaded"); ctx_loaded = sem("ctx_loaded")
        s_dve = sem("s_dve"); var_ready = sem("var_ready"); ln_done = sem("ln_done"); root_ready = sem("root_ready")
        rows_ready = sem("rows_ready"); xb_ready = sem("xb_ready")
        job_raw = sem("job_raw"); qk_raw = sem("qk_raw"); qk_normed = sem("qk_normed"); job_free = [sem("job_free0"), sem("job_free1")]
        act_part = sem("act_part"); dve_part = sem("dve_part"); k_low = sem("k_low"); q_low = sem("q_low"); q_high = sem("q_high")
        scores_raw = sem("scores_raw"); maxed = sem("maxed"); exped = sem("exped"); recip = sem("recip")
        normed = sem("normed"); pt_raw = sem("pt_raw"); pt_copied = [sem("pt_copied0"), sem("pt_copied1")]
        o_raw = sem("o_raw"); o_high = sem("o_high"); o_split = sem("o_split"); s_out = sem("s_out")

        rows = lambda a: a.rearrange("a (t p) d -> p (a t) d", p=128)
        stage = [pT[:].rearrange("p a b c s -> p (a b c s)"), vx[:, 0:ND, :].rearrange("p t n -> p (t n)"), work[:].rearrange("p a b s -> p (a b s)")]
        SPLIT = [(w["wqkv"], [t[:] for t in wqkv]), (w["wk"], [t[:] for t in wk]), (w["wv"], [t[:] for t in wv]),
                 (w["wq"], [t[:] for t in wq]), (w["wo0"], [t[:] for t in wo0]), (w["wox"], [t[:] for t in wox]),
                 (w["mk"], [t[:, :, S:KEYS] for t in ks])]
        STAGE = [0, 1, 2, 0, 1, 0, 1]
        USE = [STAGE[:n + 1].count(STAGE[n]) for n in range(len(SPLIT))]
        EARLY = 3

        def staged(n):
            a = SPLIT[n][0]
            return stage[STAGE[n]][:, 0:a.shape[1] * a.shape[2]].rearrange("p (k n) -> p k n", k=a.shape[1])

        def schedule(units, first_pair):
            at = lambda v, lag: (v - lag) // 4 if v >= lag and (v - lag) % 4 == 0 and (v - lag) // 4 < units // 4 else None
            for v in range(units + TAIL + 2):
                inside = lambda u: u if 0 <= u < units else None
                yield v, inside(v), inside(v - T_LAG), inside(v - C_LAG), at(v, V_LAG), at(v, O_LAG), at(v, L_LAG)

        acts = ["first ctxT", "first qk0", "first qk1"] + [f"k{p}" for p in range(PX)] + ["x1T", "ctxT", "qk0", "qk1"]
        ACT_PART = {n: k + 1 for k, n in enumerate(acts)}
        ACT_PARTS = len(acts) - 3
        ROOTS = {"first": 1, "first qk": 2, "x1": 3, "xn": 4, "qk": 5, "xo": 6}
        CTX_SLOT, XN_SLOT = 4 * (PX - 2) + Q_SIDE - 1, 4 * (PX - 2) + Q_SIDE + 2
        QK_SLOT = UX + T_LAG
        FILL = {2: 0, 4: 1, 6: 2, 8: 3}

        def FREED(i, name):
            return i * (JOBS // 2) + JOB[name] // 2 + 2

        def copy_pt(eng, copy, i, base, first_pair, u):
            m = first_pair + u // 4
            kx = KX if base else ND
            eng.wait_ge(pt_raw, i * U + base + u + 1 + RING)
            eng.wait_ge(o_raw, i * PAIRS + m - 1 + 2)
            copy(pT[:, m % 2, u // 2 % 2, 0:kx, u % 2 * 128:u % 2 * 128 + 128],
                 ps_t[u % 2][:, 0:kx * 128].rearrange("p (k s) -> p k s", k=kx)).then_inc(pt_copied[u % 2], 1)

        with nc.Block() as block:
            @block.sync
            def _(sp):
                def load(i):
                    sp.dma_start(x[:], rows(x_in[bass.ds(i, 1)])).then_inc(x_loaded, 16)
                    sp.dma_start(cx[:], rows(ctx_in[bass.ds(i, 1)])).then_inc(ctx_loaded, 16)

                def store(i):
                    sp.wait_ge(ln_done, i + 1)
                    sp.dma_start(rows(x_out[bass.ds(i, 1)]), xo[:]).then_inc(s_out, 16)

                for dst, src in ((bqx[:], w["bqx"]), (bkx[:], w["bkx"]), (bvx[:], w["bvx"].partition_broadcast(128)),
                                 (bo0[:], w["bo0"].partition_broadcast(128)), (box[:], w["box"].partition_broadcast(128)),
                                 (gb[:, 0, :], w["ln_g"]), (gb[:, 1, :], w["ln_b"]), (qkg[:, 0:1], w["qg"]), (qkg[:, 1:2], w["kg"]),
                                 (vx[:, ND, :], w["mvx"])):
                    sp.dma_start(dst, src).then_inc(s_small, 16)
                sp.sem_inc(s_out, 16)
                load(0)
                for n, (src, _) in enumerate(SPLIT):
                    before = [m for m in range(n) if STAGE[m] == STAGE[n]]
                    if before:
                        sp.wait_ge(w_low, before[-1] + 1)
                    sp.dma_start(staged(n), src).then_inc(s_w[STAGE[n]], 16)
                sp.wait_ge(s_zero, 1)
                sp.dma_start(slots.rearrange("(p r) d -> p r d", p=128), zero[:].unsqueeze(1).to_broadcast([128, slots.shape[0] // 128, D])).then_inc(s_filled, 16)
                with sp.Fori(0, B - 1) as i:
                    sp.wait_ge(rows_ready, 2 * i + 2)
                    load(i + 1)
                    store(i)
                sp.wait_ge(rows_ready, 2 * B)
                load(0)
                store(B - 1)
                sp.wait_ge(s_out, 16 * B + 16)
                sp.wait_ge(s_filled, 16)

            @block.gpsimd
            def _(pool):
                nc.gpsimd.memset(zero[:], 0.0).then_inc(s_zero, 1)
                nc.gpsimd.memset(ident[:], 0.0).then_inc(s_gc, 1)
                pool.wait_ge(s_gc, 1)
                nc.gpsimd.affine_select(out=ident[:], in_=ident[:], compare_op=ALU.not_equal, fill=1.0, base=0,
                                        pattern=[[-1, 128]], channel_multiplier=1).then_inc(s_gc, 1)
                for part in range(2):
                    pool.wait_ge(s_gc, 2 + 2 * part)
                    nc.gpsimd.memset(qs[part][64:128, :, 0, :].bitcast(fp32), 0.0).then_inc(s_gc, 1)
                    pool.wait_ge(s_gc, 3 + 2 * part)
                    nc.gpsimd.memset(qs[part][0:64, :, 1, :].bitcast(fp32), 0.0).then_inc(s_gc, 1)

                pool.wait_ge(s_gc, 6)

                def low_k(i, p):
                    pool.wait_ge(act_part, i * ACT_PARTS + ACT_PART[f"k{p}"])
                    nc.gpsimd.tensor_tensor(ks[1][:, p, 0:S], qkf[:, p % 2, :], ks[0][:, p, 0:S], ALU.subtract).then_inc(k_low, 1)

                def norm(i, base, u):
                    pool.wait_ge(recip, i * U + base + u + 1)
                    n = KEYS if base else S
                    nc.gpsimd.tensor_tensor(pexp[u % RING][:, 0:n], pexp[u % RING][:, 0:n], rsum[:, u % RING:u % RING + 1].to_broadcast([128, n]), ALU.mult)\
                        .then_inc(normed, 1)

                with pool.Fori(0, B) as i:
                    pool.wait_ge(rows_ready, 2 * i + 1)
                    nc.gpsimd.tensor_tensor(x[:], x[:], bo0[:].unsqueeze(1).to_broadcast([128, ND, D]), ALU.add).then_inc(xb_ready, 1)
                    low_k(i, 0)
                    low_k(i, 1)
                    for u in range(U0):
                        norm(i, 0, u)
                    low_k(i, 2)
                    low_k(i, 3)
                    for p in range(4, PX):
                        low_k(i, p)
                    pool.wait_ge(rows_ready, 2 * i + 2)
                    nc.gpsimd.tensor_tensor(x1b[:], x1[:], box[:].unsqueeze(1).to_broadcast([128, ND, D]), ALU.add).then_inc(xb_ready, 1)
                    for u in range(UX):
                        norm(i, U0, u)

            @block.scalar
            def _(act):
                nc.scalar.preload_act_table_set("natural_log_exp_and_others")

                def high_parts(numbers):
                    for n in numbers:
                        act.wait_ge(s_w[STAGE[n]], 16 * USE[n])
                        nc.scalar.copy(SPLIT[n][1][0], staged(n)).then_inc(w_high, 1)

                act.wait_ge(s_small, 160)
                act.wait_ge(s_scaled, 2)

                def take_root(i, name, n):
                    act.wait_ge(var_ready, 4 * i + ROOTS[name])
                    nc.scalar.activation(root[:, 0:n], var[:, 0:n], ACT.Ln).then_inc(s_ln, 1)
                    act.wait_ge(s_ln, 4 * i + ROOTS[name])
                    nc.scalar.activation(root[:, 0:n], root[:, 0:n], ACT.Exp, scale=-0.5).then_inc(root_ready, 1)

                def job(i, name):
                    act.wait_ge(job_raw, i * JOBS + JOB[name] + 1)
                    return ps_j[JOB[name] % 2]

                def free(name, ins):
                    ins.then_inc(job_free[JOB[name] % 2], 1)

                def keys(i, p):
                    b = job(i, f"k{p}")
                    if p >= 2:
                        act.wait_ge(k_low, i * PX + p - 1)
                    nc.scalar.activation(qkf[:, p % 2, :], b[:, 0:S], ACT.Identity, bias=bkx[:, p:p + 1]).then_inc(job_free[JOB[f"k{p}"] % 2], 1)
                    act.wait_ge(job_free[JOB[f"k{p}"] % 2], FREED(i, f"k{p}"))
                    nc.scalar.copy(ks[0][:, p, 0:S], qkf[:, p % 2, :]).then_inc(act_part, 1)

                def queries(i, p):
                    b = job(i, f"q{p}")
                    if p >= 2:
                        act.wait_ge(q_low, i * PX + p - 1)
                    nc.scalar.activation(qkf[:, 2 + p % 2, :], b[:, 0:S], ACT.Identity, bias=bqx[:, p:p + 1], scale=SCALE)\
                        .then_inc(job_free[JOB[f"q{p}"] % 2], 1)

                def attend(i, base, first_pair, units, side):
                    n = KEYS if base else S
                    for v, us, ut, uc, pv, po, pl in schedule(units, first_pair):
                        if us is not None:
                            act.wait_ge(maxed, i * U + base + us + 1)
                            act.wait_ge(pt_raw, i * U + base + (us + 1 if us >= RING else RING))
                            nc.scalar.activation(pexp[us % RING][:, 0:n], ps_s[us % BANKS][:, 0:n], ACT.Exp, bias=nmax[:, us % RING:us % RING + 1],
                                                 accum_out=sums[:, us % RING:us % RING + 1]).then_inc(exped, 1)
                        side(v)
                        if uc is not None and uc % 2 == 1:
                            copy_pt(act, nc.scalar.copy, i, base, first_pair, uc)
                        if po is not None:
                            m = first_pair + po
                            act.wait_ge(o_raw, i * PAIRS + m + 1 + 2)
                            nc.scalar.copy(oT[0][:, po, :], ps_o[:, 0:S]).then_inc(o_high, 1)

                def context(i, name):
                    b = job(i, name)
                    nc.scalar.copy(cT[0][:], b[:].rearrange("p (k s) -> p k s", k=KD)).then_inc(act_part, 1)

                def scaled_rows(i, name):
                    b = job(i, name)
                    for k in range(KD):
                        last = nc.scalar.activation(xn[:, k, :], b[:, k * S:(k + 1) * S], ACT.Identity, bias=gb[:, 1, k:k + 1], scale=gb[:, 0, k:k + 1])
                    free(name, last)

                def self_values(i, name):
                    b = job(i, name)
                    free(name, nc.scalar.copy(vself[:], b[:].rearrange("p (t d) -> p t d", t=ND)))

                def squares(entry, s):
                    act.wait_ge(qk_raw, ND * entry + s + 1)
                    nc.scalar.activation(sq[:, s, :], ps_s[s][:], ACT.Square).then_inc(act_part, 1)

                act.sem_inc(exped, BANKS)
                take_root(0, "first", ND)
                high_parts(range(0, EARLY))
                context(0, "first ctxT")
                scaled_rows(0, "first xnT")
                self_values(0, "first vself")
                squares(0, 0)
                squares(0, 1)
                take_root(0, "first qk", ND * 8)
                high_parts(range(EARLY, len(SPLIT)))
                with act.Fori(0, B) as i:
                    keys(i, 0)
                    keys(i, 1)
                    act.wait_ge(k_low, i * PX + 2)
                    for s in range(ND):
                        b = job(i, f"qkT{s}")
                        for qk in range(2):
                            last = nc.scalar.activation(qkf[:, 2 * qk:2 * qk + 2, s * 128:(s + 1) * 128],
                                                        b[:, 256 * qk:256 * qk + 256].rearrange("p (m s) -> p m s", m=2), ACT.Copy,
                                                        scale=qkg[:, qk:qk + 1])
                        free(f"qkT{s}", last)
                    attend(i, 0, 0, U0, lambda v: keys(i, FILL[v]) if FILL.get(v, 0) >= 2 else None)
                    for p in range(4, PX):
                        keys(i, p)
                    take_root(i, "x1", ND)
                    b = job(i, "x1T")
                    nc.scalar.copy(xT[0][:], b[:].rearrange("p (k s) -> p k s", k=KD)).then_inc(act_part, 1)
                    queries(i, 0)
                    queries(i, 1)

                    def side(v):
                        if v % 4 == Q_SIDE and v // 4 + 2 < PX:
                            queries(i, v // 4 + 2)
                        if v == 6:
                            take_root(i, "xn", ND)
                        if v == CTX_SLOT + 1:
                            context(i, "ctxT")
                        if v == XN_SLOT + 1:
                            scaled_rows(i, "xnT")
                        if v == QK_SLOT + 2:
                            self_values(i, "vself")
                            squares(i + 1, 0)
                            squares(i + 1, 1)

                    attend(i, U0, P0, UX, side)
                    take_root(i, "qk", ND * 8)
                    take_root(i, "xo", ND)


            LINKS = 25

            @block.vector
            def _(dve):
                chain = [0]

                def link(i, ins):
                    chain[0] += 1
                    ins.then_inc(s_dve, 1)
                    dve.wait_ge(s_dve, i * LINKS + chain[0])


                def low_parts(numbers):
                    for n in numbers:
                        dve.wait_ge(w_high, n + 1)
                        nc.vector.tensor_tensor(SPLIT[n][1][1], staged(n), SPLIT[n][1][0], ALU.subtract).then_inc(w_low, 1)

                dve.wait_ge(s_small, 160)
                nc.vector.tensor_scalar(bqx[:], bqx[:], SCALE, None, ALU.mult).then_inc(s_scaled, 1)
                nc.vector.tensor_scalar(qkg[:, 0:1], qkg[:, 0:1], SCALE, None, ALU.mult).then_inc(s_scaled, 1)

                def refine_root(i, name, n):
                    dve.wait_ge(root_ready, 4 * i + ROOTS[name])
                    link(i, nc.vector.tensor_tensor(tmp[:, 0:n], root[:, 0:n], root[:, 0:n], ALU.mult))
                    link(i, nc.vector.tensor_tensor(tmp[:, 0:n], tmp[:, 0:n], var[:, 0:n], ALU.mult))
                    link(i, nc.vector.tensor_scalar(tmp[:, 0:n], tmp[:, 0:n], -0.5, 1.5, ALU.mult, ALU.add))
                    link(i, nc.vector.tensor_tensor(root[:, 0:n], root[:, 0:n], tmp[:, 0:n], ALU.mult))

                def norm_stats(i, src):
                    for s in range(ND):
                        last = nc.vector.bn_stats(st[:, s, :], src[:, s, :])
                    link(i, last)
                    nc.vector.memset(tmp[:, 0:1], 0.0)
                    for s in range(ND):
                        last = nc.vector.bn_aggr(mv[:, s, :], st[:, s, :])
                    link(i, last)
                    nc.vector.tensor_scalar(var[:, 0:ND], mv[:, :, 1], LN_EPS, None, ALU.add).then_inc(var_ready, 1)

                def norm_apply(i, name, src, dst, done):
                    refine_root(i, name, ND)
                    for s in range(ND):
                        last = nc.vector.tensor_scalar(dst[:, s, :], src[:, s, :], mv[:, s, 0:1], root[:, s:s + 1], ALU.subtract, ALU.mult)
                    last.then_inc(done, 1)

                def job(i, name):
                    dve.wait_ge(job_raw, i * JOBS + JOB[name] + 1)
                    return ps_j[JOB[name] % 2]

                def after_act(i, name):
                    dve.wait_ge(act_part, i * ACT_PARTS + ACT_PART[name])
                    return ps_j[JOB[name] % 2]

                def after_free(i, name):
                    dve.wait_ge(job_free[JOB[name] % 2], FREED(i, name))

                def free(name, ins):
                    ins.then_inc(job_free[JOB[name] % 2], 1)

                def values(i, n):
                    b = job(i, f"v{n}")
                    s, half = n // 2, n % 2
                    free(f"v{n}", nc.vector.tensor_tensor(vx[:, s, half * 512:half * 512 + 512], b[:], bvx[:, half * 512:half * 512 + 512], ALU.add))

                def split_q(i, p):
                    after_free(i, f"q{p}")
                    for h in range(2):
                        last = nc.vector.tensor_copy(qs[0][64 * h:64 * h + 64, p % 2, h, :], qkf[64 * h:64 * h + 64, 2 + p % 2, :])
                    last.then_inc(q_high, 1)
                    dve.wait_ge(q_high, i * PX + p + 1)
                    for h in range(2):
                        last = nc.vector.tensor_tensor(qs[1][64 * h:64 * h + 64, p % 2, h, :], qkf[64 * h:64 * h + 64, 2 + p % 2, :],
                                                       qs[0][64 * h:64 * h + 64, p % 2, h, :], ALU.subtract)
                    last.then_inc(q_low, 1)

                def attend(i, base, first_pair, units, side):
                    n = KEYS if base else S
                    for v, us, ut, uc, pv, po, pl in schedule(units, first_pair):
                        if us is not None:
                            dve.wait_ge(scores_raw, i * U + base + us + 1)
                            nc.vector.tensor_reduce(nmax[:, us % RING:us % RING + 1], ps_s[us % BANKS][:, 0:n], AX.X, ALU.max, negate=True).then_inc(maxed, 1)
                        if 0 <= v - R_LAG < units:
                            r = (v - R_LAG) % RING
                            dve.wait_ge(exped, i * U + base + v - R_LAG + 1 + BANKS)
                            nc.vector.reciprocal(rsum[:, r:r + 1], sums[:, r:r + 1]).then_inc(recip, 1)
                        if uc is not None and uc % 2 == 0:
                            copy_pt(dve, nc.vector.tensor_copy, i, base, first_pair, uc)
                        side(v)
                        if pl is not None:
                            m = first_pair + pl
                            dve.wait_ge(o_high, i * PAIRS + m + 1)
                            nc.vector.tensor_tensor(oT[1][:, pl, :], ps_o[:, 0:S], oT[0][:, pl, :], ALU.subtract).then_inc(o_split, 1)

                def context(i, name):
                    b = after_act(i, name)
                    free(name, nc.vector.tensor_tensor(cT[1][:], b[:].rearrange("p (k s) -> p k s", k=KD), cT[0][:], ALU.subtract))

                def split_rows(i, name):
                    after_free(i, name)
                    link(i, nc.vector.tensor_copy(xT[0][:], xn[:]))
                    nc.vector.tensor_tensor(xT[1][:], xn[:], xT[0][:], ALU.subtract).then_inc(dve_part, 1)

                def norm_qk(i, name, first):
                    for s in range(ND):
                        dve.wait_ge(act_part, i * ACT_PARTS + ACT_PART[f"{first}qk{s}"])
                        last = nc.vector.tensor_reduce(var[:, s * 8:s * 8 + 8], sq[:, s, :].rearrange("p (h d) -> p h d", d=64), AX.X, ALU.add)
                    link(i, last)
                    nc.vector.tensor_scalar(var[:], var[:], 1.0 / 64, RMS_EPS * RMS_EPS, ALU.mult, ALU.max).then_inc(var_ready, 1)
                    refine_root(i, name, ND * 8)
                    for s in range(ND):
                        nc.vector.tensor_tensor(sq[:, s, :].rearrange("p (h d) -> p h d", d=64), ps_s[s][:].rearrange("p (h d) -> p h d", d=64),
                                                root[:, s * 8:s * 8 + 8].unsqueeze(2).to_broadcast([128, 8, 64]), ALU.mult).then_inc(qk_normed, 1)

                dve.sem_inc(o_split, 2)
                dve.wait_ge(x_loaded, 16)
                norm_stats(0, x)
                norm_apply(0, "first", x, xn, rows_ready)
                low_parts(range(0, EARLY))
                context(0, "first ctxT")
                split_rows(0, "first xnT")
                norm_qk(0, "first qk", "first ")
                low_parts(range(EARLY, len(SPLIT)))
                before = chain[0]
                with dve.Fori(0, B) as i:
                    chain[0] = before
                    after_free(i, "qkT0")
                    after_free(i, "qkT1")
                    nc.vector.tensor_copy(kself[0][:], qkf[:, 2:4, :])
                    for h in range(2):
                        last = nc.vector.tensor_copy(qs[0][64 * h:64 * h + 64, :, h, :], qkf[64 * h:64 * h + 64, 0:2, :])
                    link(i, last)
                    nc.vector.tensor_tensor(kself[1][:], qkf[:, 2:4, :], kself[0][:], ALU.subtract)
                    for h in range(2):
                        last = nc.vector.tensor_tensor(qs[1][64 * h:64 * h + 64, :, h, :], qkf[64 * h:64 * h + 64, 0:2, :],
                                                       qs[0][64 * h:64 * h + 64, :, h, :], ALU.subtract)
                    last.then_inc(dve_part, 1)
                    values(i, 0)
                    values(i, 1)
                    attend(i, 0, 0, U0, lambda v: values(i, 2 + FILL[v]) if FILL.get(v, 2) < 2 else None)
                    b = job(i, "oself")
                    dve.wait_ge(xb_ready, 2 * i + 1)
                    free("oself", nc.vector.tensor_tensor(x1[:], b[:].rearrange("p (t d) -> p t d", t=ND), x[:], ALU.add))
                    after_free(i, "oself")
                    norm_stats(i, x1)
                    norm_apply(i, "x1", x1, x1, rows_ready)
                    b = after_act(i, "x1T")
                    free("x1T", nc.vector.tensor_tensor(xT[1][:], b[:].rearrange("p (k s) -> p k s", k=KD), xT[0][:], ALU.subtract))
                    split_q(i, 0)

                    def side(v):
                        if v % 4 == SIDE and v // 4 + 1 < PX:
                            split_q(i, v // 4 + 1)
                        if v == 5:
                            dve.wait_ge(x_loaded, 16 * i + 32)
                            norm_stats(i, x)
                        if v == 8:
                            norm_apply(i, "xn", x, xn, rows_ready)
                        if v == CTX_SLOT + 2:
                            context(i, "ctxT")
                        if v == XN_SLOT + 2:
                            split_rows(i, "xnT")

                    attend(i, U0, P0, UX, side)
                    norm_qk(i, "qk", "")
                    b = job(i, "ox")
                    dve.wait_ge(xb_ready, 2 * i + 2)
                    dve.wait_ge(s_out, 16 * i + 16)
                    free("ox", nc.vector.tensor_tensor(xo[:], b[:].rearrange("p (t d) -> p t d", t=ND), x1b[:], ALU.add))
                    after_free(i, "ox")
                    norm_stats(i, xo)
                    norm_apply(i, "xo", xo, xo, ln_done)
                    assert chain[0] - before == LINKS, chain[0] - before

            @block.tensor
            def _(pe):
                pe.wait_ge(s_gc, 6)

                def bank(i, name):
                    pe.wait_ge(job_free[JOB[name] % 2], FREED(i, name) - 1)
                    return ps_j[JOB[name] % 2]

                def product(out, terms):
                    n = 0
                    for stat, mov in terms:
                        for a, b in ((0, 0), (1, 0), (0, 1)):
                            last = nc.tensor.matmul(out, stat[a], mov[b], start=(n == 0), stop=(n == 3 * len(terms) - 1))
                            n += 1
                    return last

                both = lambda t, f: [f(t[0]), f(t[1])]

                def transposed(i, name, src):
                    b = bank(i, name)
                    for k in range(KD):
                        for s in range(ND):
                            last = nc.tensor.transpose(b[:, k * S + s * 128:k * S + s * 128 + 128], src[:, s, k * 128:k * 128 + 128], ident[:])
                    last.then_inc(job_raw, 1)

                def values(i, n):
                    b = bank(i, f"v{n}")
                    s, half = n // 2, n % 2
                    product(b[:], [(both(cT, lambda t: t[:, k, s * 128:s * 128 + 128]), both(wv, lambda t: t[:, k, half * 512:half * 512 + 512]))
                                   for k in range(KD)]).then_inc(job_raw, 1)

                def project(i, name, wt, p, src):
                    b = bank(i, name)
                    product(b[:, 0:S], [(both(wt, lambda t: t[:, k, p * 128:p * 128 + 128]), both(src, lambda t: t[:, k, :]))
                                        for k in range(KD)]).then_inc(job_raw, 1)

                def output(i, name, wt, pairs):
                    b = bank(i, name)
                    for s in range(ND):
                        last = product(b[:, s * D:s * D + D], [(both(oT, lambda t: t[:, p, s * 128:s * 128 + 128]), both(wt, lambda t: t[:, p, :]))
                                                               for p in range(pairs)])
                    last.then_inc(job_raw, 1)

                def attend(i, base, first_pair, units, side):
                    n = KEYS if base else S
                    kx = KX if base else ND
                    for v, us, ut, uc, pv, po, pl in schedule(units, first_pair):
                        if us is not None:
                            p, h, s = us // 4, us // 2 % 2, us % 2
                            if us % 4 == 0 and base:
                                pe.wait_ge(k_low, i * PX + p + 1)
                                pe.wait_ge(q_low, i * PX + p + 1)
                            pe.wait_ge(exped, i * U + base + (us + 1 if us >= BANKS else BANKS))
                            k_parts = both(ks, lambda t: t[:, p, :]) if base else both(kself, lambda t: t[:, p, :])
                            product(ps_s[us % BANKS][:, 0:n], [(both(qs, lambda t: t[:, p % 2, h, s * 128:s * 128 + 128]), k_parts)])\
                                .then_inc(scores_raw, 1)
                        side(v)
                        if ut is not None:
                            g = i * U + base + ut
                            pe.wait_ge(normed, g + 1)
                            pe.wait_ge(pt_copied[ut % 2], i * (U // 2) + (base + ut) // 2 + 1)
                            for k in range(kx):
                                last = nc.tensor.transpose(ps_t[ut % 2][:, k * 128:k * 128 + 128], pexp[ut % RING][:, k * 128:k * 128 + 128], ident[:])
                            last.then_inc(pt_raw, 1)
                        if pv is not None:
                            m = first_pair + pv
                            pe.wait_ge(o_split, i * PAIRS + m + 2)
                            pe.wait_ge(pt_copied[0], i * (U // 2) + 2 * m + 3)
                            pe.wait_ge(pt_copied[1], i * (U // 2) + 2 * m + 3)
                            vals = vx if base else vself
                            for k in range(kx):
                                for h in range(2):
                                    last = nc.tensor.matmul(ps_o[64 * h:64 * h + 64, 0:S], vals[:, k, pv * 128 + 64 * h:pv * 128 + 64 * h + 64],
                                                            pT[:, m % 2, h, k, :], start=(k == 0), stop=(k == kx - 1))
                            last.then_inc(o_raw, 1)

                pe.sem_inc(pt_raw, RING)
                pe.sem_inc(o_raw, 2)
                for b in range(2):
                    pe.sem_inc(job_free[b], 1)
                    pe.sem_inc(pt_copied[b], 1)

                def self_values(i, name):
                    b = bank(i, name)
                    for s in range(ND):
                        last = product(b[:, s * D:s * D + D], [(both(xT, lambda t: t[:, k, s * 128:s * 128 + 128]), both(wqkv, lambda t: t[:, k, 2 * D:3 * D]))
                                                               for k in range(KD)])
                    last.then_inc(job_raw, 1)

                def queries_keys(s):
                    product(ps_s[s][:], [(both(xT, lambda t: t[:, k, s * 128:s * 128 + 128]), both(wqkv, lambda t: t[:, k, 0:2 * D])) for k in range(KD)])\
                        .then_inc(qk_raw, 1)

                pe.wait_ge(ctx_loaded, 16)
                transposed(0, "first ctxT", cx)
                pe.wait_ge(rows_ready, 1)
                transposed(0, "first xnT", xn)
                pe.wait_ge(dve_part, 1)
                pe.wait_ge(w_low, 1)
                self_values(0, "first vself")
                queries_keys(0)
                queries_keys(1)
                pe.wait_ge(w_low, len(SPLIT))
                pe.wait_ge(s_small, 160)
                with pe.Fori(0, B) as i:
                    project(i, "k0", wk, 0, cT)
                    project(i, "k1", wk, 1, cT)
                    for s in range(ND):
                        b = bank(i, f"qkT{s}")
                        pe.wait_ge(qk_normed, ND * i + s + 1)
                        for k in range(4):
                            last = nc.tensor.transpose(b[:, k * 128:k * 128 + 128], sq[:, s, k * 128:k * 128 + 128], ident[:])
                        last.then_inc(job_raw, 1)
                    values(i, 0)
                    values(i, 1)
                    pe.wait_ge(dve_part, 2 * i + 2)

                    def fill(v):
                        n = FILL.get(v)
                        if n is not None:
                            values(i, 2 + n) if n < 2 else project(i, f"k{n}", wk, n, cT)

                    attend(i, 0, 0, U0, fill)
                    pe.wait_ge(o_split, i * PAIRS + P0 + 2)
                    output(i, "oself", wo0, P0)
                    for p in range(4, PX):
                        project(i, f"k{p}", wk, p, cT)
                    pe.wait_ge(rows_ready, 2 * i + 2)
                    transposed(i, "x1T", x1)
                    pe.wait_ge(job_free[JOB["x1T"] % 2], FREED(i, "x1T"))
                    project(i, "q0", wq, 0, xT)
                    project(i, "q1", wq, 1, xT)

                    def side(v):
                        if v % 4 == Q_SIDE and v // 4 + 2 < PX:
                            project(i, f"q{v // 4 + 2}", wq, v // 4 + 2, xT)
                        if v == CTX_SLOT:
                            pe.wait_ge(ctx_loaded, 16 * i + 32)
                            transposed(i, "ctxT", cx)
                        if v == XN_SLOT:
                            pe.wait_ge(rows_ready, 2 * i + 3)
                            transposed(i, "xnT", xn)
                        if v == QK_SLOT:
                            pe.wait_ge(dve_part, 2 * i + 3)
                            self_values(i, "vself")
                            queries_keys(0)
                            queries_keys(1)

                    attend(i, U0, P0, UX, side)
                    pe.wait_ge(o_split, i * PAIRS + PAIRS + 2)
                    output(i, "ox", wox, PX)


def moe_layer(nc, sems, name, x, x_in, x_out, w_router, b_router, ln_rows, w_up, b_up, w_down, b_down, slots, results, act, shared, renorm):
    fp32, fp32r, i32, u32 = mybir.dt.float32, mybir.dt.float32r, mybir.dt.int32, mybir.dt.uint32
    D = x.shape[2]
    T = x.shape[1] * 128
    F = w_up.shape[3]
    E = w_router.shape[1]
    KD, FT, TT = D // 128, F // 128, T // 128
    TILES_SHARED = T // SLOTS if shared else 0
    TILES_ROUTED = (TOP_K * T + E * (SLOTS - 1)) // SLOTS
    TILES = TILES_SHARED + TILES_ROUTED
    assert TILES % 2 == 1 and TILES_SHARED % 2 == 0 and KD == 2 and FT % 4 == 0
    PAIRS, PAIRS_SHARED = TILES // 2, TILES_SHARED // 2
    DVE_LOWS, POOL_LOWS = FT // 4, FT - FT // 4
    AHEAD = 3 if FT > 4 else 2
    X_STEP = FT - 2
    assert X_STEP > FT - 1 - AHEAD
    GATHERS = 4
    GROUP = 4
    GROUPS = TT // GROUP
    first_slot = T if shared else 0
    slots, results = slots[0:TILES * SLOTS, :], results[0:TILES * SLOTS, :]
    RING = 4

    ctx = ExitStack()
    with ctx:
        def sb(n, shape, dt=fp32):
            return ctx.enter_context(nc.sbuf_tensor(f"{name}_{n}", shape, dt))

        def sem(n):
            sems.append(nc.alloc_semaphore(f"{name}_{n}"))
            return sems[-1]

        xn = sb("xn", [128, TT, D]) if ln_rows is not None else x
        bcast = sb("bcast", [128, 2, D])
        wr = sb("wr", [128, KD, E])
        br = sb("br", [128, E])
        ident = sb("ident", [128, 128])
        tri = sb("tri", [128, 128])
        ones = sb("ones", [128, 128])
        iota_e = sb("iota_e", [128, E])
        tile_start = sb("tile_start", [128, TILES_ROUTED])
        not_first = sb("not_first", [128, E, TT])
        stats = sb("stats", [128, TT, 6])
        mv = sb("mv", [128, TT, 2])
        rstd = sb("rstd", [128, TT])
        xT_r = sb("xT_r", [128, 2, KD, 128])
        prob = sb("prob", [128, TT, E])
        red = sb("red", [128, TT])
        top = sb("top", [128, TT, 8])
        topi = sb("topi", [128, TT, 8], u32)
        topf = sb("topf", [128, TT, 2])
        wt = sb("wt", [128, TT, 2])
        wsum = sb("wsum", [128, TT])
        hot = sb("hot", [128, 2, TT, E])
        hots = sb("hots", [128, TT, E])
        tot = sb("tot", [128, E, TT])
        incl = sb("incl", [128, E, TT])
        rank = sb("rank", [128, TT, E])
        cnt = sb("cnt", [128, 4, E])
        cnt_i = sb("cnt_i", [128, 2, E], i32)
        slot_f = sb("slot_f", [128, 2, TT])
        slot_i = sb("slot_i", [128, 2, TT], i32)
        cmp = sb("cmp", [128, TILES_ROUTED, E])
        te_f = sb("te_f", [128, TILES])
        te = sb("te", [128, TILES], i32)
        b2s = sb("b2s", [E, D])
        ctot = sb("ctot", [128, D])
        b1_all = sb("b1_all", [128, E, FT])

        xrow = sb("xrow", [128, 2, 2, D])
        xT = sb("xT", [128, 2, 2, KD, SLOTS], fp32r)
        w1 = sb("w1", [128, 2, KD, F])
        w2 = sb("w2", [128, 2, FT, D])
        w1s = [[sb(f"w1s{b}{h}", [128, KD, F], fp32r) for h in range(2)] for b in range(2)]
        w2s = [[sb(f"w2s{b}{h}", [128, FT, D], fp32r) for h in range(2)] for b in range(2)]
        b1 = sb("b1", [128, 2, FT])
        rb1 = sb("rb1", [128, 2, FT])
        hact = sb("hact", [128, RING, SLOTS])
        hs = [sb(f"hs{h}", [128, RING, SLOTS], fp32r) for h in range(2)]
        yrow = sb("yrow", [128, 2, 2, D])
        gath = w1[:].rearrange("p b k f -> p (b k f)").rearrange("p (n d) -> p n d", d=D)
        own = w2[:].rearrange("p b f d -> p (b f) d")

        CT_RING = 4
        ct_w = [w2[:, 0], w2[:, 1]] + [w1[:, b].rearrange("p k f -> p (k f)").rearrange("p (f d) -> p f d", d=D) for b in range(2)]

        ps = [ctx.enter_context(nc.psum_tensor(f"{name}_ps{n}", [128, 512], fp32)) for n in range(8)]
        ps_h, ps_c, ps_t, ps_r = ps[0:4], ps[4], ps[6], ps[7]
        ps_hid = [ps[r][:, 0:SLOTS] for r in range(RING)]
        ps_y = [ps[4 + b][:].rearrange("p (s d) -> p s d", s=2) for b in range(2)]

        def weights_of(i, b, kept=False):
            k = b - TILES_SHARED + shared
            return (0, 0, 0) if kept else (i * 2 + k, i + k // 2, k % 2)

        def run_tiles(eng, steps):
            if shared:
                with eng.Fori(0, PAIRS_SHARED - 1) as i:
                    steps(i, 0, True, True, 2)
                    steps(i, 1, True, True, 2)
                steps(PAIRS_SHARED - 1, 0, True, True, 2)
                steps(PAIRS_SHARED - 1, 1, True, False, 2)
            with eng.Fori(PAIRS_SHARED, PAIRS - 1) as i:
                steps(i, 0, False, False, 2)
                steps(i, 1, False, False, 2)
            steps(PAIRS - 1, 0, False, False, 2)
            steps(PAIRS - 1, 1, False, False, 1)
            steps(PAIRS, 0, False, False, 0)

        def chunk(c, weights):
            w1v, w2v = weights
            return w1v[:, :, c * 128:(c + 2) * 128] if c % 2 == 0 else w2v[:, c - 1:c + 1, :]

        def low_ready(eng, n, c):
            if c % 4 == 0:
                eng.wait_ge(w_low_dve, (n + 2) * DVE_LOWS + c // 4 + 1)
            else:
                eng.wait_ge(w_low_pool, (n + 2) * POOL_LOWS + c - c // 4)

        def make_low(op, wb, c, done):
            op(chunk(c, (w1s[wb][1], w2s[wb][1])), chunk(c, (w1[:, wb], w2[:, wb])),
               chunk(c, (w1s[wb][0], w2s[wb][0])), ALU.subtract).then_inc(done, 1)


        s_x = [sem(f"s_x{g}") for g in range(TT // 4)]; s_const = sem("s_const"); s_gconst = sem("s_gconst")
        s_xn = sem("s_xn"); s_tr = sem("s_tr"); s_ev = sem("s_ev"); s_logit = sem("s_logit")
        s_soft = sem("s_soft"); s_exp = sem("s_exp"); s_hot = sem("s_hot"); s_cnt = sem("s_cnt")
        s_slots = sem("s_slots"); s_te = sem("s_te"); s_scat = sem("s_scat"); s_dve = sem("s_dve")
        s_ctw = [sem(f"s_ctw{b}") for b in range(4)]; s_ctb = sem("s_ctb"); s_ctm = sem("s_ctm")
        s_ctp = sem("s_ctp"); s_var = sem("s_var"); s_rstd = sem("s_rstd"); s_ctot = sem("s_ctot")
        xrow_loaded = [sem(f"xrow_loaded{b}") for b in range(2)]
        w_loaded = [sem(f"w_loaded{b}") for b in range(2)]
        xT_raw = sem("xT_raw"); xT_split = sem("xT_split")
        w_high = sem("w_high"); w_low_pool = sem("w_low_pool"); w_low_dve = sem("w_low_dve"); bias_ready = sem("bias_ready")
        h_raw = sem("h_raw"); h_act = sem("h_act"); h_high = sem("h_high"); h_split = sem("h_split"); h_used = sem("h_used")
        y_copied = sem("y_copied"); y_stored = [sem(f"y_stored{b}") for b in range(2)]
        s_gath = [sem(f"s_gath{b}") for b in range(GATHERS)]; s_own = [sem(f"s_own{b}") for b in range(GATHERS)] if shared else None; s_comb = sem("s_comb"); s_norm = sem("s_norm")
        s_out = sem("s_out")

        by_tile = lambda a: a.rearrange("(t p) d -> p t d", p=128)

        with nc.Block() as block:
            @block.sync
            def _(sp):
                sp.dma_start(wr[:], w_router.rearrange("(k p) e -> p k e", p=128)).then_inc(s_const, 16)
                if b_router is not None:
                    sp.dma_start(br[:], b_router.partition_broadcast(128)).then_inc(s_const, 16)
                if ln_rows is not None:
                    for n in range(2):
                        sp.dma_start(bcast[:, n, :], ln_rows[n].partition_broadcast(128)).then_inc(s_const, 16)
                if x_in is not None:
                    for g in range(GROUPS):
                        sp.dma_start(x[:, g * GROUP:(g + 1) * GROUP, :], by_tile(x_in)[:, g * GROUP:(g + 1) * GROUP, :]).then_inc(s_x[g], 16)
                if b_down is not None:
                    sp.dma_start(b1_all[:], b_up[0:E].rearrange("e p f -> p e f")).then_inc(s_ctb, 16)
                    sp.dma_start(b2s[:], b_down).then_inc(s_ctb, 16)
                    for e in range(E):
                        if e >= CT_RING:
                            sp.wait_ge(s_ctm, e - CT_RING + 1)
                        sp.dma_start(ct_w[e % CT_RING], w_down[e]).then_inc(s_ctw[e % CT_RING], 16)

                def load_rows(i, b, routed):
                    tile = i * 2 + b
                    sp.wait_ge(xT_raw, tile + 1)
                    rows = by_tile(slots[bass.ds(tile * SLOTS, SLOTS), :]) if routed else x[:, bass.ds(tile * 2, 2), :]
                    sp.dma_start(xrow[:, b, :, :], rows).then_inc(xrow_loaded[b], 16)

                def load_weights(i, b):
                    n, half, wb = weights_of(i, b)
                    e = sp.value_load(te[0:1, bass.ds(i * 2 + b, 1)], min_val=0, max_val=w_up.shape[0] - 1)
                    sp.wait_ge(w_low_pool, (n + 1) * POOL_LOWS)
                    sp.dma_start(w2[:, wb, :, :], w_down[bass.ds(e, 1)].rearrange("a p f d -> p (a f) d")).then_inc(w_loaded[wb], 16)
                    sp.wait_ge(w_low_dve, (n + 1) * DVE_LOWS)
                    sp.dma_start(w1[:, wb, :, :], w_up[bass.ds(e, 1)].rearrange("a p k f -> p (a k) f")).then_inc(w_loaded[wb], 16)
                    if b_up is not None:
                        sp.wait_ge(h_split, n * FT + 1)
                        sp.dma_start(b1[:, wb, :], b_up[bass.ds(e, 1)].rearrange("a p f -> p (a f)")).then_inc(w_loaded[wb], 16)

                if shared:
                    sp.dma_start(w1[:, 0, :, :], w_up[E]).then_inc(w_loaded[0], 16)
                    sp.dma_start(w2[:, 0, :, :], w_down[E]).then_inc(w_loaded[0], 16)
                    with sp.Fori(0, PAIRS_SHARED) as i:
                        load_rows(i, 0, False)
                        load_rows(i, 1, False)
                sp.wait_ge(s_te, 1)
                if b_down is not None:
                    sp.wait_ge(s_ctm, E)
                load_weights(PAIRS_SHARED, 0)
                sp.wait_ge(s_scat, 16 * 2 * TT)
                load_rows(PAIRS_SHARED, 0, True)
                load_rows(PAIRS_SHARED, 1, True)
                with sp.Fori(PAIRS_SHARED, PAIRS - 1) as i:
                    for b in range(2):
                        load_weights(i, b + 1)
                        load_rows(i + 1, b, True)
                load_weights(PAIRS - 1, 1)
                load_rows(PAIRS, 0, True)
                load_weights(PAIRS - 1, 2)
                if shared:
                    sp.wait_ge(y_stored[0], 16 * (PAIRS + 2))
                    sp.wait_ge(y_stored[1], 16 * (PAIRS + 1))
                    for t in range(TT):
                        if t >= GATHERS:
                            sp.wait_ge(s_comb, t - GATHERS + 1)
                        sp.dma_start(own[:, t % GATHERS, :], results[t * 128:(t + 1) * 128, :]).then_inc(s_own[t % GATHERS], 16)
                if x_out is not None:
                    for g in range(GROUPS):
                        sp.wait_ge(s_norm, GROUP * (g + 1))
                        sp.dma_start(by_tile(x_out)[:, g * GROUP:(g + 1) * GROUP, :], x[:, g * GROUP:(g + 1) * GROUP, :]).then_inc(s_out, 16)
                    sp.wait_ge(s_out, 16 * GROUPS)

            @block.gpsimd
            def _(pool):
                nc.gpsimd.memset(ident[:], 0.0).then_inc(s_gconst, 1)
                nc.gpsimd.memset(ones[:], 1.0).then_inc(s_gconst, 1)
                nc.gpsimd.memset(not_first[:], 1.0).then_inc(s_gconst, 1)
                nc.gpsimd.iota(iota_e[:], [[1, E]], base=0, channel_multiplier=0, allow_small_or_imprecise_dtypes=True).then_inc(s_gconst, 1)
                nc.gpsimd.iota(tile_start[:], [[SLOTS, TILES_ROUTED]], base=0, channel_multiplier=0, allow_small_or_imprecise_dtypes=True).then_inc(s_gconst, 1)
                pool.wait_ge(s_gconst, 5)
                nc.gpsimd.affine_select(out=ident[:], in_=ident[:], compare_op=ALU.not_equal, fill=1.0, base=0,
                                        pattern=[[-1, 128]], channel_multiplier=1).then_inc(s_gconst, 1)
                nc.gpsimd.affine_select(out=tri[:], in_=ones[:], compare_op=ALU.is_gt, fill=0.0, base=0,
                                        pattern=[[1, 128]], channel_multiplier=-1).then_inc(s_gconst, 1)
                nc.gpsimd.memset(not_first[:, :, 0:1], 0.0).then_inc(s_gconst, 1)
                pool.wait_ge(s_slots, 1)
                for t in range(TT):
                    for k in range(2):
                        nc.gpsimd.indirect_dma_start(slots, bass.IndirectOffsetOnAxis(ap=slot_i[:, k, t:t + 1], axis=0),
                                                     xn[:, t, :], None).then_inc(s_scat, 16)

                def low_parts(i, b):
                    n, half, wb = weights_of(i, b)
                    for c in range(FT):
                        if c % 4 != 0:
                            pool.wait_ge(w_high, n * FT + c + 1)
                            make_low(nc.gpsimd.tensor_tensor, wb, c, w_low_pool)

                if shared:
                    low_parts(PAIRS_SHARED, 0)
                with pool.Fori(PAIRS_SHARED, PAIRS) as i:
                    low_parts(i, 1)
                    low_parts(i, 2)
                pool.wait_ge(y_stored[0], 16 * (PAIRS + 2))
                pool.wait_ge(y_stored[1], 16 * (PAIRS + 1))
                for t in range(TT):
                    if t >= GATHERS:
                        pool.wait_ge(s_comb, t - GATHERS + 1)
                    for k in range(2):
                        nc.gpsimd.indirect_dma_start(gath[:, t % GATHERS * 2 + k, :], None, results,
                                                     bass.IndirectOffsetOnAxis(ap=slot_i[:, k, t:t + 1], axis=0)).then_inc(s_gath[t % GATHERS], 16)

            @block.scalar
            def _(act_e):
                def take_root(g, count):
                    act_e.wait_ge(s_var, count)
                    cols = slice(g * GROUP, (g + 1) * GROUP)
                    nc.scalar.activation(rstd[:, cols], rstd[:, cols], ACT.Sqrt).then_inc(s_rstd, 1)

                for g in range(GROUPS):
                    if ln_rows is not None:
                        take_root(g, g + 1)
                    for t in range(g * GROUP, (g + 1) * GROUP):
                        act_e.wait_ge(s_tr, t + 1)
                        if t >= 2:
                            act_e.wait_ge(s_logit, t - 1)
                        nc.scalar.copy(xT_r[:, t % 2, :, :], ps_h[t % 2][:, 0:KD * 128].rearrange("p (k n) -> p k n", k=KD)).then_inc(s_ev, 1)
                act_e.wait_ge(s_soft, 1)
                nc.scalar.activation(prob[:], prob[:], ACT.Exp).then_inc(s_exp, 1)

                def high_part(weights, tile, c):
                    n, half, wb = weights
                    if c == 0:
                        act_e.wait_ge(w_loaded[wb], (half + 1) * W_DMAS * 16)
                        if tile is not None:
                            act_e.wait_ge(h_used, tile * FT + 1)
                    nc.scalar.copy(chunk(c, (w1s[wb][0], w2s[wb][0])), chunk(c, (w1[:, wb], w2[:, wb]))).then_inc(w_high, 1)

                def hidden(i, b, ft, weights):
                    wb = weights[2]
                    n = (i * 2 + b) * FT + ft
                    act_e.wait_ge(h_raw, n + 1)
                    act_e.wait_ge(h_split, n + 2 + FT - RING)
                    if b_up is not None and ft == 0:
                        act_e.wait_ge(w_loaded[wb], (weights[1] + 1) * W_DMAS * 16)
                    nc.scalar.activation(hact[:, ft % RING, :], ps_hid[ft % RING], act,
                                         bias=b1[:, wb, ft:ft + 1] if b_up is not None else 0.0).then_inc(h_act, 1)

                def result(i, b):
                    tile = i * 2 + b
                    act_e.wait_ge(h_used, tile * FT + FT + FT + 1)
                    act_e.wait_ge(y_stored[b], i * 16 + 16)
                    nc.scalar.copy(yrow[:, b, :, :], ps_y[b]).then_inc(y_copied, 1)
                    act_e.wait_ge(y_copied, tile + 3)
                    act_e.dma_start(results[bass.ds(tile * SLOTS, SLOTS), :].rearrange("(s p) d -> p s d", p=128),
                                    yrow[:, b, :, :]).then_inc(y_stored[b], 16)

                W_DMAS = 3 if b_up is not None else 2
                act_e.sem_inc(h_act, RING)
                act_e.sem_inc(y_copied, 2)
                for b in range(2):
                    act_e.sem_inc(y_stored[b], 16)
                first = weights_of(0, 0, shared)
                for c in range(FT):
                    high_part(first, None, c)
                for ft in range(AHEAD):
                    hidden(0, 0, ft, first)

                def tile_steps(i, b, kept, next_kept, tiles_after):
                    ni, nb = (i, 1) if b == 0 else (i + 1, 0)
                    now, nxt = weights_of(i, b, kept), weights_of(i, b + 1, next_kept)
                    for ft in range(FT):
                        if ft + AHEAD < FT:
                            hidden(i, b, ft + AHEAD, now)
                        elif tiles_after:
                            hidden(ni, nb, ft + AHEAD - FT, nxt)
                        if tiles_after and not next_kept:
                            high_part(nxt, i * 2 + b + 1, ft)
                    result(i, b)

                run_tiles(act_e, tile_steps)
                for g in range(GROUPS):
                    take_root(g, (GROUPS if ln_rows is not None else 0) + g + 1)

            @block.vector
            def _(dve):
                chain, norms = [0], [0]

                def link(ins):
                    chain[0] += 1
                    ins.then_inc(s_dve, 1)
                    dve.wait_ge(s_dve, chain[0])

                def norm_stats(g):
                    group = range(g * GROUP, (g + 1) * GROUP)
                    for t in group:
                        last = nc.vector.bn_stats(stats[:, t, :], x[:, t, :])
                    link(last)
                    for t in group:
                        last = nc.vector.bn_aggr(mv[:, t, :], stats[:, t, :])
                    link(last)
                    cols = slice(g * GROUP, (g + 1) * GROUP)
                    nc.vector.tensor_scalar(rstd[:, cols], mv[:, cols, 1], LN_EPS, None, ALU.add).then_inc(s_var, 1)

                def inverse_root(g):
                    norms[0] += 1
                    dve.wait_ge(s_rstd, norms[0])
                    cols = slice(g * GROUP, (g + 1) * GROUP)
                    link(nc.vector.reciprocal(rstd[:, cols], rstd[:, cols]))

                dve.wait_ge(s_const, 16 * (1 + (b_router is not None) + 2 * (ln_rows is not None)))
                for g in range(GROUPS):
                    if b_down is not None and g == 1:
                        dve.wait_ge(s_ctb, 32)
                        nc.vector.tensor_scalar(b1_all[:], b1_all[:], 0.0, None, ALU.max).then_inc(s_ctp, 1)
                    if x_in is not None:
                        dve.wait_ge(s_x[g], 16)
                    if ln_rows is not None:
                        norm_stats(g)
                        for t in range(g * GROUP, (g + 1) * GROUP):
                            last = nc.vector.scalar_tensor_tensor(xn[:, t, :], x[:, t, :], mv[:, t, 0:1], bcast[:, 0, :], ALU.subtract, ALU.mult)
                        link(last)
                        inverse_root(g)
                        for t in range(g * GROUP, (g + 1) * GROUP):
                            nc.vector.scalar_tensor_tensor(xn[:, t, :], xn[:, t, :], rstd[:, t:t + 1], bcast[:, 1, :], ALU.mult, ALU.add).then_inc(s_xn, 1)
                dve.wait_ge(s_logit, TT)
                dve.wait_ge(s_gconst, 8)
                logits = ps_r[:, 0:TT * E].rearrange("p (t e) -> p t e", e=E)
                if b_router is not None:
                    link(nc.vector.tensor_tensor(prob[:], logits, br[:].unsqueeze(1).to_broadcast([128, TT, E]), ALU.add))
                else:
                    link(nc.vector.tensor_copy(prob[:], logits))
                link(nc.vector.tensor_reduce(red[:], prob[:], AX.X, ALU.max))
                nc.vector.tensor_tensor(prob[:], prob[:], red[:].unsqueeze(2).to_broadcast([128, TT, E]), ALU.subtract).then_inc(s_soft, 1)
                dve.wait_ge(s_exp, 1)
                link(nc.vector.tensor_reduce(red[:], prob[:], AX.X, ALU.add))
                link(nc.vector.reciprocal(red[:], red[:]))
                link(nc.vector.tensor_tensor(prob[:], prob[:], red[:].unsqueeze(2).to_broadcast([128, TT, E]), ALU.mult))
                for t in range(TT):
                    last = nc.vector.max(top[:, t, :], prob[:, t, :])
                link(last)
                for t in range(TT):
                    last = nc.vector.max_index(topi[:, t, :], top[:, t, :], prob[:, t, :])
                link(last)
                nc.vector.tensor_copy(topf[:], topi[:, :, 0:2])
                link(nc.vector.tensor_tensor(wsum[:], top[:, :, 0], top[:, :, 1], ALU.add))
                if renorm:
                    link(nc.vector.reciprocal(red[:], wsum[:]))
                    link(nc.vector.tensor_tensor(wt[:], top[:, :, 0:2], red[:].unsqueeze(2).to_broadcast([128, TT, 2]), ALU.mult))
                else:
                    link(nc.vector.tensor_copy(wt[:], top[:, :, 0:2]))
                for k in range(2):
                    last = nc.vector.tensor_tensor(hot[:, k, :, :], iota_e[:].unsqueeze(1).to_broadcast([128, TT, E]),
                                                   topf[:, :, k:k + 1].to_broadcast([128, TT, E]), ALU.is_equal)
                link(last)
                nc.vector.tensor_tensor(hots[:], hot[:, 0, :, :], hot[:, 1, :, :], ALU.add).then_inc(s_hot, 1)
                dve.wait_ge(s_cnt, 1)
                link(nc.vector.tensor_copy(tot[:], ps_h[3][:, 0:TT * E].rearrange("p (t e) -> p e t", e=E)))
                link(nc.vector.tensor_tensor_scan(incl[:].rearrange("p e t -> p (e t)"), not_first[:].rearrange("p e t -> p (e t)"),
                                                  tot[:].rearrange("p e t -> p (e t)"), 0.0, ALU.mult, ALU.add))
                link(nc.vector.tensor_tensor(tot[:], incl[:], tot[:], ALU.subtract))
                link(nc.vector.tensor_scalar(cnt_i[:, 0, :], incl[:, :, TT - 1], float(SLOTS - 1), None, ALU.add))
                link(nc.vector.tensor_scalar(cnt_i[:, 1, :], cnt_i[:, 0, :], SLOT_BITS, SLOT_BITS, ALU.logical_shift_right, ALU.logical_shift_left))
                link(nc.vector.tensor_copy(cnt[:, 2, :], cnt_i[:, 1, :]))
                link(nc.vector.tensor_tensor_scan(cnt[:, 3, :], ones[:, 0:E], cnt[:, 2, :], 0.0, ALU.mult, ALU.add))
                link(nc.vector.tensor_tensor(cnt[:, 0, :], cnt[:, 3, :], cnt[:, 2, :], ALU.subtract))
                link(nc.vector.tensor_tensor(rank[:], ps_h[2][:, 0:TT * E].rearrange("p (t e) -> p t e", e=E),
                                             tot[:].rearrange("p e t -> p t e"), ALU.add))
                link(nc.vector.tensor_tensor(rank[:], rank[:], cnt[:, 0, :].unsqueeze(1).to_broadcast([128, TT, E]), ALU.add))
                for k in range(2):
                    last = nc.vector.tensor_tensor(hot[:, k, :, :], hot[:, k, :, :], rank[:], ALU.mult)
                link(last)
                for k in range(2):
                    last = nc.vector.tensor_reduce(slot_f[:, k, :], hot[:, k, :, :], AX.X, ALU.add)
                link(last)
                nc.vector.tensor_scalar(slot_i[:], slot_f[:], float(first_slot), None, ALU.add).then_inc(s_slots, 1)
                link(nc.vector.tensor_tensor(cmp[:], cnt[:, 3, :].unsqueeze(1).to_broadcast([128, TILES_ROUTED, E]),
                                             tile_start[:].unsqueeze(2).to_broadcast([128, TILES_ROUTED, E]), ALU.is_le))
                if shared:
                    link(nc.vector.memset(te_f[:], float(E)))
                link(nc.vector.tensor_reduce(te_f[:, TILES_SHARED:TILES], cmp[:], AX.X, ALU.add))
                link(nc.vector.tensor_scalar(te_f[:, TILES_SHARED:TILES], te_f[:, TILES_SHARED:TILES], float(E - 1), None, ALU.min))
                nc.vector.tensor_copy(te[:], te_f[:]).then_inc(s_te, 1)
                if b_down is not None:
                    dve.wait_ge(s_ctm, E + 1)
                    nc.vector.tensor_copy(ctot[:], ps_c[:, 0:D]).then_inc(s_ctot, 1)
                    link(nc.vector.tensor_scalar(x[:], x[:], 2.0, None, ALU.mult))

                def split_x(i, b):
                    tile = i * 2 + b
                    dve.wait_ge(xT_raw, tile + 3)
                    view = ps_t[:, 0:KD * SLOTS].rearrange("p (k n) -> p k n", k=KD)
                    nc.vector.tensor_copy(xT[:, b, 0, :, :], view).then_inc(xT_split, 1)
                    dve.wait_ge(xT_split, 2 * tile + 2)
                    nc.vector.tensor_tensor(xT[:, b, 1, :, :], view, xT[:, b, 0, :, :], ALU.subtract).then_inc(xT_split, 1)

                def split_hidden(i, b, ft, weights):
                    half, wb = weights[1:]
                    n = (i * 2 + b) * FT + ft
                    r = ft % RING
                    if b_up is not None and ft == 0:
                        dve.wait_ge(w_loaded[wb], (half + 1) * 48)
                        nc.vector.tensor_scalar(rb1[:, wb, :], b1[:, wb, :], 0.0, None, ALU.max).then_inc(bias_ready, 1)
                        dve.wait_ge(bias_ready, i * 2 + b + 1)
                    dve.wait_ge(h_act, n + 1 + RING)
                    dve.wait_ge(h_used, n + 2 + FT - RING)
                    if b_up is not None:
                        nc.vector.tensor_scalar(hs[0][:, r, :], hact[:, r, :], rb1[:, wb, ft:ft + 1], None, ALU.subtract).then_inc(h_high, 1)
                        dve.wait_ge(h_high, n + 1)
                        nc.vector.scalar_tensor_tensor(hs[1][:, r, :], hact[:, r, :], rb1[:, wb, ft:ft + 1], hs[0][:, r, :],
                                                       ALU.subtract, ALU.subtract).then_inc(h_split, 1)
                    else:
                        nc.vector.tensor_copy(hs[0][:, r, :], hact[:, r, :]).then_inc(h_high, 1)
                        dve.wait_ge(h_high, n + 1)
                        nc.vector.tensor_tensor(hs[1][:, r, :], hact[:, r, :], hs[0][:, r, :], ALU.subtract).then_inc(h_split, 1)

                dve.sem_inc(h_split, FT + 1)
                dve.sem_inc(xT_split, 1)
                dve.sem_inc(w_low_pool, 2 * POOL_LOWS)
                dve.sem_inc(w_low_dve, 2 * DVE_LOWS)
                first = weights_of(0, 0, shared)
                for c in range(FT):
                    dve.wait_ge(w_high, c + 1)
                    make_low(nc.vector.tensor_tensor, 0, c, w_low_dve if c % 4 == 0 else w_low_pool)
                split_x(0, 0)
                split_x(0, 1)
                for ft in range(AHEAD):
                    split_hidden(0, 0, ft, first)

                def tile_steps(i, b, kept, next_kept, tiles_after):
                    ni, nb = (i, 1) if b == 0 else (i + 1, 0)
                    now, nxt = weights_of(i, b, kept), weights_of(i, b + 1, next_kept)
                    for ft in range(FT):
                        if ft + AHEAD < FT:
                            split_hidden(i, b, ft + AHEAD, now)
                        elif tiles_after:
                            split_hidden(ni, nb, ft + AHEAD - FT, nxt)
                        if ft == X_STEP and tiles_after == 2:
                            split_x(i + 1, b)
                        if ft % 4 == 0 and tiles_after and not next_kept:
                            n, half, wb = nxt
                            dve.wait_ge(w_high, n * FT + ft + 1)
                            make_low(nc.vector.tensor_tensor, wb, ft, w_low_dve)

                run_tiles(dve, tile_steps)

                for g in range(GROUPS):
                    for t in range(g * GROUP, (g + 1) * GROUP):
                        dve.wait_ge(s_gath[t % GATHERS], 16 * 2 * (t // GATHERS + 1))
                        r = t % GATHERS * 2
                        link(nc.vector.scalar_tensor_tensor(x[:, t, :], gath[:, r, :], wt[:, t, 0:1], x[:, t, :], ALU.mult, ALU.add))
                        link(nc.vector.scalar_tensor_tensor(x[:, t, :], gath[:, r + 1, :], wt[:, t, 1:2], x[:, t, :], ALU.mult, ALU.add))
                        if shared:
                            dve.wait_ge(s_own[t % GATHERS], 16 * (t // GATHERS + 1))
                            nc.vector.tensor_tensor(x[:, t, :], own[:, t % GATHERS, :], x[:, t, :], ALU.add).then_inc(s_comb, 1)
                        else:
                            nc.vector.scalar_tensor_tensor(x[:, t, :], ctot[:], wsum[:, t:t + 1], x[:, t, :], ALU.mult, ALU.add).then_inc(s_comb, 1)
                    dve.wait_ge(s_comb, (g + 1) * GROUP)
                    norm_stats(g)
                    inverse_root(g)
                    for t in range(g * GROUP, (g + 1) * GROUP):
                        nc.vector.tensor_scalar(x[:, t, :], x[:, t, :], mv[:, t, 0:1], rstd[:, t:t + 1], ALU.subtract, ALU.mult).then_inc(s_norm, 1)

            @block.tensor
            def _(pe):
                pe.wait_ge(s_gconst, 8)
                pe.wait_ge(s_const, 16)

                def constant(e):
                    pe.wait_ge(s_ctp, 1)
                    pe.wait_ge(s_ctw[e % CT_RING], (e // CT_RING + 1) * 16)
                    for ft in range(FT):
                        last = nc.tensor.matmul(ps_c[:, 0:D], b1_all[:, e, ft:ft + 1].to_broadcast([128, 128]), ct_w[e % CT_RING][:, ft, :],
                                                start=(e == 0 and ft == 0), stop=False)
                    last.then_inc(s_ctm, 1)

                def router_logits(t):
                    pe.wait_ge(s_ev, t + 1)
                    for k in range(KD):
                        last = nc.tensor.matmul(ps_r[:, t * E:(t + 1) * E], xT_r[:, t % 2, k, :], wr[:, k, :],
                                                start=(k == 0), stop=(k == KD - 1))
                    last.then_inc(s_logit, 1)

                for t in range(TT):
                    if ln_rows is not None:
                        pe.wait_ge(s_xn, t + 1)
                    elif x_in is not None and t % GROUP == 0:
                        pe.wait_ge(s_x[t // GROUP], 16)
                    if t >= 2:
                        pe.wait_ge(s_ev, t - 1)
                    for k in range(KD):
                        last = nc.tensor.transpose(ps_h[t % 2][:, k * 128:(k + 1) * 128], xn[:, t, k * 128:(k + 1) * 128], ident[:])
                    last.then_inc(s_tr, 1)
                    if t >= 1:
                        router_logits(t - 1)
                router_logits(TT - 1)
                if b_down is not None:
                    constant(0)
                pe.wait_ge(s_hot, 1)
                hot_cols = hots[:].rearrange("p t e -> p (t e)")
                nc.tensor.matmul(ps_h[2][:, 0:TT * E], tri[:], hot_cols, start=True, stop=True)
                nc.tensor.matmul(ps_h[3][:, 0:TT * E], ones[:], hot_cols, start=True, stop=True).then_inc(s_cnt, 1)
                if b_down is not None:
                    for e in range(1, E):
                        constant(e)
                    nc.tensor.matmul(ps_c[:, 0:D], ones[0:E, :], b2s[:], start=False, stop=True).then_inc(s_ctm, 1)

                def transposes(i, b):
                    tile = i * 2 + b
                    pe.wait_ge(xrow_loaded[b], (i + 1) * 16)
                    pe.wait_ge(xT_split, 2 * tile + 1)
                    for k in range(KD):
                        for s in range(2):
                            last = nc.tensor.transpose(ps_t[:, k * SLOTS + s * 128:k * SLOTS + (s + 1) * 128],
                                                       xrow[:, b, s, k * 128:(k + 1) * 128], ident[:])
                    last.then_inc(xT_raw, 1)

                def up(i, b, ft, weights):
                    number, half, wb = weights
                    n = (i * 2 + b) * FT + ft
                    if ft == 0:
                        pe.wait_ge(xT_split, 4 * i + 2 * b + 3)
                    if ft % 2 == 0:
                        low_ready(pe, number, ft)
                    pe.wait_ge(h_act, n + 1)
                    for k in range(KD):
                        for wp, xp in ((0, 0), (1, 0), (0, 1)):
                            last = nc.tensor.matmul(ps_hid[ft % RING], w1s[wb][wp][:, k, ft * 128:(ft + 1) * 128],
                                                    xT[:, b, xp, k, :], start=(k == 0 and wp == 0 and xp == 0),
                                                    stop=(k == KD - 1 and xp == 1))
                    last.then_inc(h_raw, 1)

                def down(i, b, ft, weights):
                    number, half, wb = weights
                    n = (i * 2 + b) * FT + ft
                    if ft == 0:
                        pe.wait_ge(y_copied, i * 2 + b + 1)
                    if ft % 2 == 0:
                        low_ready(pe, number, ft + 1)
                    pe.wait_ge(h_split, n + 2 + FT)
                    for s in range(2):
                        for hp, wp in ((0, 0), (1, 0), (0, 1)):
                            last = nc.tensor.matmul(ps_y[b][:, s, :], hs[hp][:, ft % RING, s * 128:(s + 1) * 128],
                                                    w2s[wb][wp][:, ft, :], start=(ft == 0 and s == 0 and hp == 0 and wp == 0),
                                                    stop=(ft == FT - 1 and wp == 1 and s == 1))
                    last.then_inc(h_used, 1)

                pe.sem_inc(xT_raw, 2)
                pe.sem_inc(h_used, FT + 1)
                if b_down is not None:
                    pe.wait_ge(s_ctot, 1)
                transposes(0, 0)
                transposes(0, 1)
                first = weights_of(0, 0, shared)
                for ft in range(AHEAD):
                    up(0, 0, ft, first)

                def tile_steps(i, b, kept, next_kept, tiles_after):
                    ni, nb = (i, 1) if b == 0 else (i + 1, 0)
                    now, nxt = weights_of(i, b, kept), weights_of(i, b + 1, next_kept)
                    for ft in range(FT):
                        if ft == X_STEP and tiles_after == 2:
                            transposes(i + 1, b)
                        if ft + AHEAD < FT:
                            up(i, b, ft + AHEAD, now)
                        elif tiles_after:
                            up(ni, nb, ft + AHEAD - FT, nxt)
                        down(i, b, ft, now)

                run_tiles(pe, tile_steps)


def state_space_layer(nc, sems, x, S, w):
    fp32, fp32r = mybir.dt.float32, mybir.dt.float32r
    TT, D = x.shape[1:]
    T, KD = TT * 128, D // 128
    N = w["a_log"].shape[2]
    R = w["dt_w"].shape[0]
    RBC = R + 2 * N
    CH = T // 512
    RING = 4
    RING_C = 4
    GROUP = TT // 4
    assert KD == 2 and N % 4 == 0

    ctx = ExitStack()
    with ctx:
        def sb(n, shape, dt=fp32):
            return ctx.enter_context(nc.sbuf_tensor(f"s_{n}", shape, dt))

        def sem(n):
            sems.append(nc.alloc_semaphore(f"s_{n}"))
            return sems[-1]

        xT = sb("xT", [128, KD, T])
        delta = sb("delta", [128, KD, T])
        dx = sb("dx", [128, KD, T])
        y = x[:].rearrange("p t d -> p (t d)").rearrange("p (k n) -> p k n", k=KD)
        proj = sb("proj", [128, KD, RBC])
        dtw = sb("dtw", [RBC, D])
        dtb = sb("dtb", [128, KD])
        dskip = sb("dskip", [128, KD])
        neg_a = sb("neg_a", [128, KD, N])
        ident = sb("ident", [128, 128])
        ident_r = sb("ident_r", [128, 128], fp32r)
        rbc_p = [sb(f"rbc{n}", [RBC, T], fp32r) for n in range(2)]
        decay = sb("decay", [128, 2, T])
        inp = sb("inp", [128, 2, T])
        h = sb("h", [128, RING, T])
        hc = sb("hc", [128, RING_C, T])
        rbc = hc[0:RBC, RING_C - 1, :]
        b_rows = sb("b_rows", [128, T])
        c_rows = sb("c_rows", [128, 2, T])
        stats = sb("stats", [128, TT, 6])
        mv = sb("mv", [128, TT, 2])
        rstd = sb("rstd", [128, TT])
        one = sb("one", [128, 1])
        rows = decay[:].rearrange("p a n -> p (a n)").rearrange("p (t d) -> p t d", t=TT)

        spread_ps, sum_ps = [ctx.enter_context(nc.psum_tensor(f"s_ps{n}", [128, T], fp32)) for n in ("spread", "sum")]
        bank = [t[:, c * 512:c * 512 + 512] for t in (spread_ps, sum_ps) for c in range(4)]

        def on_pool(u):
            return u % KD == 1 and u < KD * (N - 1) or u % (2 * KD) == 0

        def pool_weighs(u):
            return sum(on_pool(v) for v in range(u))

        def summed_before(eng, u):
            if u > 0:
                eng.wait_ge(summed, (u + 1) // KD)
            if u > 1:
                eng.wait_ge(pe_summed, u // KD)

        def weighted_before(eng, u):
            if pool_weighs(u):
                eng.wait_ge(weighted_pool, pool_weighs(u))
            if u - pool_weighs(u):
                eng.wait_ge(weighted_dve, u - pool_weighs(u))
        s_w = sem("s_w"); s_gc = sem("s_gc"); s_ext = sem("s_ext"); s_zero = sem("s_zero")
        xt_raw = sem("xt_raw"); xt_copied = sem("xt_copied"); rbc_raw = sem("rbc_raw"); rbc_copied = sem("rbc_copied")
        rbc_split = sem("rbc_split"); dt_raw = sem("dt_raw"); dt_biased = sem("dt_biased"); dt_soft = sem("dt_soft"); dt_ready = sem("dt_ready")
        a_exp = sem("a_exp"); a_ready = sem("a_ready")
        b_raw = sem("b_raw"); c_raw = sem("c_raw"); c_copied = sem("c_copied"); b_copied = sem("b_copied"); pe_summed = sem("pe_summed"); y_total = sem("y_total"); decayed = sem("decayed"); cut = sem("cut"); inp_ready = sem("inp_ready")
        scanned = sem("scanned"); weighted_dve = sem("weighted_dve"); weighted_pool = sem("weighted_pool"); skip_ready = sem("skip_ready"); dx_ready = [sem("dx_ready0"), sem("dx_ready1")]; summed = sem("summed")
        y_init = sem("y_init"); yt_raw = sem("yt_raw"); yt_copied = sem("yt_copied"); s_dve = sem("s_dve"); s_var = sem("s_var"); s_rstd = sem("s_rstd")
        e_done = sem("e_done")

        with nc.Block() as block:
            @block.sync
            def _(sp):
                sp.wait_ge(s_zero, 1)
                for dst, src in ((proj[:], w["proj"]), (dtw[0:R, :], w["dt_w"]), (dtb[:], w["dt_b"]), (dskip[:], w["d"]), (neg_a[:], w["a_log"])):
                    sp.dma_start(dst, src).then_inc(s_w, 16)

            @block.gpsimd
            def _(pool):
                nc.gpsimd.memset(one[:], 1.0).then_inc(s_ext, 1)
                nc.gpsimd.memset(dtw[:], 0.0).then_inc(s_zero, 1)
                pool.wait_ge(s_zero, 1)
                nc.gpsimd.memset(ident[:], 0.0).then_inc(s_gc, 1)
                pool.wait_ge(s_gc, 1)
                nc.gpsimd.affine_select(out=ident[:], in_=ident[:], compare_op=ALU.not_equal, fill=1.0, base=0,
                                        pattern=[[-1, 128]], channel_multiplier=1).then_inc(s_gc, 1)
                pool.wait_ge(s_gc, 2)
                nc.gpsimd.tensor_copy(ident_r[:], ident[:]).then_inc(s_gc, 1)
                pool.wait_ge(dt_ready, KD)
                nc.gpsimd.tensor_tensor(dx[:, 1, :], delta[:, 1, :], xT[:, 1, :], ALU.mult).then_inc(dx_ready[1], 1)
                pool.wait_ge(y_init, 1)
                for u in range(N * KD):
                    if on_pool(u):
                        pool.wait_ge(scanned, u + 1)
                        pool.wait_ge(c_copied, u // KD + 1)
                        summed_before(pool, u - RING_C + 1)
                        nc.gpsimd.tensor_tensor(hc[:, u % RING_C, :], h[:, u % RING, :], c_rows[:, u // KD % 2, :], ALU.mult).then_inc(weighted_pool, 1)
                    if u % KD == 0:
                        weighted_before(pool, u + 1)
                        if u > 0:
                            pool.wait_ge(summed, u // KD)
                        nc.gpsimd.tensor_tensor(y[:, 0, :], y[:, 0, :], hc[:, u % RING_C, :], ALU.add).then_inc(summed, 1)

            @block.scalar
            def _(act):
                nc.scalar.preload_act_table_set("natural_log_exp_and_others")

                def take_root(g):
                    act.wait_ge(s_var, g + 1)
                    nc.scalar.activation(rstd[:, g * GROUP:(g + 1) * GROUP], rstd[:, g * GROUP:(g + 1) * GROUP], ACT.Sqrt).then_inc(s_rstd, 1)

                for t in range(TT):
                    act.wait_ge(xt_raw, t + 1)
                    nc.scalar.copy(xT[:, :, t * 128:t * 128 + 128], bank[t % 4][:, 0:256].rearrange("p (k s) -> p k s", k=KD)).then_inc(xt_copied, 1)
                act.wait_ge(s_w, 80)
                act.wait_ge(s_ext, 1)
                nc.scalar.activation(neg_a[:], neg_a[:], ACT.Exp).then_inc(a_exp, 1)
                for c in range(CH):
                    act.wait_ge(rbc_raw, c + 1)
                    nc.scalar.copy(rbc[:, c * 512:c * 512 + 512], bank[4 + c % 2][0:RBC, :]).then_inc(rbc_copied, 1)
                for k in range(KD):
                    act.wait_ge(dt_biased, (k + 1) * CH)
                    nc.scalar.activation(delta[:, k, :], delta[:, k, :], ACT.Exp).then_inc(e_done, 1)
                    act.wait_ge(e_done, k + 1)
                    nc.scalar.activation(delta[:, k, :], delta[:, k, :], ACT.Ln, bias=one[:, 0:1]).then_inc(dt_soft, 1)
                act.wait_ge(skip_ready, 1)
                for k in range(KD):
                    last = nc.scalar.activation(y[:, k, :], xT[:, k, :], ACT.Copy, scale=dskip[:, k:k + 1])
                last.then_inc(y_init, 1)
                act.wait_ge(a_ready, 1)
                for n in range(N):
                    act.wait_ge(b_raw, n + 1)
                    if n >= 1:
                        act.wait_ge(inp_ready, n * KD)
                    nc.scalar.copy(b_rows[:], spread_ps[:]).then_inc(b_copied, 1)
                    for k in range(KD):
                        u = n * KD + k
                        if n == 0:
                            act.wait_ge(dt_ready, k + 1)
                        if u >= 2:
                            act.wait_ge(scanned, u - 1)
                        nc.scalar.activation(decay[:, u % 2, :], delta[:, k, :], ACT.Exp, scale=neg_a[:, k, n:n + 1]).then_inc(decayed, 1)
                        if k == 0:
                            act.wait_ge(c_raw, n + 1)
                            if n >= 2:
                                weighted_before(act, (n - 1) * KD)
                            nc.scalar.copy(c_rows[:, n % 2, :], spread_ps[:]).then_inc(c_copied, 1)
                act.wait_ge(scanned, N * KD)
                for t in range(TT):
                    act.wait_ge(yt_raw, t + 1)
                    nc.scalar.copy(rows[:, t, :], bank[t % 4][:, 0:256]).then_inc(yt_copied, 1)
                    if t % GROUP == GROUP - 1 and t >= GROUP:
                        take_root(t // GROUP - 1)
                take_root(3)

            @block.vector
            def _(dve):
                chain = [0]

                def link(ins):
                    chain[0] += 1
                    ins.then_inc(s_dve, 1)
                    dve.wait_ge(s_dve, chain[0])

                def normalise(g):
                    dve.wait_ge(yt_raw, TT)
                    cols = slice(g * GROUP, (g + 1) * GROUP)
                    dve.wait_ge(s_rstd, g + 1)
                    link(nc.vector.reciprocal(rstd[:, cols], rstd[:, cols]))
                    for t in range(g * GROUP, (g + 1) * GROUP):
                        nc.vector.tensor_scalar(x[:, t, :], rows[:, t, :], mv[:, t, 0:1], rstd[:, t:t + 1], ALU.subtract, ALU.mult)

                dve.wait_ge(a_exp, 1)
                nc.vector.tensor_scalar(dskip[:], dskip[:], 1.0, None, ALU.add).then_inc(skip_ready, 1)
                nc.vector.tensor_scalar(neg_a[:], neg_a[:], -1.0, None, ALU.mult).then_inc(a_ready, 1)
                for c in range(CH):
                    dve.wait_ge(rbc_copied, c + 1)
                    part = slice(c * 512, c * 512 + 512)
                    link(nc.vector.tensor_copy(rbc_p[0][:, part], rbc[:, part]))
                    nc.vector.tensor_tensor(rbc_p[1][:, part], rbc[:, part], rbc_p[0][:, part], ALU.subtract).then_inc(rbc_split, 1)
                for k in range(KD):
                    for c in range(CH):
                        u = k * CH + c
                        dve.wait_ge(dt_raw, u + 1)
                        nc.vector.tensor_scalar(delta[:, k, c * 512:c * 512 + 512], bank[6 + u % 2][:], dtb[:, k:k + 1], 20.0, ALU.add, ALU.min).then_inc(dt_biased, 1)
                for k in range(KD):
                    dve.wait_ge(dt_soft, k + 1)
                    nc.vector.tensor_scalar(delta[:, k, :], delta[:, k, :], DT_MIN, DT_MAX, ALU.max, ALU.min).then_inc(dt_ready, 1)
                dve.wait_ge(dt_ready, 1)
                nc.vector.tensor_tensor(dx[:, 0, :], delta[:, 0, :], xT[:, 0, :], ALU.mult).then_inc(dx_ready[0], 1)

                def weigh(u):
                    dve.wait_ge(scanned, u + 1)
                    dve.wait_ge(c_copied, u // KD + 1)
                    summed_before(dve, u - RING_C + 1)
                    nc.vector.tensor_tensor(hc[:, u % RING_C, :], h[:, u % RING, :], c_rows[:, u // KD % 2, :], ALU.mult).then_inc(weighted_dve, 1)

                for n in range(N):
                    for k in range(KD):
                        u = n * KD + k
                        dve.wait_ge(b_copied, n + 1)
                        if n == 0:
                            dve.wait_ge(dx_ready[k], 1)
                        nc.vector.tensor_tensor(inp[:, k, :], dx[:, k, :], b_rows[:], ALU.mult).then_inc(inp_ready, 1)
                        dve.wait_ge(decayed, u + 1)
                        nc.vector.memset(decay[:, u % 2, :].rearrange("p (a s) -> p a s", s=S)[:, :, 0:1], 0.0).then_inc(cut, 1)
                        dve.wait_ge(inp_ready, u + 1)
                        dve.wait_ge(cut, u + 1)
                        if u >= RING:
                            weighted_before(dve, u - RING + 1)
                        nc.vector.tensor_tensor_scan(h[:, u % RING, :], decay[:, u % 2, :], inp[:, k, :], 0.0, ALU.mult, ALU.add).then_inc(scanned, 1)
                        if u >= 1 and not on_pool(u - 1):
                            weigh(u - 1)
                weigh(N * KD - 1)
                dve.wait_ge(pe_summed, N)
                dve.wait_ge(y_init, 1)
                nc.vector.tensor_tensor(y[:, 1, :], sum_ps[:], y[:, 1, :], ALU.add).then_inc(y_total, 1)
                for g in range(4):
                    group = range(g * GROUP, (g + 1) * GROUP)
                    cols = slice(g * GROUP, (g + 1) * GROUP)
                    for t in group:
                        dve.wait_ge(yt_copied, t + 1)
                        last = nc.vector.bn_stats(stats[:, t, :], rows[:, t, :])
                    link(last)
                    for t in group:
                        last = nc.vector.bn_aggr(mv[:, t, :], stats[:, t, :])
                    link(last)
                    nc.vector.tensor_scalar(rstd[:, cols], mv[:, cols, 1], LN_EPS, None, ALU.add).then_inc(s_var, 1)
                    if g >= 1:
                        normalise(g - 1)
                normalise(3)

            @block.tensor
            def _(pe):
                pe.wait_ge(s_gc, 3)
                for t in range(TT):
                    if t >= 4:
                        pe.wait_ge(xt_copied, t - 3)
                    for k in range(KD):
                        last = nc.tensor.transpose(bank[t % 4][:, k * 128:k * 128 + 128], x[:, t, k * 128:k * 128 + 128], ident[:])
                    last.then_inc(xt_raw, 1)
                pe.wait_ge(s_w, 80)
                for c in range(CH):
                    pe.wait_ge(xt_copied, (c + 1) * TT // CH)
                    if c >= 2:
                        pe.wait_ge(rbc_copied, c - 1)
                    for k in range(KD):
                        last = nc.tensor.matmul(bank[4 + c % 2][0:RBC, :], proj[:, k, :], xT[:, k, c * 512:c * 512 + 512], start=(k == 0), stop=(k == KD - 1))
                    last.then_inc(rbc_raw, 1)
                for k in range(KD):
                    for c in range(CH):
                        u = k * CH + c
                        pe.wait_ge(rbc_copied, c + 1)
                        if u >= 2:
                            pe.wait_ge(dt_biased, u - 1)
                        nc.tensor.matmul(bank[6 + u % 2][:], dtw[:, k * 128:k * 128 + 128], rbc[:, c * 512:c * 512 + 512], start=True, stop=True).then_inc(dt_raw, 1)

                def spread(banks, row, done):
                    for c in range(CH):
                        for part in range(2):
                            last = nc.tensor.matmul(banks[c][:], ident_r[0:RBC, row:row + 1].to_broadcast([RBC, 128]),
                                                    rbc_p[part][:, c * 512:c * 512 + 512], start=(part == 0), stop=(part == 1))
                    last.then_inc(done, 1)

                pe.wait_ge(rbc_split, CH)
                pe.wait_ge(dt_biased, KD * CH)

                def accumulate(n):
                    u = n * KD + 1
                    weighted_before(pe, u + 1)
                    for c in range(CH):
                        last = nc.tensor.matmul(bank[4 + c], ident[:], hc[:, u % RING_C, c * 512:c * 512 + 512], start=(n == 0), stop=(n == N - 1))
                    last.then_inc(pe_summed, 1)

                for n in range(N):
                    if n >= 1:
                        pe.wait_ge(c_copied, n)
                    spread(bank[0:4], R + n, b_raw)
                    pe.wait_ge(b_copied, n + 1)
                    spread(bank[0:4], R + N + n, c_raw)
                    if n >= 2:
                        accumulate(n - 2)
                accumulate(N - 2)
                accumulate(N - 1)
                pe.wait_ge(summed, N)
                pe.wait_ge(y_total, 1)
                for t in range(TT):
                    if t >= 4:
                        pe.wait_ge(yt_copied, t - 3)
                    for k in range(KD):
                        last = nc.tensor.transpose(bank[t % 4][:, k * 128:k * 128 + 128], y[:, k, t * 128:t * 128 + 128], ident[:])
                    last.then_inc(yt_raw, 1)


def linear_attention_layer(nc, sems, x, ctx_in, w):
    fp32 = mybir.dt.float32
    B, S, D = ctx_in.shape
    KD, TT, ND = D // 128, B * S // 128, S // 128
    T = B * S
    HD = 16

    ctx = ExitStack()
    with ctx:
        def sb(n, shape, dt=fp32):
            return ctx.enter_context(nc.sbuf_tensor(f"l_{n}", shape, dt))

        def sem(n):
            sems.append(nc.alloc_semaphore(f"l_{n}"))
            return sems[-1]

        cx = sb("cx", [128, TT, D])
        xT = sb("xT", [128, KD, T])
        cT = sb("cT", [128, KD, T])
        kT = sb("kT", [128, KD, T])
        kR = sb("kR", [128, TT, D])
        v = sb("v", [128, TT, D])
        qT = sb("qT", [128, KD, T])
        cm = sb("cm", [128, B, KD, 128])
        att = cT
        wts = {n: sb(n, [128, KD, D]) for n in ("wq", "wk", "wv", "wo")}
        bq = sb("bq", [128, KD])
        bk = sb("bk", [128, KD])
        bv = sb("bv", [128, D])
        bo = sb("bo", [128, D])
        mask = sb("mask", [128, KD, 128])
        ident = sb("ident", [128, 128])
        nmax = sb("nmax", [128, KD, B])
        sums = sb("sums", [128, KD, B])
        stats = sb("stats", [128, TT, 6])
        mv = sb("mv", [128, TT, 2])
        rstd = sb("rstd", [128, TT])
        bank = [ctx.enter_context(nc.psum_tensor(f"l_ps{n}", [128, 512], fp32)) for n in range(8)]

        JOBS = ([(f"cT{b}", "act" if b % 2 else "dve") for b in range(B)]
                + [(f"k{m}{c}", "act") for c in range(T // 512) for m in range(KD)]
                + [(f"v{b}", "dve") for b in range(B)]
                + [(f"xT{b}", "act") for b in range(B)]
                + [(f"q{m}{c}", "act") for c in range(T // 512) for m in range(KD)]
                + [(f"kR{b}", "act") for b in range(B)]
                + [(f"c{b}", "dve") for b in range(B)]
                + [(f"a{b}", "act") for b in range(B)]
                + [(f"o{b}", "dve") for b in range(B)])
        NUMBER = {n: j for j, (n, _) in enumerate(JOBS)}
        ENGINE = dict(JOBS)
        COUNT = {n: sum(e == ENGINE[n] for _, e in JOBS[:NUMBER[n] + 1]) for n in NUMBER}

        s_cx = [sem(f"s_cx{c}") for c in range(4)]; s_w = sem("s_w"); s_gc = sem("s_gc"); raw = sem("raw")
        out_of = {"act": sem("out_act"), "dve": sem("out_dve")}
        kmaxed = sem("kmaxed"); kexped = sem("kexped"); s_xb = sem("s_xb")
        s_dve = sem("s_dve"); s_var = sem("s_var"); s_rstd = sem("s_rstd");

        rows_of = lambda a: a.rearrange("a (t p) d -> p (a t) d", p=128)
        cx_rows = rows_of(ctx_in)
        QT4 = TT // 4

        with nc.Block() as block:
            @block.sync
            def _(sp):
                for c in range(4):
                    sp.dma_start(cx[:, c * QT4:(c + 1) * QT4, :], cx_rows[:, c * QT4:(c + 1) * QT4, :]).then_inc(s_cx[c], 16)
                for dst, src in [(wts[n][:], w[n]) for n in ("wk", "wv")]:
                    sp.dma_start(dst, src).then_inc(s_w, 16)
                for dst, src in [(wts[n][:], w[n]) for n in ("wq", "wo")] + [
                        (bq[:], w["bq"]), (bk[:], w["bk"]), (bv[:], w["bv"].partition_broadcast(128)), (bo[:], w["bo"].partition_broadcast(128)), (mask[:], w["mask"])]:
                    sp.dma_start(dst, src).then_inc(s_w, 16)

            @block.gpsimd
            def _(pool):
                nc.gpsimd.memset(ident[:], 0.0).then_inc(s_gc, 1)
                pool.wait_ge(s_gc, 1)
                nc.gpsimd.affine_select(out=ident[:], in_=ident[:], compare_op=ALU.not_equal, fill=1.0, base=0,
                                        pattern=[[-1, 128]], channel_multiplier=1).then_inc(s_gc, 1)
                pool.wait_ge(s_w, 144)
                for b in range(B):
                    pool.wait_ge(raw, NUMBER[f"xT{b}"] + 1)
                    nc.gpsimd.tensor_tensor(x[:, b * ND:(b + 1) * ND, :], x[:, b * ND:(b + 1) * ND, :],
                                            bo[:].unsqueeze(1).to_broadcast([128, ND, D]), ALU.add).then_inc(s_xb, 1)

            def taken(eng, me, name):
                eng.wait_ge(raw, NUMBER[name] + 1)
                return bank[NUMBER[name] % 8]

            halves = lambda a: a.rearrange("p (k s) -> p k s", k=2)

            @block.scalar
            def _(act):
                nc.scalar.preload_act_table_set("exp_and_others")
                act.wait_ge(s_w, 144)
                for b in range(B):
                    if ENGINE[f"cT{b}"] == "act":
                        p = taken(act, "act", f"cT{b}")
                        nc.scalar.copy(cT[:, :, b * S:(b + 1) * S], halves(p[:])).then_inc(out_of["act"], 1)
                for c in range(T // 512):
                    for m in range(KD):
                        p = taken(act, "act", f"k{m}{c}")
                        nc.scalar.activation(kT[:, m, c * 512:c * 512 + 512], p[:], ACT.Identity, bias=bk[:, m:m + 1]).then_inc(out_of["act"], 1)
                for b in range(B):
                    p = taken(act, "act", f"xT{b}")
                    nc.scalar.copy(xT[:, :, b * S:(b + 1) * S], halves(p[:])).then_inc(out_of["act"], 1)
                act.wait_ge(kmaxed, 1)
                for m in range(KD):
                    for b in range(B):
                        nc.scalar.activation(kT[:, m, b * S:(b + 1) * S], kT[:, m, b * S:(b + 1) * S], ACT.Exp, bias=nmax[:, m, b:b + 1],
                                             accum_out=sums[:, m, b:b + 1]).then_inc(kexped, 1)
                for c in range(T // 512):
                    for m in range(KD):
                        p = taken(act, "act", f"q{m}{c}")
                        nc.scalar.activation(qT[:, m, c * 512:c * 512 + 512], p[:], ACT.Identity, bias=bq[:, m:m + 1]).then_inc(out_of["act"], 1)
                for b in range(B):
                    p = taken(act, "act", f"kR{b}")
                    nc.scalar.copy(kR[:, b * ND:(b + 1) * ND, :], p[:].rearrange("p (t d) -> p t d", t=ND)).then_inc(out_of["act"], 1)
                for b in range(B):
                    p = taken(act, "act", f"a{b}")
                    nc.scalar.copy(att[:, :, b * S:(b + 1) * S], halves(p[:])).then_inc(out_of["act"], 1)
                for g in range(4):
                    act.wait_ge(s_var, g + 1)
                    nc.scalar.activation(rstd[:, g * QT4:(g + 1) * QT4], rstd[:, g * QT4:(g + 1) * QT4], ACT.Sqrt).then_inc(s_rstd, 1)

            @block.vector
            def _(dve):
                chain = [0]

                def link(ins):
                    chain[0] += 1
                    ins.then_inc(s_dve, 1)
                    dve.wait_ge(s_dve, chain[0])

                for b in range(B):
                    if ENGINE[f"cT{b}"] == "dve":
                        p = taken(dve, "dve", f"cT{b}")
                        nc.vector.tensor_copy(cT[:, :, b * S:(b + 1) * S], halves(p[:])).then_inc(out_of["dve"], 1)
                dve.wait_ge(s_w, 144)
                for b in range(B):
                    p = taken(dve, "dve", f"v{b}")
                    nc.vector.tensor_tensor(v[:, b * ND:(b + 1) * ND, :], p[:].rearrange("p (t d) -> p t d", t=ND),
                                            bv[:].unsqueeze(1).to_broadcast([128, ND, D]), ALU.add).then_inc(out_of["dve"], 1)
                dve.wait_ge(out_of["act"], COUNT[f"k{KD - 1}{T // 512 - 1}"])
                nc.vector.tensor_reduce(nmax[:], kT[:].rearrange("p m (b s) -> p m b s", b=B), AX.X, ALU.max, negate=True).then_inc(kmaxed, 1)
                dve.wait_ge(kexped, KD * B)
                link(nc.vector.reciprocal(sums[:], sums[:]))
                for b in range(B):
                    p = taken(dve, "dve", f"c{b}")
                    for m in range(KD):
                        last = nc.vector.scalar_tensor_tensor(cm[:, b, m, :], p[:, m * 128:m * 128 + 128], sums[:, m, b:b + 1], mask[:, m, :], ALU.mult, ALU.mult)
                    last.then_inc(out_of["dve"], 1)
                def normalise(g):
                    cols = slice(g * QT4, (g + 1) * QT4)
                    dve.wait_ge(s_rstd, g + 1)
                    link(nc.vector.reciprocal(rstd[:, cols], rstd[:, cols]))
                    for t in range(g * QT4, (g + 1) * QT4):
                        nc.vector.tensor_scalar(x[:, t, :], x[:, t, :], mv[:, t, 0:1], rstd[:, t:t + 1], ALU.subtract, ALU.mult)

                for g in range(4):
                    cols = slice(g * QT4, (g + 1) * QT4)
                    for b in range(g * B // 4, (g + 1) * B // 4):
                        p = taken(dve, "dve", f"o{b}")
                        dve.wait_ge(s_xb, b + 1)
                        nc.vector.tensor_tensor(x[:, b * ND:(b + 1) * ND, :], p[:].rearrange("p (t d) -> p t d", t=ND),
                                                x[:, b * ND:(b + 1) * ND, :], ALU.add).then_inc(out_of["dve"], 1)
                        dve.wait_ge(out_of["dve"], COUNT[f"o{b}"])
                        for t in range(b * ND, (b + 1) * ND):
                            last = nc.vector.bn_stats(stats[:, t, :], x[:, t, :])
                    link(last)
                    for t in range(g * QT4, (g + 1) * QT4):
                        last = nc.vector.bn_aggr(mv[:, t, :], stats[:, t, :])
                    link(last)
                    nc.vector.tensor_scalar(rstd[:, cols], mv[:, cols, 1], LN_EPS, None, ALU.add).then_inc(s_var, 1)
                    if g >= 1:
                        normalise(g - 1)
                normalise(3)

            @block.tensor
            def _(pe):
                def done(name):
                    pe.wait_ge(out_of[ENGINE[name]], COUNT[name])

                def start(name):
                    j = NUMBER[name]
                    if j >= 8:
                        done(JOBS[j - 8][0])
                    return bank[j % 8]

                def transposed(name, src, b):
                    p = start(name)
                    for k in range(KD):
                        for s in range(ND):
                            last = nc.tensor.transpose(p[:, k * S + s * 128:k * S + s * 128 + 128], src[:, b * ND + s, k * 128:k * 128 + 128], ident[:])
                    last.then_inc(raw, 1)

                def project(name, wt, m, c, src):
                    p = start(name)
                    for k in range(KD):
                        last = nc.tensor.matmul(p[:], wt[:, k, m * 128:m * 128 + 128], src[:, k, c * 512:c * 512 + 512], start=(k == 0), stop=(k == KD - 1))
                    last.then_inc(raw, 1)

                def rows_product(name, b, src, wt):
                    p = start(name)
                    for s in range(ND):
                        for k in range(KD):
                            last = nc.tensor.matmul(p[:, s * D:s * D + D], src[:, k, b * S + s * 128:b * S + s * 128 + 128], wt[:, k, :],
                                                    start=(k == 0), stop=(k == KD - 1))
                    last.then_inc(raw, 1)

                pe.wait_ge(s_gc, 2)
                for b in range(B):
                    pe.wait_ge(s_cx[b * 4 // B], 16)
                    transposed(f"cT{b}", cx, b)
                pe.wait_ge(s_w, 144)
                for c in range(T // 512):
                    done(f"cT{2 * c}")
                    done(f"cT{2 * c + 1}")
                    for m in range(KD):
                        project(f"k{m}{c}", wts["wk"], m, c, cT)
                for b in range(B):
                    rows_product(f"v{b}", b, cT, wts["wv"])
                for b in range(B):
                    transposed(f"xT{b}", x, b)
                for c in range(T // 512):
                    done(f"xT{2 * c + 1}")
                    for m in range(KD):
                        project(f"q{m}{c}", wts["wq"], m, c, xT)
                for b in range(B):
                    pe.wait_ge(kexped, B + b + 1)
                    p = start(f"kR{b}")
                    for s in range(ND):
                        for m in range(KD):
                            last = nc.tensor.transpose(p[:, s * D + m * 128:s * D + m * 128 + 128], kT[:, m, b * S + s * 128:b * S + s * 128 + 128], ident[:])
                    last.then_inc(raw, 1)
                for b in range(B):
                    done(f"kR{b}")
                    p = start(f"c{b}")
                    for m in range(KD):
                        for s in range(ND):
                            t = b * ND + s
                            last = nc.tensor.matmul(p[:, m * 128:m * 128 + 128], kR[:, t, m * 128:m * 128 + 128], v[:, t, m * 128:m * 128 + 128],
                                                    start=(s == 0), stop=(s == ND - 1))
                    last.then_inc(raw, 1)
                for b in range(B):
                    done(f"c{b}")
                    p = start(f"a{b}")
                    for m in range(KD):
                        last = nc.tensor.matmul(p[:, m * S:m * S + S], cm[:, b, m, :], qT[:, m, b * S:(b + 1) * S], start=True, stop=True)
                    last.then_inc(raw, 1)
                for b in range(B):
                    done(f"a{b}")
                    rows_product(f"o{b}", b, att, wts["wo"])


def decoder(nc, a, out):
    fp32 = mybir.dt.float32
    B, S, D = a["x"].shape
    T = B * S
    E = a["wr0"].shape[1]
    rows = T + (TOP_K * T + E * (SLOTS - 1)) // SLOTS * SLOTS
    slots = nc.dram_tensor("slots", (rows, D), fp32).ap()
    results = nc.dram_tensor("results", (rows, D), fp32).ap()
    attended = nc.dram_tensor("attended", (B, S, D), fp32).ap()
    flat = lambda t: t.rearrange("a s d -> (a s) d")
    sems = []

    def layer_ends():
        with nc.Block() as block:
            @block.gpsimd
            def _(pool):
                nc.clear_and_free_semaphores(sems)
        sems.clear()

    attention_layers(nc, sems, a["x"], a["ctx"], attended, slots, a)
    layer_ends()
    with nc.sbuf_tensor("tokens", [128, T // 128, D], fp32) as tokens:
        moe_layer(nc, sems, "m0", tokens, flat(attended), None, a["wr0"], a["br0"], (a["g0"], a["b0"]), a["up0"], a["bup0"],
                  a["down0"], a["bdown0"], slots, results, ACT.Relu, False, False)
        layer_ends()
        state_space_layer(nc, sems, tokens, S, a)
        layer_ends()
        linear_attention_layer(nc, sems, tokens, a["ctx"], {n[2:]: t for n, t in a.items() if n.startswith("l_")})
        layer_ends()
        moe_layer(nc, sems, "m1", tokens, None, flat(out), a["wr1"], None, None, a["up1"], None, a["down1"], None,
                  slots, results, ACT.Gelu, True, True)


def kernel(**inputs):
    import numpy as np
    import concourse.bacc as bacc
    from concourse.bass_utils import run_bass_kernel_spmd

    g = {k: np.asarray(v) for k, v in inputs.items()}

    def tiles(a):
        *e, k, n = a.shape
        return np.moveaxis(a.reshape(*e, k // 128, 128, n), -3, -2)

    def column(a):
        return a.reshape(-1, 128).T

    A, X, F0, F1, M, L = "L0_attn_", "L0_xattn_", "L0_ffn_", "L1_ffn_", "L1_attn_", "L1_xattn_"
    heads = 128 // g[A + "q_gamma"].shape[0]
    blocks = np.kron(np.eye(8, dtype=np.float32), np.ones((16, 16), np.float32))
    arrays = {
        "x": g["x"], "ctx": g["ctx_1024"],
        "wqkv": tiles(np.concatenate([g[A + "Wq"].T, g[A + "Wk"].T, g[A + "Wv"].T], 1)), "wo0": tiles(g[A + "Wo"].T), "bo0": g[A + "bo"],
        "ln_g": column(g[A + "ln_g"]), "ln_b": column(g[A + "ln_b"]),
        "qg": np.concatenate([g[A + "q_gamma"]] * heads)[:, None], "kg": np.concatenate([g[A + "k_gamma"]] * heads)[:, None],
        "wq": tiles(g[X + "wq_w"]), "wk": tiles(g[X + "wk_w"]), "wv": tiles(g[X + "wv_w"]), "wox": tiles(g[X + "wo_w"]),
        "bqx": column(g[X + "wq_b"]), "bkx": column(g[X + "wk_b"]), "bvx": g[X + "wv_b"], "box": g[X + "wo_b"],
        "mk": tiles(g[X + "mk"][0].T), "mvx": g[X + "mv"][0],
        "wr0": g[F0 + "Wr"], "br0": g[F0 + "br"], "g0": g[F0 + "gamma"], "b0": g[F0 + "beta"],
        "up0": tiles(g[F0 + "W1"]), "bup0": np.moveaxis(g[F0 + "b1"].reshape(8, -1, 128), 1, 2), "down0": tiles(g[F0 + "W2"]), "bdown0": g[F0 + "b2"],
        "proj": tiles(np.concatenate([g[M + "x_proj_w"], g[M + "B_proj_w"], g[M + "C_proj_w"]]).T), "dt_w": g[M + "dt_proj_w"].T,
        "dt_b": column(g[M + "dt_proj_b"]), "d": column(g[M + "D"]), "a_log": tiles(g[M + "A_log"]),
        "l_wq": tiles(g[L + "Wq"].T), "l_wk": tiles(g[L + "Wk"].T), "l_wv": tiles(g[L + "Wv"].T), "l_wo": tiles(g[L + "Wo"].T),
        "l_bq": column(g[L + "bq"]), "l_bk": column(g[L + "bk"]), "l_bv": g[L + "bv"], "l_bo": g[L + "bo"],
        "l_mask": np.stack([blocks, blocks], 1),
        "wr1": g[F1 + "Wg"], "up1": tiles(np.concatenate([g[F1 + "Wu"], g[F1 + "W1"][None]])),
        "down1": tiles(np.concatenate([g[F1 + "Wd"], g[F1 + "W2"][None]])),
    }
    nc = bacc.Bacc("TRN2", target_bir_lowering=False, num_devices=1)
    arrays = {f"in_{n}": np.ascontiguousarray(v) for n, v in arrays.items()}
    a = {n[3:]: nc.dram_tensor(n, v.shape, mybir.dt.from_np(v.dtype), kind="ExternalInput").ap() for n, v in arrays.items()}
    out = nc.dram_tensor("out", g["x"].shape, mybir.dt.float32, kind="ExternalOutput").ap()
    decoder(nc, a, out)
    r = run_bass_kernel_spmd(nc, [arrays], core_ids=[0])
    return r.results[0]["out"]
```
